# Optimizing a Trainium2 kernel written in Bass

```python
import numpy as np
import jax
import jax.numpy as jnp

def _softmax(x, axis=-1):
    return jax.nn.softmax(x, axis=axis)

def _gelu(x):
    return jax.nn.gelu(x, approximate=True)

def _silu(x):
    return jax.nn.silu(x)

def _sigmoid(x):
    return jax.nn.sigmoid(x)

def _layernorm(x, axis=-1, eps=1e-05):
    m = jnp.mean(x, axis=axis, keepdims=True)
    v = jnp.var(x, axis=axis, keepdims=True)
    return (x - m) / jnp.sqrt(v + eps)

def _scatter_add(tgt, idx, src, axis=0):
    return tgt.at[idx].add(src)

def _segment_sum(src, seg, n):
    return jax.ops.segment_sum(src, seg, n)
kernel_name = 'mk_gnn_resnorm_d1_gnn_r8_e66906'

def setup_inputs(seed: int=0):
    np.random.seed(seed)
    _w = jnp.asarray

    def _rec_inputs():
        import jax
        import jax.numpy as jnp
        _gk = jax.random.key(seed)
        x = -6.415e-05 + 1 * jax.random.normal(jax.random.fold_in(_gk, 1), (2500, 512), jnp.float32)
        src = jax.random.randint(jax.random.fold_in(_gk, 2), (40000,), 0, 2500, jnp.int32)
        dst = jax.random.randint(jax.random.fold_in(_gk, 3), (40000,), 0, 2500, jnp.int32)
        _o = jnp.argsort(dst, stable=True)
        src = src[_o]
        dst = dst[_o]
        edge_type_10 = jax.random.randint(jax.random.fold_in(_gk, 12), (40000,), 0, 10, jnp.int32)
        edge_weight = 0.000747931 + 0.998196 * jax.random.normal(jax.random.fold_in(_gk, 13), (40000,), jnp.float32)
        return (x, src, dst, edge_type_10, edge_weight)
    x, src, dst, edge_type_10, edge_weight = _rec_inputs()

    def _L0_gnn_setup():
        import jax, jax.numpy as jnp
        import numpy as np
        N, E, H, D, C, L = (2500, 40000, 8, 64, 512, 2)

        def layer_norm(x, g, b, eps=1e-05):
            mu = x.mean(-1, keepdims=True)
            var = ((x - mu) ** 2).mean(-1, keepdims=True)
            return (x - mu) / jnp.sqrt(var + eps) * g + b
        key = jax.random.key(seed)
        ks = jax.random.split(key, 14)
        s = 0.02
        x = jax.random.normal(ks[0], (N, C), jnp.float32)
        edge_index = jax.random.randint(ks[1], (2, E), 0, N, jnp.int32)
        edge_type = jax.random.randint(ks[2], (E,), 0, 10, jnp.int32)
        edge_repre = jax.random.normal(ks[3], (E,), jnp.float32)
        Wq = jax.random.normal(ks[4], (L, C, C), jnp.float32) * s
        Wk = jax.random.normal(ks[5], (L, C, C), jnp.float32) * s
        Wv = jax.random.normal(ks[6], (L, C, C), jnp.float32) * s
        Ws = jax.random.normal(ks[7], (L, C, C), jnp.float32) * s
        bq = jnp.zeros((L, C), jnp.float32)
        bk = jnp.zeros((L, C), jnp.float32)
        bv = jnp.zeros((L, C), jnp.float32)
        bs = jnp.zeros((L, C), jnp.float32)
        W1 = jax.random.normal(ks[8], (C, 2 * C), jnp.float32) * s
        b1 = jnp.zeros((2 * C,), jnp.float32)
        W2 = jax.random.normal(ks[9], (2 * C, C), jnp.float32) * s
        b2 = jnp.zeros((C,), jnp.float32)
        ln_g = jnp.ones((C,), jnp.float32)
        ln_b = jnp.zeros((C,), jnp.float32)
        return {'x': x, 'edge_index': edge_index, 'edge_type': edge_type, 'edge_repre': edge_repre, 'Wq': Wq, 'bq': bq, 'Wk': Wk, 'bk': bk, 'Wv': Wv, 'bv': bv, 'Ws': Ws, 'bs': bs, 'W1': W1, 'b1': b1, 'W2': W2, 'b2': b2, 'ln_g': ln_g, 'ln_b': ln_b}
    _L0_gnn_all = _L0_gnn_setup()
    _L0_gnn_in = {k: v for k, v in _L0_gnn_all.items() if k in ('Wq', 'bq', 'Wk', 'bk', 'Wv', 'bv', 'Ws', 'bs', 'W1', 'b1', 'W2', 'b2', 'ln_g', 'ln_b')}
    del _L0_gnn_all
    return {'x': x, 'src': src, 'dst': dst, 'edge_type_10': edge_type_10, 'edge_weight': edge_weight, 'L0_gnn_Wq': _L0_gnn_in['Wq'], 'L0_gnn_bq': _L0_gnn_in['bq'], 'L0_gnn_Wk': _L0_gnn_in['Wk'], 'L0_gnn_bk': _L0_gnn_in['bk'], 'L0_gnn_Wv': _L0_gnn_in['Wv'], 'L0_gnn_bv': _L0_gnn_in['bv'], 'L0_gnn_Ws': _L0_gnn_in['Ws'], 'L0_gnn_bs': _L0_gnn_in['bs'], 'L0_gnn_W1': _L0_gnn_in['W1'], 'L0_gnn_b1': _L0_gnn_in['b1'], 'L0_gnn_W2': _L0_gnn_in['W2'], 'L0_gnn_b2': _L0_gnn_in['b2'], 'L0_gnn_ln_g': _L0_gnn_in['ln_g'], 'L0_gnn_ln_b': _L0_gnn_in['ln_b']}

def reference(x, src, dst, edge_type_10, edge_weight, L0_gnn_Wq, L0_gnn_bq, L0_gnn_Wk, L0_gnn_bk, L0_gnn_Wv, L0_gnn_bv, L0_gnn_Ws, L0_gnn_bs, L0_gnn_W1, L0_gnn_b1, L0_gnn_W2, L0_gnn_b2, L0_gnn_ln_g, L0_gnn_ln_b):
    import jax
    import jax.numpy as jnp

    def _L0_gnn_ref(x, edge_index, edge_type, edge_repre, Wq, bq, Wk, bk, Wv, bv, Ws, bs, W1, b1, W2, b2, ln_g, ln_b):
        import jax, jax.numpy as jnp
        import numpy as np
        N, E, H, D, C, L = (2500, 40000, 8, 64, 512, 2)

        def layer_norm(x, g, b, eps=1e-05):
            mu = x.mean(-1, keepdims=True)
            var = ((x - mu) ** 2).mean(-1, keepdims=True)
            return (x - mu) / jnp.sqrt(var + eps) * g + b
        src, dst = (edge_index[0], edge_index[1])
        enc = x
        scale = 1.0 / jnp.sqrt(jnp.float32(D))
        for l in range(L):
            q = (x @ Wq[l] + bq[l]).reshape(N, H, D)
            k = (x @ Wk[l] + bk[l]).reshape(N, H, D)
            v = (x @ Wv[l] + bv[l]).reshape(N, H, D)
            a = (q[dst] * k[src]).sum(-1) * scale
            amax = jax.ops.segment_max(a, dst, num_segments=N)
            amax = jnp.where(jnp.isfinite(amax), amax, 0.0)
            e = jnp.exp(a - amax[dst])
            denom = jax.ops.segment_sum(e, dst, num_segments=N)
            alpha = e / (denom[dst] + 1e-16)
            agg = jax.ops.segment_sum(alpha[:, :, None] * v[src], dst, num_segments=N).reshape(N, C)
            x = agg + (x @ Ws[l] + bs[l]) + enc
        x = layer_norm(x, ln_g, ln_b)
        x = jax.nn.relu(x @ W1 + b1) @ W2 + b2 + x
        x = layer_norm(x, ln_g, ln_b)
        return x + enc
    edge_index = jnp.stack([src, dst])
    x = _layernorm(x + _L0_gnn_ref(x, edge_index, edge_type_10, edge_weight, L0_gnn_Wq, L0_gnn_bq, L0_gnn_Wk, L0_gnn_bk, L0_gnn_Wv, L0_gnn_bv, L0_gnn_Ws, L0_gnn_bs, L0_gnn_W1, L0_gnn_b1, L0_gnn_W2, L0_gnn_b2, L0_gnn_ln_g, L0_gnn_ln_b), axis=-1)
    return x

_drawn_inputs = setup_inputs


def setup_inputs(seed=0):
    import zlib

    import numpy as np

    out = dict(_drawn_inputs(seed))
    spreads = {'L0_gnn_bq': (0.0, 0.8),
     'L0_gnn_bk': (0.0, 0.8),
     'L0_gnn_bv': (0.0, 0.1),
     'L0_gnn_bs': (0.0, 0.1),
     'L0_gnn_b1': (0.0, 0.542),
     'L0_gnn_b2': (0.0, 0.1),
     'L0_gnn_ln_g': (1.0, 0.2),
     'L0_gnn_ln_b': (0.0, 0.1)}
    factors = {'L0_gnn_Wq': 5.039, 'L0_gnn_Wk': 4.929}
    for name, (base, spread) in spreads.items():
        noise = np.random.default_rng([zlib.crc32(name.encode()), seed]).standard_normal(out[name].shape)
        drawn = base * np.exp(spread * noise) if base else spread * noise
        out[name] = jnp.asarray(drawn.astype(out[name].dtype))
    for name, factor in factors.items():
        out[name] = (out[name] * factor).astype(out[name].dtype)
    return out
```

```python
import concourse.bass as bass
from concourse import mybir
from contextlib import ExitStack

F32 = mybir.dt.float32
F32R = mybir.dt.float32r
BF16 = mybir.dt.bfloat16
I32 = mybir.dt.int32
ALU = mybir.AluOpType
ACT = mybir.ActivationFunctionType
AX = mybir.AxisListType

P = 128
NODES, EDGES, C, HEADS, LAYERS = 2500, 40000, 512, 8, 2
HID = 2 * C
D = C // HEADS
KC = C // P
FC = HID // P
BLOCKS = -(-NODES // P)
ROWS = BLOCKS * P
TPS = 2
SE = TPS * P
EDGE_ROWS = -(-EDGES // SE)
STEPS = EDGE_ROWS + BLOCKS - 1
TILES = STEPS * TPS
STEP_GROUPS = 2
TABLE = STEP_GROUPS * P
CHUNKS = P // HEADS
CT = TILES // CHUNKS
SLOTS = CT * P
HALF = 4
BODY = 2 * HALF
RING = 4
AGG = C + HEADS
DVE_HEADS1, DVE_HEADS2 = 4, 5
BIG = 1e30
PAD_DST = 1 << 20
EPS = 1e-5
assert STEPS % BODY == 0 and TILES % CHUNKS == 0 and STEPS + HALF <= TABLE


class Shared:
    pass


class Phase:

    def __init__(self, nc, stack, tag):
        self.nc, self.stack, self.tag = nc, stack, tag

    def sb(self, name, shape, dt=F32):
        return self.stack.enter_context(self.nc.sbuf_tensor(f"{self.tag}_{name}", shape, dt))

    def ps(self, name, shape):
        return self.stack.enter_context(self.nc.psum_tensor(f"{self.tag}_{name}", shape, F32))

    def sem(self, name):
        return self.nc.alloc_semaphore(f"{self.tag}_{name}")


def chain(eng, sem):
    count = [0]

    def link(ins):
        count[0] += 1
        ins.then_inc(sem, 1)
        eng.wait_ge(sem, count[0])

    return link


def build_constants(nc, k):
    with ExitStack() as stack:
        ph = Phase(nc, stack, "const")
        row_i = ph.sb("row_i", [P, P], I32)
        col_i = ph.sb("col_i", [P, 1], I32)
        iotas_done, steps = ph.sem("iotas_done"), ph.sem("steps")
        with nc.Block() as block:
            @block.gpsimd
            def _(pool):
                nc.gpsimd.iota(row_i[:], pattern=[[1, P]], base=0, channel_multiplier=0).then_inc(iotas_done, 1)
                nc.gpsimd.iota(col_i[:], pattern=[[0, 1]], base=0, channel_multiplier=1).then_inc(iotas_done, 1)

            @block.vector
            def _(dve):
                link = chain(dve, steps)
                nc.vector.memset(k.ones[:], 1.0)
                nc.vector.memset(k.eps[:], EPS)
                dve.wait_ge(iotas_done, 2)
                nc.vector.tensor_copy(k.iota_row[:], row_i[:])
                link(nc.vector.tensor_copy(k.iota_col[:], col_i[:]))
                link(nc.vector.tensor_scalar(k.ident[:], k.iota_row[:], k.iota_col[:, 0:1], None, ALU.is_equal))


def build_step_tables(nc, k):
    with ExitStack() as stack:
        ph = Phase(nc, stack, "tab")
        cols = EDGE_ROWS * SE // P
        dst_i = ph.sb("dst_i", [P, cols], I32)
        dst_f = ph.sb("dst_f", [P, cols])
        bound_i = ph.sb("bound_i", [P, BLOCKS + 1], I32)
        bound = ph.sb("bound", [P, BLOCKS + 1])
        below = ph.sb("below", [P, BLOCKS + 1, cols])
        count = ph.sb("count", [P, BLOCKS + 1])
        start = ph.sb("start", [P, BLOCKS + 1])
        start_i = ph.sb("start_i", [P, BLOCKS + 1], I32)
        first_row = ph.sb("first_row", [P, BLOCKS])
        stop_row = ph.sb("stop_row", [P, BLOCKS])
        n_steps = ph.sb("n_steps", [P, BLOCKS])
        zeros = ph.sb("zeros", [P, BLOCKS])
        steps_end = ph.sb("steps_end", [P, BLOCKS])
        lead = ph.sb("lead", [P, BLOCKS])
        lead_diff = ph.sb("lead_diff", [P, BLOCKS])
        passed = ph.sb("passed", [P, BLOCKS])
        step_no = ph.sb("step_no", [P, STEP_GROUPS])
        block_no = ph.sb("block_no", [P, STEP_GROUPS])
        block_lo = ph.sb("block_lo", [P, STEP_GROUPS])
        row_no = ph.sb("row_no", [P, STEP_GROUPS])
        row_i = ph.sb("row_i", [P, STEP_GROUPS], I32)
        src_i = ph.sb("src_i", [P, STEP_GROUPS, SE], I32)
        sdst_i = ph.sb("sdst_i", [P, STEP_GROUPS, SE], I32)
        src_f = ph.sb("src_f", [P, STEP_GROUPS, SE])
        sdst_f = ph.sb("sdst_f", [P, STEP_GROUPS, SE])
        local = ph.sb("local", [P, STEP_GROUPS, SE])
        inside = ph.sb("inside", [P, STEP_GROUPS, SE])
        inside_hi = ph.sb("inside_hi", [P, STEP_GROUPS, SE])
        key = ph.sb("key", [P, STEP_GROUPS, SE])
        local16 = ph.sb("local16", [P, STEP_GROUPS, SE], BF16)
        key_t = ph.sb("key_t", [P, TABLE, TPS])
        key8 = ph.sb("key8", [P, CT, CHUNKS, HEADS])
        key_s = ph.sb("key_s", [P, SLOTS])
        row_first = ph.sb("row_first", [1, HEADS, CHUNKS])
        row_last = ph.sb("row_last", [1, HEADS, CHUNKS])
        goes_on = ph.sb("goes_on", [1, HEADS, CHUNKS])
        whole = ph.sb("whole", [1, HEADS, CHUNKS])
        big = ph.ps("big", [P, 6 * 512])
        small = ph.ps("small", [P, 512])
        ends = ph.ps("ends", [P, 512])

        dst_in, bound_in, steps = ph.sem("dst_in"), ph.sem("bound_in"), ph.sem("steps")
        counted, summed = ph.sem("counted"), ph.sem("summed")
        rows_known, src_in, sdst_in = ph.sem("rows_known"), ph.sem("src_in"), ph.sem("sdst_in")
        steps_known, turned = ph.sem("steps_known"), ph.sem("turned")
        local_known, local_out = ph.sem("local_known"), ph.sem("local_out")
        keys_ready, keys_turned = ph.sem("keys_ready"), ph.sem("keys_turned")
        ends_ready, ends_turned = ph.sem("ends_ready"), ph.sem("ends_turned")

        def pair(which, g, t):
            n = (which * STEP_GROUPS + g) * TPS + t
            return big[:, n * P:(n + 1) * P]

        with nc.Block() as block:
            @block.sync
            def _(sp):
                sp.dma_start(dst_i[:], k.dst.rearrange("(p c) -> p c", p=P)).then_inc(dst_in, 16)
                sp.wait_ge(local_known, 1)
                for g in range(STEP_GROUPS):
                    sp.dma_start(k.local_d[g * P * SE:(g + 1) * P * SE].rearrange("(p e) -> p e", p=P),
                                 local16[:, g, :]).then_inc(local_out, 16)
                sp.wait_ge(local_out, 16 * STEP_GROUPS)

            @block.gpsimd
            def _(pool):
                nc.gpsimd.iota(bound_i[:], pattern=[[P, BLOCKS + 1]], base=0,
                               channel_multiplier=0).then_inc(bound_in, 1)
                pool.wait_ge(rows_known, 1)
                for g in range(STEP_GROUPS):
                    at = bass.IndirectOffsetOnAxis(ap=row_i[:, g:g + 1], axis=0)
                    nc.gpsimd.indirect_dma_start(src_i[:, g, :], None, k.src, at).then_inc(src_in, 16)
                    nc.gpsimd.indirect_dma_start(sdst_i[:, g, :], None,
                                                 k.dst.rearrange("(r e) -> r e", e=SE), at).then_inc(sdst_in, 16)

            @block.vector
            def _(dve):
                link = chain(dve, steps)
                v = nc.vector
                dve.wait_ge(bound_in, 1)
                v.tensor_copy(bound[:], bound_i[:])
                dve.wait_ge(dst_in, 16)
                link(v.tensor_copy(dst_f[:], dst_i[:]))
                link(v.tensor_tensor(below[:], dst_f[:].unsqueeze(1).to_broadcast([P, BLOCKS + 1, cols]),
                                     bound[:].unsqueeze(2).to_broadcast([P, BLOCKS + 1, cols]), ALU.is_lt))
                v.tensor_reduce(count[:], below[:], AX.X, ALU.add).then_inc(counted, 1)
                dve.wait_ge(summed, 1)
                link(v.tensor_copy(start[:], small[:, 0:BLOCKS + 1]))
                link(v.tensor_copy(start_i[:], start[:]))
                link(v.tensor_scalar(start_i[:], start_i[:], SE.bit_length() - 1, None, ALU.logical_shift_right))
                link(v.tensor_copy(first_row[:], start_i[:, 0:BLOCKS]))
                link(v.tensor_scalar(stop_row[:], start[:, 1:], float(SE - 1), None, ALU.add))
                link(v.tensor_copy(start_i[:, 0:BLOCKS], stop_row[:]))
                link(v.tensor_scalar(start_i[:], start_i[:], SE.bit_length() - 1, None, ALU.logical_shift_right))
                link(v.tensor_copy(stop_row[:], start_i[:, 0:BLOCKS]))
                link(v.tensor_tensor(n_steps[:], stop_row[:], first_row[:], ALU.subtract))
                link(v.tensor_tensor(passed[:], start[:, 1:], start[:, 0:BLOCKS], ALU.is_gt))
                link(v.tensor_tensor(n_steps[:], n_steps[:], passed[:], ALU.mult))
                link(v.memset(zeros[:], 0.0))
                link(v.tensor_tensor_scan(steps_end[:], n_steps[:], zeros[:], 0.0, ALU.add, ALU.add))
                link(v.tensor_tensor(lead[:], first_row[:], n_steps[:], ALU.add))
                link(v.tensor_tensor(lead[:], lead[:], steps_end[:], ALU.subtract))
                link(v.memset(lead_diff[:], 0.0))
                link(v.tensor_tensor(lead_diff[:, 0:BLOCKS - 1], lead[:, 1:], lead[:, 0:BLOCKS - 1], ALU.subtract))
                for g in range(STEP_GROUPS):
                    link(v.tensor_scalar(step_no[:, g:g + 1], k.iota_col[:], float(g * P), None, ALU.add))
                    link(v.tensor_scalar(passed[:], steps_end[:], step_no[:, g:g + 1], None, ALU.is_le))
                    link(v.tensor_reduce(block_no[:, g:g + 1], passed[:], AX.X, ALU.add))
                    link(v.tensor_tensor(passed[:], passed[:], lead_diff[:], ALU.mult))
                    link(v.tensor_reduce(row_no[:, g:g + 1], passed[:], AX.X, ALU.add))
                    link(v.tensor_tensor(row_no[:, g:g + 1], row_no[:, g:g + 1], lead[:, 0:1], ALU.add))
                    link(v.tensor_tensor(row_no[:, g:g + 1], row_no[:, g:g + 1], step_no[:, g:g + 1], ALU.add))
                link(v.tensor_scalar(row_no[:], row_no[:], float(EDGE_ROWS - 1), 0.0, ALU.min, ALU.max))
                v.tensor_copy(row_i[:], row_no[:]).then_inc(rows_known, 1)
                link(v.tensor_scalar(block_lo[:], block_no[:], float(P), None, ALU.mult))
                v.tensor_scalar(block_no[:], block_no[:], float(BLOCKS - 1), None, ALU.min).then_inc(steps_known, 1)

                dve.wait_ge(src_in, 16 * STEP_GROUPS)
                link(v.tensor_copy(src_f[:], src_i[:]))
                dve.wait_ge(sdst_in, 16 * STEP_GROUPS)
                link(v.tensor_copy(sdst_f[:], sdst_i[:]))
                for g in range(STEP_GROUPS):
                    link(v.tensor_scalar(local[:, g, :], sdst_f[:, g, :], block_lo[:, g:g + 1], None, ALU.subtract))
                link(v.tensor_scalar(inside[:], local[:], 0.0, None, ALU.is_ge))
                link(v.tensor_scalar(inside_hi[:], local[:], float(P), None, ALU.is_lt))
                link(v.tensor_tensor(inside[:], inside[:], inside_hi[:], ALU.mult))
                for out, of in ((local, local), (key, sdst_f)):
                    link(v.tensor_scalar(out[:], of[:], 1.0, None, ALU.add))
                    link(v.tensor_tensor(out[:], out[:], inside[:], ALU.mult))
                    link(v.tensor_scalar(out[:], out[:], -1.0, None, ALU.add))
                v.tensor_copy(local16[:], local[:]).then_inc(local_known, 1)

                dve.wait_ge(turned, 1)
                v.tensor_copy(k.block_row[:], small[0:1, 128:128 + TABLE])
                for g in range(STEP_GROUPS):
                    for t in range(TPS):
                        at = slice(g * P, (g + 1) * P)
                        v.tensor_copy(k.src_t[:, at, t], pair(0, g, t))
                        v.tensor_copy(k.local_t[:, at, t], pair(1, g, t))
                        link(v.tensor_copy(key_t[:, at, t], pair(2, g, t)))
                used = key_t[:].rearrange("p s t -> p (s t)")[:, 0:TILES].rearrange("p (c g) -> p g c", g=CT)
                v.tensor_copy(key8[:], used.unsqueeze(3).to_broadcast([P, CT, CHUNKS, HEADS])).then_inc(keys_ready, 1)

                dve.wait_ge(keys_turned, 1)
                link(v.tensor_copy(key_s[:], big[:, 0:SLOTS]))
                v.tensor_copy(row_first[0:1, 0, 0:1], key_s[0:1, 0:1]).then_inc(ends_ready, 1)
                link(v.memset(k.fresh[:], 0.0))
                link(v.tensor_tensor(k.fresh[:, 1:SLOTS], key_s[:, 1:], key_s[:, 0:SLOTS - 1], ALU.not_equal))
                link(v.tensor_scalar(k.fresh[:, 1:SLOTS], k.fresh[:, 1:SLOTS], -BIG, None, ALU.mult))
                dve.wait_ge(ends_turned, 1)
                v.tensor_copy(row_first[:], ends[0:1, 0:P].rearrange("p (c h) -> p h c", h=HEADS))
                link(v.tensor_copy(row_last[:], ends[0:1, P:2 * P].rearrange("p (c h) -> p h c", h=HEADS)))
                link(v.memset(goes_on[:], 0.0))
                link(v.tensor_tensor(goes_on[:, :, 1:], row_first[:, :, 1:], row_last[:, :, 0:CHUNKS - 1], ALU.is_equal))
                link(v.tensor_tensor(whole[:], row_first[:], row_last[:], ALU.is_equal))
                for x in (k.link_f, k.link_b, k.seed_b):
                    link(v.memset(x[:], 0.0))
                a, b = slice(1, CHUNKS), slice(0, CHUNKS - 1)
                link(v.tensor_tensor(k.link_f[:, :, a], goes_on[:, :, a], whole[:, :, b], ALU.mult))
                link(v.tensor_tensor(k.link_b[:, :, b], goes_on[:, :, a], whole[:, :, a], ALU.mult))
                link(v.tensor_copy(k.seed_b[:, :, b], goes_on[:, :, a]))
                link(v.tensor_copy(k.seed_f[:], goes_on[:]))
                for x in (k.link_f, k.link_b, k.seed_f, k.seed_b):
                    link(v.tensor_scalar(x[:], x[:], -1.0, BIG, ALU.add, ALU.mult))

            @block.tensor
            def _(pe):
                pe.wait_ge(counted, 1)
                nc.tensor.matmul(small[:, 0:BLOCKS + 1], k.ones[:], count[:], start=True, stop=True).then_inc(summed, 1)
                pe.wait_ge(steps_known, 1)
                pe.wait_ge(local_known, 1)
                for g in range(STEP_GROUPS):
                    nc.tensor.matmul(small[0:1, 128 + g * P:128 + (g + 1) * P], block_no[:, g:g + 1], k.ident[:],
                                     start=True, stop=True)
                for which, table in enumerate((src_f, local, key)):
                    for g in range(STEP_GROUPS):
                        for t in range(TPS):
                            last = nc.tensor.transpose(pair(which, g, t), table[:, g, t * P:(t + 1) * P], k.ident[:])
                last.then_inc(turned, 1)
                pe.wait_ge(keys_ready, 1)
                for g in range(CT):
                    last = nc.tensor.transpose(big[:, g * P:(g + 1) * P],
                                               key8[:, g].rearrange("p c h -> p (c h)"), k.ident[:])
                last.then_inc(keys_turned, 1)
                pe.wait_ge(ends_ready, 1)
                nc.tensor.matmul(ends[0:1, 0:P], key_s[:, 0:1], k.ident[:], start=True, stop=True)
                nc.tensor.matmul(ends[0:1, P:2 * P], key_s[:, SLOTS - 1:SLOTS], k.ident[:],
                                 start=True, stop=True).then_inc(ends_turned, 1)


def load_split(nc, block_of, pieces, stage, split, sems):
    raw_in, hi_done, lo_done = sems
    with nc.Block() as block:
        @block.sync
        def _(sp):
            for n, piece in enumerate(pieces):
                if n >= 2:
                    sp.wait_ge(lo_done, n - 1)
                sp.dma_start(stage[:, n % 2], piece).then_inc(raw_in[n % 2], 16)

        @block.scalar
        def _(act):
            for n in range(len(pieces)):
                act.wait_ge(raw_in[n % 2], 16 * (n // 2 + 1))
                nc.scalar.activation(split[n][0], stage[:, n % 2], ACT.Copy).then_inc(hi_done, 1)

        @block.vector
        def _(dve):
            for n in range(len(pieces)):
                dve.wait_ge(hi_done, n + 1)
                nc.vector.tensor_tensor(split[n][1], stage[:, n % 2], split[n][0].bitcast(F32),
                                        ALU.subtract).then_inc(lo_done, 1)


def split_product(nc, out, a_hi, a_lo, b_hi, b_lo, chunks):
    n = 3 * len(chunks)
    i = 0
    for c in chunks:
        for a, b in ((a_hi, b_hi), (a_hi, b_lo), (a_lo, b_hi)):
            last = nc.tensor.matmul(out, a(c), b(c), start=i == 0, stop=i == n - 1)
            i += 1
    return last


def project(nc, k, layer):
    with ExitStack() as stack:
        ph = Phase(nc, stack, f"proj{layer}")
        OUTS = 4
        w = [[ph.sb(f"w{i}{part}", [P, KC, C], F32R) for part in ("hi", "lo")] for i in range(OUTS)]
        bias = ph.sb("bias", [P, OUTS, C])
        x = ph.sb("x", [P, 2, C])
        enc = ph.sb("enc", [P, 2, C]) if layer else x
        skip = ph.sb("skip", [P, 2, C]) if layer else None
        inv = ph.sb("inv", [P, 2, HEADS]) if layer else None
        xt_hi = ph.sb("xt_hi", [P, 2, KC, P], F32R)
        xt_lo = ph.sb("xt_lo", [P, 2, KC, P], F32R)
        staged = ph.sb("staged", [P, 2, 3, C])
        xt_ps = [ph.ps(f"xt_ps{i}", [P, C]) for i in range(2)]
        out_ps = [ph.ps(f"out_ps{i}", [P, C]) for i in range(OUTS)]
        with ExitStack() as early:
            stage = early.enter_context(nc.sbuf_tensor(f"proj{layer}_stage", [P, 2, KC, C], F32))
            load_split(nc, None, [m[layer].rearrange("(c p) n -> p c n", p=P) for m in (k.Wk, k.Wv, k.Ws, k.Wq)],
                       stage, [(a[:], b[:]) for a, b in w],
                       ([ph.sem("raw_in0"), ph.sem("raw_in1")], ph.sem("hi_done"), ph.sem("lo_done")))

        bias_in = ph.sem("bias_in")
        x_in = [ph.sem("x_in0"), ph.sem("x_in1")]
        x_ready, x_free, turned = ph.sem("x_ready"), ph.sem("x_free"), ph.sem("turned")
        hi_ready, lo_ready, product = ph.sem("hi_ready"), ph.sem("lo_ready"), ph.sem("product")
        out_done, steps, stage_free = ph.sem("out_done"), ph.sem("steps"), ph.sem("stage_free")
        stored = [ph.sem("stored0"), ph.sem("stored1")]
        loads = 2 if layer else 1
        node_rows = lambda b: bass.ds(b * P, P)

        with nc.Block() as block:
            @block.gpsimd
            def _(pool):
                for i, b in enumerate((k.bk, k.bv, k.bs, k.bq)):
                    pool.dma_start(bias[:, i, :], b[layer].partition_broadcast(P)).then_inc(bias_in, 16)
                with pool.Fori(0, BLOCKS // 2) as it:
                    for u in range(2):
                        pool.wait_ge(x_free, 2 * it + u + 1)
                        pool.dma_start(enc[:, u, :], k.x[node_rows(2 * it + u), :]).then_inc(x_in[u], 16)
                        if layer:
                            pool.dma_start(skip[:, u, :], k.skip_d[node_rows(2 * it + u), :]).then_inc(x_in[u], 16)

            @block.tensor
            def _(pe):
                def turn(b, u, it):
                    if layer:
                        pe.wait_ge(x_ready, b + 1)
                    else:
                        pe.wait_ge(x_in[u], 16 * (it + 1))
                    pe.wait_ge(lo_ready, b + 1)
                    for c in range(KC):
                        last = nc.tensor.transpose(xt_ps[u][:, c * P:(c + 1) * P], x[:, u, c * P:(c + 1) * P], k.ident[:])
                    last.then_inc(turned, 1)

                def products(b, u, it, ahead):
                    pe.wait_ge(lo_ready, b + 3)
                    for i in range(OUTS):
                        pe.wait_ge(out_done, OUTS * b + i + 1)
                        split_product(nc, out_ps[i][:], lambda c: xt_hi[:, u, c, :], lambda c: xt_lo[:, u, c, :],
                                      lambda c: w[i][0][:, c, :], lambda c: w[i][1][:, c, :],
                                      range(KC)).then_inc(product, 1)
                        if i == 0 and ahead:
                            turn(b + 1, 1 - u, it + u)

                turn(0, 0, 0)
                with pe.Fori(0, BLOCKS // 2 - 1) as it:
                    for u in range(2):
                        products(2 * it + u, u, it, True)
                products(BLOCKS - 2, 0, BLOCKS // 2 - 1, True)
                products(BLOCKS - 1, 1, BLOCKS // 2 - 1, False)

            @block.scalar
            def _(act):
                with act.Fori(0, BLOCKS // 2) as it:
                    for u in range(2):
                        b = 2 * it + u
                        act.wait_ge(turned, b + 1)
                        act.wait_ge(product, OUTS * b + OUTS)
                        nc.scalar.activation(xt_hi[:, u].rearrange("p c n -> p (c n)"), xt_ps[u][:],
                                             ACT.Copy).then_inc(hi_ready, 1)

            @block.vector
            def _(dve):
                dve.sem_inc(x_free, 2)
                dve.sem_inc(lo_ready, 2)
                dve.sem_inc(out_done, OUTS)
                dve.sem_inc(product, 2 * OUTS)
                dve.wait_ge(bias_in, 16 * OUTS)

                def assemble(b, u, it):
                    dve.wait_ge(x_in[u], 32 * (it + 1))
                    sums = k.work[:, bass.ds(b * AGG, C)]
                    total = k.work[:, bass.ds(b * AGG + C, HEADS)]
                    nc.vector.tensor_scalar(inv[:, u, :], total, 1e-16, None, ALU.add).then_inc(steps, 1)
                    dve.wait_ge(steps, 3 * b + 1)
                    nc.vector.reciprocal(inv[:, u, :], inv[:, u, :]).then_inc(steps, 1)
                    dve.wait_ge(steps, 3 * b + 2)
                    nc.vector.tensor_tensor(x[:, u, :].rearrange("p (h d) -> p h d", h=HEADS),
                                            sums.rearrange("p (h d) -> p h d", h=HEADS),
                                            inv[:, u, :].unsqueeze(2).to_broadcast([P, HEADS, D]), ALU.mult).then_inc(steps, 1)
                    dve.wait_ge(steps, 3 * b + 3)
                    nc.vector.tensor_tensor(x[:, u, :], x[:, u, :], skip[:, u, :], ALU.add).then_inc(x_ready, 1)

                def low_part(b, u):
                    dve.wait_ge(hi_ready, b + 1)
                    nc.vector.tensor_tensor(xt_lo[:, u].rearrange("p c n -> p (c n)"), xt_ps[u][:],
                                            xt_hi[:, u].rearrange("p c n -> p (c n)").bitcast(F32),
                                            ALU.subtract).then_inc(lo_ready, 1)

                def outputs(b, u, ahead):
                    dve.wait_ge(stage_free, b + 1)
                    for i in range(3):
                        dve.wait_ge(product, OUTS * (b + 2) + i + 1)
                        nc.vector.tensor_tensor(staged[:, u, i, :], out_ps[i][:], bias[:, i, :], ALU.add).then_inc(out_done, 1)
                        if i == 0 and ahead:
                            low_part(b + 1, 1 - u)
                    dve.wait_ge(out_done, OUTS * (b + 1) + 3)
                    nc.vector.tensor_tensor(staged[:, u, 2, :], staged[:, u, 2, :], enc[:, u, :], ALU.add).then_inc(x_free, 1)
                    dve.wait_ge(product, OUTS * (b + 2) + 4)
                    nc.vector.tensor_tensor(k.work[:, bass.ds(b * C, C)], out_ps[3][:], bias[:, 3, :],
                                            ALU.add).then_inc(out_done, 1)

                dve.sem_inc(stage_free, 2)
                if layer:
                    assemble(0, 0, 0)
                low_part(0, 0)
                with dve.Fori(0, BLOCKS // 2 - 1) as it:
                    for u in range(2):
                        if layer:
                            assemble(2 * it + u + 1, 1 - u, it + u)
                        outputs(2 * it + u, u, True)
                if layer:
                    assemble(BLOCKS - 1, 1, BLOCKS // 2 - 1)
                outputs(BLOCKS - 2, 0, True)
                outputs(BLOCKS - 1, 1, False)

            @block.sync
            def _(sp):
                with sp.Fori(0, BLOCKS // 2) as it:
                    for u in range(2):
                        b = 2 * it + u
                        first = sp.snap(b * P)
                        sp.wait_ge(out_done, OUTS * (b + 2))
                        for i, table in enumerate((k.k_d, k.v_d, k.skip_d)):
                            sp.dma_start(table[bass.ds(first, P), :], staged[:, u, i, :]).then_inc(stored[u], 16)
                        sp.wait_ge(stored[u], 48 * (it + 1))
                        sp.sem_inc(stage_free, 1)


def score(nc, k, layer):
    with ExitStack() as stack:
        ph = Phase(nc, stack, f"score{layer}")
        rows = ph.sb("rows", [P, RING, TPS, C])
        index = ph.sb("index", [P, 2, HALF * TPS], I32)
        local = ph.sb("local", [P, 2, HALF * SE], BF16)
        hot = ph.sb("hot", [P, 2, HALF * SE])
        prod = ph.sb("prod", [P, RING, TPS, C])
        q_ps = [ph.ps(f"q_ps{i}", [P, TPS, C]) for i in range(2)]

        index_ready = ph.sem("index_ready")
        asked = ph.sem("asked")
        rows_in = [ph.sem(f"rows_in{r}") for r in range(RING)]
        local_in = [ph.sem("local_in0"), ph.sem("local_in1")]
        hot_ready, q_ready = ph.sem("hot_ready"), ph.sem("q_ready")
        multiplied, act_summed, dve_summed = ph.sem("multiplied"), ph.sem("act_summed"), ph.sem("dve_summed")
        half_edges = HALF * SE

        with nc.Block() as block:
            @block.gpsimd
            def _(pool):
                with pool.Fori(0, STEPS // BODY) as it:
                    for q in range(2):
                        nc.gpsimd.tensor_copy(index[:, q, :], src_flat(k)[:, bass.ds((2 * it + q) * HALF * TPS, HALF * TPS)]
                                              ).then_inc(index_ready, 1)
                        pool.wait_ge(index_ready, 2 * it + q + 1)
                        for s in range(HALF):
                            pool.wait_ge(multiplied, BODY * it + HALF * q + s + 1)
                            pool.sem_inc(asked, 1)
                            for t in range(TPS):
                                at = bass.IndirectOffsetOnAxis(ap=index[:, q, s * TPS + t:s * TPS + t + 1], axis=0)
                                nc.gpsimd.indirect_dma_start(rows[:, s % RING, t, :], None, k.k_d, at
                                                             ).then_inc(rows_in[s % RING], 16)

            @block.sync
            def _(sp):
                def load(first, q):
                    sp.dma_start(local[:, q, :], k.local_d[bass.ds(first, half_edges)].partition_broadcast(P)
                                 ).then_inc(local_in[q], 16)

                load(0, 0)
                with sp.Fori(0, STEPS // BODY) as it:
                    for q in range(2):
                        first = sp.snap((2 * it + q + 1) * half_edges)
                        sp.wait_ge(hot_ready, 2 * it + q + 1)
                        load(first, 1 - q)

            @block.tensor
            def _(pe):
                pe.sem_inc(q_ready, HALF)
                with pe.Fori(0, STEPS // BODY) as it:
                    for q in range(2):
                        pe.wait_ge(hot_ready, 2 * it + q + 2)
                        for s in range(HALF):
                            n = BODY * it + HALF * q + s
                            node_block = pe.value_load(k.block_row[0:1, bass.ds(n, 1)], min_val=0, max_val=BLOCKS - 1)
                            pe.wait_ge(multiplied, n + RING - 1)
                            for t in range(TPS):
                                e = (s * TPS + t) * P
                                last = nc.tensor.matmul(q_ps[s % 2][:, t, :], hot[:, q, e:e + P],
                                                        k.work[:, bass.ds(node_block * C, C)], start=True, stop=True)
                            last.then_inc(q_ready, 1)

            @block.vector
            def _(dve):
                def one_hot(half_done, q, times):
                    dve.wait_ge(local_in[q], 16 * times)
                    if half_done is not None:
                        dve.wait_ge(q_ready, half_done)
                    nc.vector.tensor_scalar(hot[:, q, :], local[:, q, :], k.iota_col[:, 0:1], None,
                                            ALU.is_equal).then_inc(hot_ready, 1)

                def multiply(n, s, times):
                    dve.wait_ge(rows_in[s % RING], 16 * TPS * times)
                    dve.wait_ge(q_ready, n + HALF + 1)
                    dve.wait_ge(act_summed, n + 1)
                    dve.wait_ge(dve_summed, n + 1)
                    nc.vector.tensor_tensor(prod[:, s % RING], q_ps[s % 2][:], rows[:, s % RING], ALU.mult
                                            ).then_inc(multiplied, 1)

                def add_up(n, s):
                    dve.wait_ge(multiplied, n + RING + 1)
                    nc.vector.tensor_reduce(
                        k.edge[:, bass.ds(n * TPS, TPS), 0:DVE_HEADS1],
                        prod[:, s % RING, :, 0:DVE_HEADS1 * D].rearrange("p t (h d) -> p t h d", d=D), AX.X, ALU.add
                    ).then_inc(dve_summed, 1)

                dve.sem_inc(multiplied, RING)
                dve.sem_inc(dve_summed, RING)
                dve.sem_inc(hot_ready, 1)
                one_hot(None, 0, 1)
                with dve.Fori(0, STEPS // BODY) as it:
                    for q in range(2):
                        n = BODY * it + HALF * q
                        multiply(n, 0, 2 * it + q + 1)
                        one_hot(HALF * (2 * it + q) + HALF, 1 - q, it + q + 1)
                        for s in range(1, HALF):
                            multiply(n + s, s, 2 * it + q + 1)
                            add_up(n + s - 1, s - 1)
                        add_up(n + HALF - 1, HALF - 1)

            @block.scalar
            def _(act):
                act.sem_inc(act_summed, RING)
                with act.Fori(0, STEPS // BODY) as it:
                    for s in range(BODY):
                        n = BODY * it + s
                        act.wait_ge(multiplied, n + RING + 1)
                        for t in range(TPS):
                            for h in range(DVE_HEADS1, HEADS):
                                at = prod[:, s % RING, t, h * D:(h + 1) * D]
                                last = nc.scalar.activation(
                                    at, at, ACT.Copy,
                                    accum_out=k.edge[:, bass.ds(n * TPS + t, 1), h:h + 1].rearrange("p a b -> p (a b)"))
                        last.then_inc(act_summed, 1)


def src_flat(k):
    return k.src_t[:].rearrange("p s t -> p (s t)")


def soften(nc, k, layer):
    with ExitStack() as stack:
        ph = Phase(nc, stack, f"soft{layer}")
        fwd = ph.sb("fwd", [P, SLOTS])
        bwd = ph.sb("bwd", [P, SLOTS])
        seeds = [ph.sb(f"seeds{i}", [1, HEADS, CHUNKS]) for i in range(2)]
        carry = [ph.sb(f"carry{i}", [1, HEADS, CHUNKS]) for i in range(2)]
        carry_ch = [ph.sb(f"carry_ch{i}", [1, CHUNKS, HEADS]) for i in range(2)]
        carry_col = ph.sb("carry_col", [P, 2])
        big = ph.ps("big", [P, 6 * 512])
        small = ph.ps("small", [P, 512])
        cols = ph.ps("cols", [P, 512])
        sorted_out, turned = ph.sem("sorted_out"), ph.sem("turned")
        ends_ready, ends_turned = ph.sem("ends_ready"), ph.sem("ends_turned")
        carry_ready, carry_turned = ph.sem("carry_ready"), ph.sem("carry_turned")
        less_max, raised, back, steps = ph.sem("less_max"), ph.sem("raised"), ph.sem("back"), ph.sem("steps")
        scores = k.edge[:].rearrange("p (c g) h -> p g c h", g=CT)
        flat = lambda x: x[:].rearrange("p h c -> p (h c)")
        flip = lambda x: x[:, ::-1]
        QUART = 4

        with nc.Block() as block:
            @block.tensor
            def _(pe):
                pe.wait_ge(sorted_out, 1)
                for g in range(CT):
                    last = nc.tensor.transpose(big[:, g * P:(g + 1) * P], fwd[:, g * P:(g + 1) * P], k.ident[:])
                last.then_inc(turned, 1)
                pe.wait_ge(ends_ready, 1)
                nc.tensor.matmul(small[0:1, 0:P], fwd[:, SLOTS - 1:SLOTS], k.ident[:], start=True, stop=True)
                nc.tensor.matmul(small[0:1, P:2 * P], bwd[:, 0:1], k.ident[:], start=True, stop=True).then_inc(ends_turned, 1)
                pe.wait_ge(carry_ready, 1)
                for i in range(2):
                    last = nc.tensor.matmul(cols[:, i:i + 1], carry_ch[i][:].rearrange("p c h -> p (c h)"),
                                            k.ones[0:1, 0:1], start=True, stop=True)
                last.then_inc(carry_turned, 1)
                pe.wait_ge(raised, 1)
                for g in range(CT):
                    last = nc.tensor.transpose(big[:, g * P:(g + 1) * P], bwd[:, g * P:(g + 1) * P], k.ident[:])
                    if g % QUART == QUART - 1 or g == CT - 1:
                        last.then_inc(back, 1)

            @block.vector
            def _(dve):
                link = chain(dve, steps)
                v = nc.vector
                scan = lambda out, flags, data, first: v.tensor_tensor_scan(out, flags, data, first, ALU.add, ALU.max)
                before, after = k.fresh[:, 0:SLOTS], k.fresh[:, 1:SLOTS + 1]
                v.tensor_copy(fwd[:].rearrange("p (g c h) -> p g c h", g=CT, h=HEADS), scores).then_inc(sorted_out, 1)
                for x in seeds:
                    v.memset(x[:], -BIG)
                dve.wait_ge(turned, 1)
                link(scan(fwd[:], before, big[:, 0:SLOTS], -BIG))
                scan(flip(bwd), flip(after), flip(big[:, 0:SLOTS]), -BIG).then_inc(ends_ready, 1)
                dve.wait_ge(ends_turned, 1)
                a, b = slice(1, CHUNKS), slice(0, CHUNKS - 1)
                last_f = small[0:1, 0:P].rearrange("p (c h) -> p h c", h=HEADS)
                first_b = small[0:1, P:2 * P].rearrange("p (c h) -> p h c", h=HEADS)
                link(v.tensor_tensor(seeds[0][:, :, a], last_f[:, :, b], k.seed_f[:, :, a], ALU.add))
                link(v.tensor_tensor(seeds[1][:, :, b], first_b[:, :, a], k.seed_b[:, :, b], ALU.add))
                link(scan(flat(carry[0]), flat(k.link_f), flat(seeds[0]), -BIG))
                link(scan(flip(flat(carry[1])), flip(flat(k.link_b)), flip(flat(seeds[1])), -BIG))
                v.tensor_copy(carry_ch[0][:], carry[0][:].rearrange("p h c -> p c h"))
                v.tensor_copy(carry_ch[1][:], carry[1][:].rearrange("p h c -> p c h")).then_inc(carry_ready, 1)
                dve.wait_ge(carry_turned, 1)
                link(v.tensor_copy(carry_col[:], cols[:, 0:2]))
                link(scan(fwd[:], before, big[:, 0:SLOTS], carry_col[:, 0:1]))
                link(scan(flip(bwd), flip(after), flip(big[:, 0:SLOTS]), carry_col[:, 1:2]))
                link(v.tensor_tensor(fwd[:], fwd[:], bwd[:], ALU.max))
                v.tensor_tensor(fwd[:], big[:, 0:SLOTS], fwd[:], ALU.subtract).then_inc(less_max, 1)
                for n, g in enumerate(range(0, CT, QUART)):
                    if n % 2 == 0:
                        m = min(QUART, CT - g)
                        dve.wait_ge(back, n + 1)
                        v.tensor_copy(scores[:, g:g + m],
                                      big[:, g * P:(g + m) * P].rearrange("p (g c h) -> p g c h", g=m, h=HEADS))

            @block.scalar
            def _(act):
                act.wait_ge(less_max, 1)
                nc.scalar.activation(bwd[:], fwd[:], ACT.Exp, scale=float(D) ** -0.5).then_inc(raised, 1)
                for n, g in enumerate(range(0, CT, QUART)):
                    if n % 2 == 1:
                        m = min(QUART, CT - g)
                        act.wait_ge(back, n + 1)
                        nc.scalar.activation(scores[:, g:g + m],
                                             big[:, g * P:(g + m) * P].rearrange("p (g c h) -> p g c h", g=m, h=HEADS),
                                             ACT.Copy)

            @block.gpsimd
            def _(pool):
                nc.gpsimd.memset(k.work[:], 0.0)


def collect(nc, k, layer):
    with ExitStack() as stack:
        ph = Phase(nc, stack, f"coll{layer}")
        rows = ph.sb("rows", [P, RING, TPS, C])
        index = ph.sb("index", [P, 2, HALF * TPS], I32)
        hot = ph.sb("hot", [P, 2, HALF * TPS, P])
        ev = ph.sb("ev", [P, 2, TPS, C])
        sum_ps = [ph.ps(f"sum_ps{i}", [P, 2 * C]) for i in range(2)]

        index_ready = ph.sem("index_ready")
        asked = ph.sem("asked")
        rows_in = [ph.sem(f"rows_in{r}") for r in range(RING)]
        hot_ready, ev_dve, ev_act = ph.sem("hot_ready"), ph.sem("ev_dve"), ph.sem("ev_act")
        summed, added = ph.sem("summed"), ph.sem("added")
        local_flat = k.local_t[:].rearrange("p s t -> p (s t)")

        with nc.Block() as block:
            @block.gpsimd
            def _(pool):
                with pool.Fori(0, STEPS // BODY) as it:
                    for q in range(2):
                        nc.gpsimd.tensor_copy(index[:, q, :], src_flat(k)[:, bass.ds((2 * it + q) * HALF * TPS, HALF * TPS)]
                                              ).then_inc(index_ready, 1)
                        pool.wait_ge(index_ready, 2 * it + q + 1)
                        for s in range(HALF):
                            pool.wait_ge(ev_dve, BODY * it + HALF * q + s + 1)
                            pool.wait_ge(ev_act, BODY * it + HALF * q + s + 1)
                            pool.sem_inc(asked, 1)
                            for t in range(TPS):
                                at = bass.IndirectOffsetOnAxis(ap=index[:, q, s * TPS + t:s * TPS + t + 1], axis=0)
                                nc.gpsimd.indirect_dma_start(rows[:, s % RING, t, :], None, k.v_d, at
                                                             ).then_inc(rows_in[s % RING], 16)

            @block.vector
            def _(dve):
                def one_hot(half, half_done, q):
                    if half_done is not None:
                        dve.wait_ge(summed, half_done)
                    n = HALF * TPS
                    nc.vector.tensor_tensor(hot[:, q], k.iota_row[:].unsqueeze(1).to_broadcast([P, n, P]),
                                            local_flat[:, bass.ds(half * n, n)].unsqueeze(2).to_broadcast([P, n, P]),
                                            ALU.is_equal).then_inc(hot_ready, 1)

                def weigh(n, s, times):
                    dve.wait_ge(rows_in[s % RING], 16 * TPS * times)
                    dve.wait_ge(summed, n + RING - 1)
                    cut = DVE_HEADS2 * D
                    nc.vector.tensor_tensor(
                        ev[:, s % 2, :, 0:cut].rearrange("p t (h d) -> p t h d", d=D),
                        rows[:, s % RING, :, 0:cut].rearrange("p t (h d) -> p t h d", d=D),
                        k.edge[:, bass.ds(n * TPS, TPS), 0:DVE_HEADS2].unsqueeze(3).to_broadcast([P, TPS, DVE_HEADS2, D]),
                        ALU.mult).then_inc(ev_dve, 1)

                def add(n, s):
                    node_block = dve.value_load(k.block_row[0:1, bass.ds(n, 1)], min_val=0, max_val=BLOCKS - 1)
                    at = k.work[:, bass.ds(node_block * AGG, AGG)]
                    dve.wait_ge(summed, n + RING + 1)
                    dve.wait_ge(added, n + 2)
                    nc.vector.tensor_tensor(at, at, sum_ps[s % 2][:, 0:AGG], ALU.add).then_inc(added, 1)

                dve.sem_inc(ev_dve, RING)
                dve.sem_inc(summed, RING)
                dve.sem_inc(added, 2)
                one_hot(0, None, 0)
                weigh(0, 0, 1)

                def body(it, last):
                    for s in range(BODY):
                        n = BODY * it + s
                        if s % HALF == 1:
                            half = 2 * it + s // HALF
                            one_hot(half + 1, HALF * half + HALF, 1 - s // HALF)
                        if not (last and s == BODY - 1):
                            nxt = s + 1
                            weigh(n + 1, nxt % RING, 2 * it + nxt // HALF + 1)
                        add(n, s)

                with dve.Fori(0, STEPS // BODY - 1) as it:
                    body(it, False)
                body(STEPS // BODY - 1, True)

            @block.scalar
            def _(act):
                act.sem_inc(ev_act, RING)
                with act.Fori(0, STEPS // BODY) as it:
                    for s in range(BODY):
                        n = BODY * it + s
                        act.wait_ge(rows_in[s % RING], 16 * TPS * (2 * it + s // HALF + 1))
                        act.wait_ge(summed, n + RING - 1)
                        for t in range(TPS):
                            for h in range(DVE_HEADS2, HEADS):
                                last = nc.scalar.activation(
                                    ev[:, s % 2, t, h * D:(h + 1) * D], rows[:, s % RING, t, h * D:(h + 1) * D], ACT.Copy,
                                    scale=k.edge[:, bass.ds(n * TPS + t, 1), h:h + 1].rearrange("p a b -> p (a b)"))
                        last.then_inc(ev_act, 1)

            @block.tensor
            def _(pe):
                with pe.Fori(0, STEPS // BODY) as it:
                    for s in range(BODY):
                        n, q = BODY * it + s, s // HALF
                        if s % HALF == 0:
                            pe.wait_ge(hot_ready, 2 * it + q + 1)
                        pe.wait_ge(ev_dve, n + RING + 1)
                        pe.wait_ge(ev_act, n + RING + 1)
                        pe.wait_ge(added, n + 1)
                        for t in range(TPS):
                            m = hot[:, q, (s % HALF) * TPS + t, :]
                            nc.tensor.matmul(sum_ps[s % 2][:, 0:C], m, ev[:, s % 2, t, :], start=t == 0, stop=t == TPS - 1)
                            last = nc.tensor.matmul(sum_ps[s % 2][:, C:AGG], m,
                                                    k.edge[:, bass.ds(n * TPS + t, 1), :].rearrange("p a h -> p (a h)"),
                                                    start=t == 0, stop=t == TPS - 1)
                        last.then_inc(summed, 1)


def finish(nc, k):
    GB = 4
    GROUPS = BLOCKS // GB
    GN = GB * P
    with ExitStack() as stack:
        ph = Phase(nc, stack, "mlp")
        w1 = [ph.sb(f"w1{part}", [P, KC, HID], F32R) for part in ("hi", "lo")]
        w2 = [ph.sb(f"w2{part}", [P, FC, C], F32R) for part in ("hi", "lo")]
        with ExitStack() as early:
            stage = early.enter_context(nc.sbuf_tensor("mlp_stage", [P, 2, KC, C], F32))
            w1_v = k.W1.rearrange("(c p) n -> p c n", p=P)
            w2_v = k.W2.rearrange("(c p) n -> p c n", p=P)
            pieces = [w1_v[:, :, i * C:(i + 1) * C] for i in range(2)] + [w2_v[:, i * KC:(i + 1) * KC, :] for i in range(2)]
            split = [[part[:, :, i * C:(i + 1) * C] for part in w1] for i in range(2)]
            split += [[part[:, i * KC:(i + 1) * KC, :] for part in w2] for i in range(2)]
            load_split(nc, None, pieces, stage, split,
                       ([ph.sem("raw_in0"), ph.sem("raw_in1")], ph.sem("hi_done"), ph.sem("lo_done")))
        gain, shift, b2 = (ph.sb(n, [P, C]) for n in ("gain", "shift", "b2"))
        b1 = ph.sb("b1", [P, FC])
        skip = ph.sb("skip", [P, 2, C])
        enc = ph.sb("enc", [P, 2, C])
        x = ph.sb("x", [P, 2, C])
        y = ph.sb("y", [P, 2, GB, C])
        yt_hi = ph.sb("yt_hi", [P, KC, GN], F32R)
        yt_lo = ph.sb("yt_lo", [P, KC, GN], F32R)
        h_all = ph.sb("h_all", [P, 2, GN])
        h_hi = ph.sb("h_hi", [P, FC, GN], F32R)
        h_lo = ph.sb("h_lo", [P, FC, GN], F32R)
        z = ph.sb("z", [P, 2, C])
        inv = ph.sb("inv", [P, HEADS])
        stats = ph.sb("stats", [P, 6])
        mean_var = ph.sb("mean_var", [P, 2])
        std = ph.sb("std", [P, 1])
        scale = ph.sb("scale", [P, 1])
        yt_ps = [ph.ps(f"yt_ps{i}", [P, C]) for i in range(2)]
        h_ps = [ph.ps(f"h_ps{i}", [P, GN]) for i in range(2)]
        z_ps = [ph.ps(f"z_ps{i}", [P, C]) for i in range(2)]

        const_in, b1_in = ph.sem("const_in"), ph.sem("b1_in")
        skip_in = [ph.sem("skip_in0"), ph.sem("skip_in1")]
        enc_in = [ph.sem("enc_in0"), ph.sem("enc_in1")]
        skip_free, enc_free = ph.sem("skip_free"), ph.sem("enc_free")
        steps, var_known, std_known = ph.sem("steps"), ph.sem("var_known"), ph.sem("std_known")
        y_ready, turned, y_hi, y_lo = ph.sem("y_ready"), ph.sem("turned"), ph.sem("y_hi"), ph.sem("y_lo")
        h_product, h_taken, h_split = ph.sem("h_product"), ph.sem("h_taken"), ph.sem("h_split")
        z_product, z_taken = ph.sem("z_product"), ph.sem("z_taken")
        out_ready, out_free = ph.sem("out_ready"), ph.sem("out_free")
        stored = [ph.sem("stored0"), ph.sem("stored1")]

        with nc.Block() as block:
            @block.gpsimd
            def _(pool):
                for t, a in ((gain, k.ln_g), (shift, k.ln_b), (b2, k.b2)):
                    pool.dma_start(t[:], a.partition_broadcast(P)).then_inc(const_in, 16)
                with pool.Fori(0, BLOCKS // 2) as it:
                    for u in range(2):
                        b = 2 * it + u
                        pool.wait_ge(skip_free, b + 1)
                        pool.dma_start(skip[:, u, :], k.skip_d[bass.ds(b * P, P), :]).then_inc(skip_in[u], 16)

            @block.sync
            def _(sp):
                with nc.allow_non_contiguous_dma(reason="a few hundred elements"):
                    sp.dma_start(b1[:], k.b1.rearrange("(c p) -> p c", p=P)).then_inc(b1_in, 16)

                def load(b, u):
                    first = sp.snap(b * P)
                    sp.wait_ge(enc_free, b + 1)
                    sp.dma_start(enc[:, u, :], k.x[bass.ds(first, P), :]).then_inc(enc_in[u], 16)

                def store(b, u, it, rows):
                    first = sp.snap(b * P)
                    sp.wait_ge(out_ready, b + 1)
                    sp.dma_start(k.out[bass.ds(first, rows), :], z[0:rows, u, :]).then_inc(stored[u], 16)
                    sp.wait_ge(stored[u], 16 * (it + 1))
                    sp.sem_inc(out_free, 1)

                load(0, 0)
                with sp.Fori(0, BLOCKS // 2 - 1) as it:
                    for u in range(2):
                        load(2 * it + u + 1, 1 - u)
                        store(2 * it + u, u, it, P)
                load(BLOCKS - 1, 1)
                store(BLOCKS - 2, 0, BLOCKS // 2 - 1, P)
                store(BLOCKS - 1, 1, BLOCKS // 2 - 1, NODES - (BLOCKS - 1) * P)

            @block.vector
            def _(dve):
                v = nc.vector
                dve.sem_inc(skip_free, 2)
                dve.sem_inc(enc_free, 2)
                dve.sem_inc(z_taken, 2)
                dve.sem_inc(h_split, 2)

                LINKS_A, LINKS_C, NORMS = 9, 12, 3

                def norm(out, of, tick, norms):
                    tick(v.bn_stats(stats[:], of))
                    v.bn_aggr(mean_var[:], stats[:]).then_inc(var_known, 1)
                    dve.wait_ge(std_known, norms)
                    tick(v.reciprocal(scale[:], std[:]))
                    return v.tensor_scalar(out, of, mean_var[:, 0:1], scale[:, 0:1], ALU.subtract, ALU.mult)

                def ticker(base):
                    count = [0]

                    def tick(ins):
                        count[0] += 1
                        ins.then_inc(steps, 1)
                        dve.wait_ge(steps, base + count[0])

                    return tick

                def first_norm(g, par, i, base, norms):
                    u = i % 2
                    b = GB * g + i
                    tick = ticker(base)
                    sums = k.work[:, bass.ds(b * AGG, C)]
                    tick(v.tensor_scalar(inv[:], k.work[:, bass.ds(b * AGG + C, HEADS)], 1e-16, None, ALU.add))
                    tick(v.reciprocal(inv[:], inv[:]))
                    tick(v.tensor_tensor(x[:, u, :].rearrange("p (h d) -> p h d", h=HEADS),
                                         sums.rearrange("p (h d) -> p h d", h=HEADS),
                                         inv[:].unsqueeze(2).to_broadcast([P, HEADS, D]), ALU.mult))
                    dve.wait_ge(skip_in[u], 16 * (GB // 2 * g + i // 2 + 1))
                    tick(v.tensor_tensor(x[:, u, :], x[:, u, :], skip[:, u, :], ALU.add))
                    dve.sem_inc(skip_free, 1)
                    tick(norm(x[:, u, :], x[:, u, :], tick, norms))
                    tick(v.tensor_tensor(x[:, u, :], x[:, u, :], gain[:], ALU.mult))
                    v.tensor_tensor(y[:, par, i, :], x[:, u, :], shift[:], ALU.add).then_inc(y_ready, 1)

                def y_low(g, i):
                    b = GB * g + i
                    dve.wait_ge(y_hi, b + 1)
                    v.tensor_tensor(yt_lo[:, :, i * P:(i + 1) * P], yt_ps[i % 2][:].rearrange("p (c n) -> p c n", c=KC),
                                    yt_hi[:, :, i * P:(i + 1) * P].bitcast(F32), ALU.subtract).then_inc(y_lo, 1)

                def h_low(g):
                    for f in range(FC):
                        dve.wait_ge(h_taken, 2 * (FC * g + f + 1))
                        v.tensor_tensor(h_lo[:, f, :], h_all[:, f % 2, :], h_hi[:, f, :].bitcast(F32),
                                        ALU.subtract).then_inc(h_split, 1)

                def last_norms(g, par, i, base, norms):
                    u = i % 2
                    b = GB * g + i
                    tick = ticker(base)
                    at = z[:, u, :]
                    dve.wait_ge(z_product, b + 1)
                    dve.wait_ge(out_free, b + 1)
                    ins = v.tensor_tensor(at, z_ps[u][:], b2[:], ALU.add)
                    ins.then_inc(z_taken, 1)
                    dve.wait_ge(z_taken, b + 3)
                    tick(v.tensor_tensor(at, at, y[:, par, i, :], ALU.add))
                    tick(norm(at, at, tick, norms))
                    tick(v.tensor_tensor(at, at, gain[:], ALU.mult))
                    tick(v.tensor_tensor(at, at, shift[:], ALU.add))
                    dve.wait_ge(enc_in[u], 16 * (GB // 2 * g + i // 2 + 1))
                    tick(v.tensor_tensor(at, at, enc[:, u, :], ALU.add))
                    tick(v.tensor_tensor(at, at, enc[:, u, :], ALU.add))
                    dve.sem_inc(enc_free, 1)
                    norm(at, at, tick, norms + 1).then_inc(out_ready, 1)

                A, Z = 8, 10
                dve.sem_inc(out_free, 2)
                dve.wait_ge(const_in, 48)

                def first_norms(g, par, tick0, norm0):
                    for i in range(GB):
                        first_norm(g, par, i, tick0 + A * i, norm0 + i + 1)

                def rest(g, par, tick0, norm0):
                    for i in range(GB):
                        last_norms(g, par, i, tick0 + Z * i, norm0 + 2 * i + 1)

                per_ticks, per_norms = GB * (A + Z), GB * 3
                first_norms(0, 0, 0, 0)
                for i in range(GB):
                    y_low(0, i)
                for g in range(GROUPS):
                    h_low(g)
                    tick0, norm0 = GB * A + per_ticks * g, GB + per_norms * g
                    if g + 1 < GROUPS:
                        first_norms(g + 1, (g + 1) % 2, tick0, norm0)
                        for i in range(GB):
                            y_low(g + 1, i)
                        tick0, norm0 = tick0 + GB * A, norm0 + GB
                    rest(g, g % 2, tick0, norm0)

            @block.scalar
            def _(act):
                act.wait_ge(b1_in, 16)

                def roots(first, n):
                    for m in range(n):
                        act.wait_ge(var_known, first + m + 1)
                        nc.scalar.activation(std[:], mean_var[:, 1:2], ACT.Sqrt, bias=k.eps[:, 0:1]).then_inc(std_known, 1)

                def y_high(g, i):
                    b = GB * g + i
                    act.wait_ge(turned, b + 1)
                    nc.scalar.activation(yt_hi[:, :, i * P:(i + 1) * P], yt_ps[i % 2][:].rearrange("p (c n) -> p c n", c=KC),
                                         ACT.Copy).then_inc(y_hi, 1)

                def h_high(g):
                    for f in range(FC):
                        n = FC * g + f
                        act.wait_ge(h_product, n + 1)
                        act.wait_ge(h_split, n + 1)
                        nc.scalar.activation(h_all[:, f % 2, :], h_ps[f % 2][:], ACT.Relu, bias=b1[:, f:f + 1]).then_inc(h_taken, 1)
                        nc.scalar.activation(h_hi[:, f, :], h_ps[f % 2][:], ACT.Relu, bias=b1[:, f:f + 1]).then_inc(h_taken, 1)

                roots(0, GB)
                for i in range(GB):
                    y_high(0, i)
                for g in range(GROUPS):
                    h_high(g)
                    norms = GB + 3 * GB * g
                    if g + 1 < GROUPS:
                        roots(norms, GB)
                        for i in range(GB):
                            y_high(g + 1, i)
                        norms += GB
                    roots(norms, 2 * GB)

            @block.tensor
            def _(pe):
                def turn(g, par):
                    for i in range(GB):
                        b = GB * g + i
                        pe.wait_ge(y_ready, b + 1)
                        if b >= 2:
                            pe.wait_ge(y_lo, b - 1)
                        for c in range(KC):
                            last = nc.tensor.transpose(yt_ps[i % 2][:, c * P:(c + 1) * P],
                                                       y[:, par, i, c * P:(c + 1) * P], k.ident[:])
                        last.then_inc(turned, 1)

                turn(0, 0)
                for g in range(GROUPS):
                    pe.wait_ge(y_lo, GB * (g + 1))
                    for f in range(FC):
                        n = FC * g + f
                        if n >= 2:
                            pe.wait_ge(h_taken, 2 * (n - 1))
                        split_product(nc, h_ps[f % 2][:], lambda c: w1[0][:, c, f * P:(f + 1) * P],
                                      lambda c: w1[1][:, c, f * P:(f + 1) * P], lambda c: yt_hi[:, c, :],
                                      lambda c: yt_lo[:, c, :], range(KC)).then_inc(h_product, 1)
                    pe.wait_ge(h_split, FC * (g + 1) + 2)
                    for i in range(GB):
                        b = GB * g + i
                        pe.wait_ge(z_taken, b + 1)
                        at = slice(i * P, (i + 1) * P)
                        split_product(nc, z_ps[i % 2][:], lambda f: h_hi[:, f, at], lambda f: h_lo[:, f, at],
                                      lambda f: w2[0][:, f, :], lambda f: w2[1][:, f, :], range(FC)).then_inc(z_product, 1)
                        if i == 1 and g + 1 < GROUPS:
                            turn(g + 1, (g + 1) % 2)


def graph_attention(nc, x, src, dst, Wq, bq, Wk, bk, Wv, bv, Ws, bs, W1, b1, W2, b2, ln_g, ln_b, out):
    k = Shared()
    k.x, k.src, k.dst, k.out = x, src, dst, out
    k.Wq, k.bq, k.Wk, k.bk, k.Wv, k.bv, k.Ws, k.bs = Wq, bq, Wk, bk, Wv, bv, Ws, bs
    k.W1, k.b1, k.W2, k.b2, k.ln_g, k.ln_b = W1, b1, W2, b2, ln_g, ln_b
    k.k_d, k.v_d, k.skip_d = (nc.dram_tensor(n, [ROWS, C], F32).ap() for n in ("k_rows", "v_rows", "skip_rows"))
    k.local_d = nc.dram_tensor("local_dst", [TABLE * SE], BF16).ap()
    with ExitStack() as stack:
        ph = Phase(nc, stack, "all")
        k.ident, k.iota_row, k.ones = (ph.sb(n, [P, P]) for n in ("ident", "iota_row", "ones"))
        k.iota_col, k.eps = ph.sb("iota_col", [P, 1]), ph.sb("eps", [P, 1])
        k.work = ph.sb("work", [P, BLOCKS * AGG])
        build_constants(nc, k)
        with ExitStack() as graph:
            gr = Phase(nc, graph, "graph")
            k.src_t = gr.sb("src_t", [P, TABLE, TPS], I32)
            k.local_t = gr.sb("local_t", [P, TABLE, TPS])
            k.block_row = gr.sb("block_row", [1, TABLE], I32)
            k.fresh = gr.sb("fresh", [P, SLOTS + 1])
            k.link_f, k.link_b, k.seed_f, k.seed_b = (gr.sb(n, [1, HEADS, CHUNKS])
                                                      for n in ("link_f", "link_b", "seed_f", "seed_b"))
            build_step_tables(nc, k)
            for layer in range(LAYERS):
                project(nc, k, layer)
                with ExitStack() as edges:
                    k.edge = Phase(nc, edges, f"layer{layer}").sb("edge", [P, TILES, HEADS])
                    score(nc, k, layer)
                    soften(nc, k, layer)
                    collect(nc, k, layer)
        finish(nc, k)


_WEIGHTS = ["Wq", "bq", "Wk", "bk", "Wv", "bv", "Ws", "bs", "W1", "b1", "W2", "b2", "ln_g", "ln_b"]


def kernel(**inputs):
    import numpy as _np
    import concourse.bacc as _bacc
    from concourse.bass_utils import run_bass_kernel_spmd as _run

    x = _np.zeros((ROWS, C), _np.float32)
    x[:NODES] = inputs["x"]
    src = _np.zeros((EDGE_ROWS, SE), _np.int32)
    src.reshape(-1)[:EDGES] = inputs["src"]
    dst = _np.full(EDGE_ROWS * SE, PAD_DST, _np.int32)
    dst[:EDGES] = inputs["dst"]
    arrays = {"x": x, "src": src, "dst": dst}
    for name in _WEIGHTS:
        arrays[name] = _np.ascontiguousarray(inputs[f"L0_gnn_{name}"])

    nc = _bacc.Bacc("TRN2", target_bir_lowering=False, num_devices=1)
    args = {n: nc.dram_tensor(f"in_{n}", a.shape, mybir.dt.from_np(a.dtype), kind="ExternalInput").ap()
            for n, a in arrays.items()}
    out = nc.dram_tensor("out_0", (NODES, C), F32, kind="ExternalOutput").ap()
    graph_attention(nc, out=out, **args)
    r = _run(nc, [{f"in_{n}": a for n, a in arrays.items()}], core_ids=[0])
    return r.results[0]["out_0"]
```

```python
import concourse.bass as bass
from concourse import mybir
from contextlib import ExitStack

F32 = mybir.dt.float32
F32R = mybir.dt.float32r
BF16 = mybir.dt.bfloat16
I32 = mybir.dt.int32
ALU = mybir.AluOpType
ACT = mybir.ActivationFunctionType
AX = mybir.AxisListType

P = 128
NODES, EDGES, C, HEADS, LAYERS = 2500, 40000, 512, 8, 2
HID = 2 * C
D = C // HEADS
KC = C // P
FC = HID // P
BLOCKS = -(-NODES // P)
ROWS = BLOCKS * P
TPS = 2
SE = TPS * P
EDGE_ROWS = -(-EDGES // SE)
STEPS = EDGE_ROWS + BLOCKS - 1
TILES = STEPS * TPS
STEP_GROUPS = 2
TABLE = STEP_GROUPS * P
CHUNKS = P // HEADS
CT = TILES // CHUNKS
SLOTS = CT * P
HALF = 8
BODY = 2 * HALF
RING = HALF
PRODS = 4
SUMS = 4
HOT_STEPS, HOTS = 2, 4
AGG = C + HEADS
DVE_HEADS1, DVE_HEADS2 = 4, 5
BIG = 1e30
PAD_DST = 1 << 20
EPS = 1e-5
assert STEPS % BODY == 0 and TILES % CHUNKS == 0 and STEPS + HALF <= TABLE


class Shared:
    pass


class Phase:

    def __init__(self, nc, stack, tag):
        self.nc, self.stack, self.tag, self.sems = nc, stack, tag, []

    def sb(self, name, shape, dt=F32):
        return self.stack.enter_context(self.nc.sbuf_tensor(f"{self.tag}_{name}", shape, dt))

    def ps(self, name, shape):
        return self.stack.enter_context(self.nc.psum_tensor(f"{self.tag}_{name}", shape, F32))

    def sem(self, name):
        self.sems.append(self.nc.alloc_semaphore(f"{self.tag}_{name}"))
        return self.sems[-1]

    def give_back(self):
        self.nc.clear_and_free_semaphores(self.sems)
        self.nc.all_engine_barrier()


def chain(eng, sem):
    count = [0]

    def link(ins):
        count[0] += 1
        ins.then_inc(sem, 1)
        eng.wait_ge(sem, count[0])

    return link


def build_constants(nc, k):
    with ExitStack() as stack:
        ph = Phase(nc, stack, "const")
        row_i = ph.sb("row_i", [P, P], I32)
        col_i = ph.sb("col_i", [P, 1], I32)
        iotas_done, steps = ph.sem("iotas_done"), ph.sem("steps")
        with nc.Block() as block:
            @block.gpsimd
            def _(pool):
                nc.gpsimd.iota(row_i[:], pattern=[[1, P]], base=0, channel_multiplier=0).then_inc(iotas_done, 1)
                nc.gpsimd.iota(col_i[:], pattern=[[0, 1]], base=0, channel_multiplier=1).then_inc(iotas_done, 1)

            @block.vector
            def _(dve):
                link = chain(dve, steps)
                nc.vector.memset(k.ones[:], 1.0)
                nc.vector.memset(k.eps[:], EPS)
                dve.wait_ge(iotas_done, 2)
                nc.vector.tensor_copy(k.iota_row[:], row_i[:])
                link(nc.vector.tensor_copy(k.iota_col[:], col_i[:]))
                link(nc.vector.tensor_scalar(k.ident[:], k.iota_row[:], k.iota_col[:, 0:1], None, ALU.is_equal))


def build_step_tables(nc, k):
    with ExitStack() as stack:
        ph = Phase(nc, stack, "tab")
        cols = EDGE_ROWS * SE // P
        dst_i = ph.sb("dst_i", [P, cols], I32)
        dst_f = ph.sb("dst_f", [P, cols])
        bound_i = ph.sb("bound_i", [P, BLOCKS + 1], I32)
        bound = ph.sb("bound", [P, BLOCKS + 1])
        below = ph.sb("below", [P, BLOCKS + 1, cols])
        count = ph.sb("count", [P, BLOCKS + 1])
        start = ph.sb("start", [P, BLOCKS + 1])
        start_i = ph.sb("start_i", [P, BLOCKS + 1], I32)
        first_row = ph.sb("first_row", [P, BLOCKS])
        stop_row = ph.sb("stop_row", [P, BLOCKS])
        n_steps = ph.sb("n_steps", [P, BLOCKS])
        zeros = ph.sb("zeros", [P, BLOCKS])
        steps_end = ph.sb("steps_end", [P, BLOCKS])
        lead = ph.sb("lead", [P, BLOCKS])
        lead_diff = ph.sb("lead_diff", [P, BLOCKS])
        passed = ph.sb("passed", [P, BLOCKS])
        step_no = ph.sb("step_no", [P, STEP_GROUPS])
        block_no = ph.sb("block_no", [P, STEP_GROUPS])
        block_lo = ph.sb("block_lo", [P, STEP_GROUPS])
        row_no = ph.sb("row_no", [P, STEP_GROUPS])
        row_i = ph.sb("row_i", [P, STEP_GROUPS], I32)
        src_i = ph.sb("src_i", [P, STEP_GROUPS, SE], I32)
        sdst_i = ph.sb("sdst_i", [P, STEP_GROUPS, SE], I32)
        src_f = ph.sb("src_f", [P, STEP_GROUPS, SE])
        sdst_f = ph.sb("sdst_f", [P, STEP_GROUPS, SE])
        local = ph.sb("local", [P, STEP_GROUPS, SE])
        inside = ph.sb("inside", [P, STEP_GROUPS, SE])
        inside_hi = ph.sb("inside_hi", [P, STEP_GROUPS, SE])
        key = ph.sb("key", [P, STEP_GROUPS, SE])
        local16 = ph.sb("local16", [P, STEP_GROUPS, SE], BF16)
        key_t = ph.sb("key_t", [P, TABLE, TPS])
        key8 = ph.sb("key8", [P, CT, CHUNKS, HEADS])
        key_s = ph.sb("key_s", [P, SLOTS])
        row_first = ph.sb("row_first", [1, HEADS, CHUNKS])
        row_last = ph.sb("row_last", [1, HEADS, CHUNKS])
        goes_on = ph.sb("goes_on", [1, HEADS, CHUNKS])
        whole = ph.sb("whole", [1, HEADS, CHUNKS])
        big = ph.ps("big", [P, 6 * 512])
        small = ph.ps("small", [P, 512])
        ends = ph.ps("ends", [P, 512])

        dst_in, bound_in, steps = ph.sem("dst_in"), ph.sem("bound_in"), ph.sem("steps")
        counted, summed = ph.sem("counted"), ph.sem("summed")
        rows_known, src_in, sdst_in = ph.sem("rows_known"), ph.sem("src_in"), ph.sem("sdst_in")
        steps_known, turned = ph.sem("steps_known"), ph.sem("turned")
        local_known, local_out = ph.sem("local_known"), ph.sem("local_out")
        keys_ready, keys_turned = ph.sem("keys_ready"), ph.sem("keys_turned")
        ends_ready, ends_turned = ph.sem("ends_ready"), ph.sem("ends_turned")

        def pair(which, g, t):
            n = (which * STEP_GROUPS + g) * TPS + t
            return big[:, n * P:(n + 1) * P]

        with nc.Block() as block:
            @block.sync
            def _(sp):
                sp.dma_start(dst_i[:], k.dst.rearrange("(p c) -> p c", p=P)).then_inc(dst_in, 16)
                sp.wait_ge(local_known, 1)
                for g in range(STEP_GROUPS):
                    sp.dma_start(k.local_d[g * P * SE:(g + 1) * P * SE].rearrange("(p e) -> p e", p=P),
                                 local16[:, g, :]).then_inc(local_out, 16)
                sp.wait_ge(local_out, 16 * STEP_GROUPS)

            @block.gpsimd
            def _(pool):
                nc.gpsimd.iota(bound_i[:], pattern=[[P, BLOCKS + 1]], base=0,
                               channel_multiplier=0).then_inc(bound_in, 1)
                pool.wait_ge(rows_known, 1)
                for g in range(STEP_GROUPS):
                    at = bass.IndirectOffsetOnAxis(ap=row_i[:, g:g + 1], axis=0)
                    nc.gpsimd.indirect_dma_start(src_i[:, g, :], None, k.src, at).then_inc(src_in, 16)
                    nc.gpsimd.indirect_dma_start(sdst_i[:, g, :], None,
                                                 k.dst.rearrange("(r e) -> r e", e=SE), at).then_inc(sdst_in, 16)

            @block.vector
            def _(dve):
                link = chain(dve, steps)
                v = nc.vector
                dve.wait_ge(bound_in, 1)
                v.tensor_copy(bound[:], bound_i[:])
                dve.wait_ge(dst_in, 16)
                link(v.tensor_copy(dst_f[:], dst_i[:]))
                link(v.tensor_tensor(below[:], dst_f[:].unsqueeze(1).to_broadcast([P, BLOCKS + 1, cols]),
                                     bound[:].unsqueeze(2).to_broadcast([P, BLOCKS + 1, cols]), ALU.is_lt))
                v.tensor_reduce(count[:], below[:], AX.X, ALU.add).then_inc(counted, 1)
                dve.wait_ge(summed, 1)
                link(v.tensor_copy(start[:], small[:, 0:BLOCKS + 1]))
                link(v.tensor_copy(start_i[:], start[:]))
                link(v.tensor_scalar(start_i[:], start_i[:], SE.bit_length() - 1, None, ALU.logical_shift_right))
                link(v.tensor_copy(first_row[:], start_i[:, 0:BLOCKS]))
                link(v.tensor_scalar(stop_row[:], start[:, 1:], float(SE - 1), None, ALU.add))
                link(v.tensor_copy(start_i[:, 0:BLOCKS], stop_row[:]))
                link(v.tensor_scalar(start_i[:], start_i[:], SE.bit_length() - 1, None, ALU.logical_shift_right))
                link(v.tensor_copy(stop_row[:], start_i[:, 0:BLOCKS]))
                link(v.tensor_tensor(n_steps[:], stop_row[:], first_row[:], ALU.subtract))
                link(v.tensor_tensor(passed[:], start[:, 1:], start[:, 0:BLOCKS], ALU.is_gt))
                link(v.tensor_tensor(n_steps[:], n_steps[:], passed[:], ALU.mult))
                link(v.memset(zeros[:], 0.0))
                link(v.tensor_tensor_scan(steps_end[:], n_steps[:], zeros[:], 0.0, ALU.add, ALU.add))
                link(v.tensor_tensor(lead[:], first_row[:], n_steps[:], ALU.add))
                link(v.tensor_tensor(lead[:], lead[:], steps_end[:], ALU.subtract))
                link(v.memset(lead_diff[:], 0.0))
                link(v.tensor_tensor(lead_diff[:, 0:BLOCKS - 1], lead[:, 1:], lead[:, 0:BLOCKS - 1], ALU.subtract))
                for g in range(STEP_GROUPS):
                    link(v.tensor_scalar(step_no[:, g:g + 1], k.iota_col[:], float(g * P), None, ALU.add))
                    link(v.tensor_scalar(passed[:], steps_end[:], step_no[:, g:g + 1], None, ALU.is_le))
                    link(v.tensor_reduce(block_no[:, g:g + 1], passed[:], AX.X, ALU.add))
                    link(v.tensor_tensor(passed[:], passed[:], lead_diff[:], ALU.mult))
                    link(v.tensor_reduce(row_no[:, g:g + 1], passed[:], AX.X, ALU.add))
                    link(v.tensor_tensor(row_no[:, g:g + 1], row_no[:, g:g + 1], lead[:, 0:1], ALU.add))
                    link(v.tensor_tensor(row_no[:, g:g + 1], row_no[:, g:g + 1], step_no[:, g:g + 1], ALU.add))
                link(v.tensor_scalar(row_no[:], row_no[:], float(EDGE_ROWS - 1), 0.0, ALU.min, ALU.max))
                v.tensor_copy(row_i[:], row_no[:]).then_inc(rows_known, 1)
                link(v.tensor_scalar(block_lo[:], block_no[:], float(P), None, ALU.mult))
                v.tensor_scalar(block_no[:], block_no[:], float(BLOCKS - 1), None, ALU.min).then_inc(steps_known, 1)

                dve.wait_ge(src_in, 16 * STEP_GROUPS)
                link(v.tensor_copy(src_f[:], src_i[:]))
                dve.wait_ge(sdst_in, 16 * STEP_GROUPS)
                link(v.tensor_copy(sdst_f[:], sdst_i[:]))
                for g in range(STEP_GROUPS):
                    link(v.tensor_scalar(local[:, g, :], sdst_f[:, g, :], block_lo[:, g:g + 1], None, ALU.subtract))
                link(v.tensor_scalar(inside[:], local[:], 0.0, None, ALU.is_ge))
                link(v.tensor_scalar(inside_hi[:], local[:], float(P), None, ALU.is_lt))
                link(v.tensor_tensor(inside[:], inside[:], inside_hi[:], ALU.mult))
                for out, of in ((local, local), (key, sdst_f)):
                    link(v.tensor_scalar(out[:], of[:], 1.0, None, ALU.add))
                    link(v.tensor_tensor(out[:], out[:], inside[:], ALU.mult))
                    link(v.tensor_scalar(out[:], out[:], -1.0, None, ALU.add))
                v.tensor_copy(local16[:], local[:]).then_inc(local_known, 1)

                dve.wait_ge(turned, 1)
                v.tensor_copy(k.block_row[:], small[0:1, 128:128 + TABLE])
                for g in range(STEP_GROUPS):
                    for t in range(TPS):
                        at = slice(g * P, (g + 1) * P)
                        v.tensor_copy(k.src_t[:, at, t], pair(0, g, t))
                        v.tensor_copy(k.local_t[:, at, t], pair(1, g, t))
                        link(v.tensor_copy(key_t[:, at, t], pair(2, g, t)))
                used = key_t[:].rearrange("p s t -> p (s t)")[:, 0:TILES].rearrange("p (c g) -> p g c", g=CT)
                v.tensor_copy(key8[:], used.unsqueeze(3).to_broadcast([P, CT, CHUNKS, HEADS])).then_inc(keys_ready, 1)

                dve.wait_ge(keys_turned, 1)
                link(v.tensor_copy(key_s[:], big[:, 0:SLOTS]))
                v.tensor_copy(row_first[0:1, 0, 0:1], key_s[0:1, 0:1]).then_inc(ends_ready, 1)
                link(v.memset(k.fresh[:], 0.0))
                link(v.tensor_tensor(k.fresh[:, 1:SLOTS], key_s[:, 1:], key_s[:, 0:SLOTS - 1], ALU.not_equal))
                link(v.tensor_scalar(k.fresh[:, 1:SLOTS], k.fresh[:, 1:SLOTS], -BIG, None, ALU.mult))
                dve.wait_ge(ends_turned, 1)
                v.tensor_copy(row_first[:], ends[0:1, 0:P].rearrange("p (c h) -> p h c", h=HEADS))
                link(v.tensor_copy(row_last[:], ends[0:1, P:2 * P].rearrange("p (c h) -> p h c", h=HEADS)))
                link(v.memset(goes_on[:], 0.0))
                link(v.tensor_tensor(goes_on[:, :, 1:], row_first[:, :, 1:], row_last[:, :, 0:CHUNKS - 1], ALU.is_equal))
                link(v.tensor_tensor(whole[:], row_first[:], row_last[:], ALU.is_equal))
                for x in (k.link_f, k.link_b, k.seed_b):
                    link(v.memset(x[:], 0.0))
                a, b = slice(1, CHUNKS), slice(0, CHUNKS - 1)
                link(v.tensor_tensor(k.link_f[:, :, a], goes_on[:, :, a], whole[:, :, b], ALU.mult))
                link(v.tensor_tensor(k.link_b[:, :, b], goes_on[:, :, a], whole[:, :, a], ALU.mult))
                link(v.tensor_copy(k.seed_b[:, :, b], goes_on[:, :, a]))
                link(v.tensor_copy(k.seed_f[:], goes_on[:]))
                for x in (k.link_f, k.link_b, k.seed_f, k.seed_b):
                    link(v.tensor_scalar(x[:], x[:], -1.0, BIG, ALU.add, ALU.mult))

            @block.tensor
            def _(pe):
                pe.wait_ge(counted, 1)
                nc.tensor.matmul(small[:, 0:BLOCKS + 1], k.ones[:], count[:], start=True, stop=True).then_inc(summed, 1)
                pe.wait_ge(steps_known, 1)
                pe.wait_ge(local_known, 1)
                for g in range(STEP_GROUPS):
                    nc.tensor.matmul(small[0:1, 128 + g * P:128 + (g + 1) * P], block_no[:, g:g + 1], k.ident[:],
                                     start=True, stop=True)
                for which, table in enumerate((src_f, local, key)):
                    for g in range(STEP_GROUPS):
                        for t in range(TPS):
                            last = nc.tensor.transpose(pair(which, g, t), table[:, g, t * P:(t + 1) * P], k.ident[:])
                last.then_inc(turned, 1)
                pe.wait_ge(keys_ready, 1)
                for g in range(CT):
                    last = nc.tensor.transpose(big[:, g * P:(g + 1) * P],
                                               key8[:, g].rearrange("p c h -> p (c h)"), k.ident[:])
                last.then_inc(keys_turned, 1)
                pe.wait_ge(ends_ready, 1)
                nc.tensor.matmul(ends[0:1, 0:P], key_s[:, 0:1], k.ident[:], start=True, stop=True)
                nc.tensor.matmul(ends[0:1, P:2 * P], key_s[:, SLOTS - 1:SLOTS], k.ident[:],
                                 start=True, stop=True).then_inc(ends_turned, 1)
        ph.give_back()


def split_product(nc, out, a_hi, a_lo, b_hi, b_lo, chunks):
    n = 3 * len(chunks)
    i = 0
    for c in chunks:
        for a, b in ((a_hi, b_hi), (a_hi, b_lo), (a_lo, b_hi)):
            last = nc.tensor.matmul(out, a(c), b(c), start=i == 0, stop=i == n - 1)
            i += 1
    return last


def project(nc, k, layer):
    with ExitStack() as stack:
        ph = Phase(nc, stack, f"proj{layer}")
        OUTS = 4
        raw = ph.sb("raw", [P, OUTS, KC, C])
        w = [[ph.sb(f"w{i}{part}", [P, KC, C], F32R) for part in ("hi", "lo")] for i in range(OUTS)]
        bias = ph.sb("bias", [P, OUTS, C])
        x = ph.sb("x", [P, 2, C])
        enc = ph.sb("enc", [P, 2, C]) if layer else x
        skip = ph.sb("skip", [P, 2, C]) if layer else None
        inv = ph.sb("inv", [P, 2, HEADS]) if layer else None
        xt_hi = ph.sb("xt_hi", [P, 2, KC, P], F32R)
        xt_lo = ph.sb("xt_lo", [P, 2, KC, P], F32R)
        staged = ph.sb("staged", [P, 2, 3, C])
        xt_ps = [ph.ps(f"xt_ps{i}", [P, C]) for i in range(2)]
        out_ps = [ph.ps(f"out_ps{i}", [P, C]) for i in range(OUTS)]

        raw_in = [ph.sem(f"raw_in{i}") for i in range(OUTS)]
        w_hi, w_lo = ph.sem("w_hi"), ph.sem("w_lo")
        bias_in = ph.sem("bias_in")
        enc_in = [ph.sem("enc_in0"), ph.sem("enc_in1")]
        skip_in = [ph.sem("skip_in0"), ph.sem("skip_in1")] if layer else None
        enc_free, skip_free = ph.sem("enc_free"), ph.sem("skip_free")
        x_ready, turned = ph.sem("x_ready"), ph.sem("turned")
        hi_ready, lo_ready, product = ph.sem("hi_ready"), ph.sem("lo_ready"), ph.sem("product")
        out_done, steps, stage_free = ph.sem("out_done"), ph.sem("steps"), ph.sem("stage_free")
        stored = [ph.sem("stored0"), ph.sem("stored1")]
        node_rows = lambda b: bass.ds(b * P, P)

        with nc.Block() as block:
            @block.gpsimd
            def _(pool):
                for i, b in enumerate((k.bk, k.bv, k.bs, k.bq)):
                    pool.dma_start(bias[:, i, :], b[layer].partition_broadcast(P)).then_inc(bias_in, 16)

            @block.tensor
            def _(pe):
                def turn(b, u, it):
                    if layer:
                        pe.wait_ge(x_ready, b + 1)
                    else:
                        pe.wait_ge(enc_in[u], 16 * (it + 1))
                    pe.wait_ge(lo_ready, b + 1)
                    for c in range(KC):
                        last = nc.tensor.transpose(xt_ps[u][:, c * P:(c + 1) * P], x[:, u, c * P:(c + 1) * P], k.ident[:])
                    last.then_inc(turned, 1)

                def products(b, u, it, first, ahead):
                    pe.wait_ge(lo_ready, b + 3)
                    for i in range(OUTS):
                        if first:
                            pe.wait_ge(w_lo, i + 1)
                        pe.wait_ge(out_done, OUTS * b + i + 1)
                        split_product(nc, out_ps[i][:], lambda c: xt_hi[:, u, c, :], lambda c: xt_lo[:, u, c, :],
                                      lambda c: w[i][0][:, c, :], lambda c: w[i][1][:, c, :],
                                      range(KC)).then_inc(product, 1)
                        if i == 1 and ahead:
                            turn(b + 1, 1 - u, it + u)

                turn(0, 0, 0)
                products(0, 0, 0, True, True)
                products(1, 1, 0, False, True)
                with pe.Fori(1, BLOCKS // 2 - 1) as it:
                    for u in range(2):
                        products(2 * it + u, u, it, False, True)
                products(BLOCKS - 2, 0, BLOCKS // 2 - 1, False, True)
                products(BLOCKS - 1, 1, BLOCKS // 2 - 1, False, False)

            @block.scalar
            def _(act):
                def load(b, u):
                    first = act.snap(b * P)
                    if layer:
                        act.wait_ge(skip_free, b + 1)
                        act.dma_start(skip[:, u, :], k.skip_d[bass.ds(first, P), :]).then_inc(skip_in[u], 16)
                    act.wait_ge(enc_free, b + 1)
                    act.dma_start(enc[:, u, :], k.x[bass.ds(first, P), :]).then_inc(enc_in[u], 16)

                def high_part(b, u):
                    act.wait_ge(turned, b + 1)
                    act.wait_ge(product, OUTS * b + OUTS)
                    nc.scalar.activation(xt_hi[:, u].rearrange("p c n -> p (c n)"), xt_ps[u][:],
                                         ACT.Copy).then_inc(hi_ready, 1)

                load(0, 0)
                load(1, 1)
                for i in range(OUTS):
                    act.wait_ge(raw_in[i], 16)
                    nc.scalar.activation(w[i][0][:], raw[:, i], ACT.Copy).then_inc(w_hi, 1)
                    if i == 0:
                        high_part(0, 0)
                high_part(1, 1)
                with act.Fori(1, BLOCKS // 2) as it:
                    for u in range(2):
                        load(2 * it + u, u)
                        high_part(2 * it + u, u)

            @block.vector
            def _(dve):
                dve.sem_inc(enc_free, 2)
                dve.sem_inc(skip_free, 2)
                dve.sem_inc(lo_ready, 2)
                dve.sem_inc(out_done, OUTS)
                dve.sem_inc(product, 2 * OUTS)
                dve.sem_inc(stage_free, 2)

                def weight_low(i):
                    dve.wait_ge(w_hi, i + 1)
                    nc.vector.tensor_tensor(w[i][1][:], raw[:, i], w[i][0][:].bitcast(F32),
                                            ALU.subtract).then_inc(w_lo, 1)

                def assemble(b, u, it):
                    sums = k.work[:, bass.ds(b * AGG, C)]
                    total = k.work[:, bass.ds(b * AGG + C, HEADS)]
                    nc.vector.tensor_scalar(inv[:, u, :], total, 1e-16, None, ALU.add).then_inc(steps, 1)
                    dve.wait_ge(steps, 3 * b + 1)
                    nc.vector.reciprocal(inv[:, u, :], inv[:, u, :]).then_inc(steps, 1)
                    dve.wait_ge(steps, 3 * b + 2)
                    nc.vector.tensor_tensor(x[:, u, :].rearrange("p (h d) -> p h d", h=HEADS),
                                            sums.rearrange("p (h d) -> p h d", h=HEADS),
                                            inv[:, u, :].unsqueeze(2).to_broadcast([P, HEADS, D]), ALU.mult).then_inc(steps, 1)
                    dve.wait_ge(steps, 3 * b + 3)
                    dve.wait_ge(skip_in[u], 16 * (it + 1))
                    nc.vector.tensor_tensor(x[:, u, :], x[:, u, :], skip[:, u, :], ALU.add).then_inc(x_ready, 1)
                    dve.wait_ge(x_ready, b + 1)
                    dve.sem_inc(skip_free, 1)

                def low_part(b, u):
                    dve.wait_ge(hi_ready, b + 1)
                    nc.vector.tensor_tensor(xt_lo[:, u].rearrange("p c n -> p (c n)"), xt_ps[u][:],
                                            xt_hi[:, u].rearrange("p c n -> p (c n)").bitcast(F32),
                                            ALU.subtract).then_inc(lo_ready, 1)

                def outputs(b, u, it, ahead):
                    dve.wait_ge(stage_free, b + 1)
                    for i in range(3):
                        dve.wait_ge(product, OUTS * (b + 2) + i + 1)
                        nc.vector.tensor_tensor(staged[:, u, i, :], out_ps[i][:], bias[:, i, :], ALU.add).then_inc(out_done, 1)
                        if i == 0 and ahead and layer:
                            assemble(b + 1, 1 - u, it + u)
                        if i == 1 and ahead:
                            low_part(b + 1, 1 - u)
                    dve.wait_ge(out_done, OUTS * (b + 1) + 3)
                    dve.wait_ge(enc_in[u], 16 * (it + 1))
                    nc.vector.tensor_tensor(staged[:, u, 2, :], staged[:, u, 2, :], enc[:, u, :], ALU.add).then_inc(enc_free, 1)
                    dve.wait_ge(product, OUTS * (b + 2) + 4)
                    nc.vector.tensor_tensor(k.work[:, bass.ds(b * C, C)], out_ps[3][:], bias[:, 3, :],
                                            ALU.add).then_inc(out_done, 1)

                weight_low(0)
                if layer:
                    assemble(0, 0, 0)
                low_part(0, 0)
                for i in range(1, OUTS):
                    weight_low(i)
                dve.wait_ge(bias_in, 16 * OUTS)
                with dve.Fori(0, BLOCKS // 2 - 1) as it:
                    for u in range(2):
                        outputs(2 * it + u, u, it, True)
                outputs(BLOCKS - 2, 0, BLOCKS // 2 - 1, True)
                outputs(BLOCKS - 1, 1, BLOCKS // 2 - 1, False)

            @block.sync
            def _(sp):
                for i, m in enumerate((k.Wk, k.Wv, k.Ws, k.Wq)):
                    sp.dma_start(raw[:, i], m[layer].rearrange("(c p) n -> p c n", p=P)).then_inc(raw_in[i], 16)
                with sp.Fori(0, BLOCKS // 2) as it:
                    for u in range(2):
                        b = 2 * it + u
                        first = sp.snap(b * P)
                        sp.wait_ge(out_done, OUTS * (b + 2))
                        for i, table in enumerate((k.k_d, k.v_d, k.skip_d)):
                            sp.dma_start(table[bass.ds(first, P), :], staged[:, u, i, :]).then_inc(stored[u], 16)
                        sp.wait_ge(stored[u], 48 * (it + 1))
                        sp.sem_inc(stage_free, 1)


def gather_rows(nc, k, pool, table, rows, index, index_ready, asked, rows_used):
    sources = k.src_t[:].rearrange("p s t -> p (s t)")
    n = HALF * TPS
    nc.gpsimd.tensor_copy(index[:, 0, :], sources[:, 0:n]).then_inc(index_ready, 1)
    with pool.Fori(0, STEPS // BODY) as it:
        for q in range(2):
            half = 2 * it + q
            pool.wait_ge(index_ready, half + 1)
            for s in range(HALF):
                for used in rows_used:
                    pool.wait_ge(used, HALF * half + s + 1)
                pool.sem_inc(asked, 1)
                if s == HALF - 1:
                    nc.gpsimd.tensor_copy(index[:, 1 - q, :], sources[:, bass.ds((half + 1) * n, n)]).then_inc(index_ready, 1)
                for t in range(TPS):
                    at = bass.IndirectOffsetOnAxis(ap=index[:, q, s * TPS + t:s * TPS + t + 1], axis=0)
                    nc.gpsimd.indirect_dma_start(rows[:, s, t, :], None, table, at).then_inc(k.rows_in[s], 16)


def score(nc, k, layer):
    with ExitStack() as stack:
        ph = Phase(nc, stack, f"score{layer}")
        rows = ph.sb("rows", [P, RING, TPS, C])
        index = ph.sb("index", [P, 2, HALF * TPS], I32)
        local = ph.sb("local", [P, 2, HALF * SE], BF16)
        hot = ph.sb("hot", [P, 2, HALF * SE])
        prod = ph.sb("prod", [P, PRODS, TPS, C])
        q_ps = [ph.ps(f"q_ps{i}", [P, TPS, C]) for i in range(2)]

        index_ready = ph.sem("index_ready")
        asked = ph.sem("asked")
        gathered_before = 2 * layer * STEPS // RING
        local_in = [ph.sem("local_in0"), ph.sem("local_in1")]
        hot_ready, q_ready = ph.sem("hot_ready"), ph.sem("q_ready")
        multiplied, act_summed, dve_summed = ph.sem("multiplied"), ph.sem("act_summed"), ph.sem("dve_summed")
        half_edges = HALF * SE

        with nc.Block() as block:
            @block.gpsimd
            def _(pool):
                gather_rows(nc, k, pool, k.k_d, rows, index, index_ready, asked, [multiplied])

            @block.sync
            def _(sp):
                def load(first, q):
                    sp.dma_start(local[:, q, :], k.local_d[bass.ds(first, half_edges)].partition_broadcast(P)
                                 ).then_inc(local_in[q], 16)

                load(0, 0)
                with sp.Fori(0, STEPS // BODY) as it:
                    for q in range(2):
                        first = sp.snap((2 * it + q + 1) * half_edges)
                        sp.wait_ge(hot_ready, 2 * it + q + 1)
                        load(first, 1 - q)

            @block.tensor
            def _(pe):
                pe.sem_inc(q_ready, HALF)
                with pe.Fori(0, STEPS // BODY) as it:
                    for q in range(2):
                        pe.wait_ge(hot_ready, 2 * it + q + 2)
                        for s in range(HALF):
                            n = BODY * it + HALF * q + s
                            node_block = pe.value_load(k.block_row[0:1, bass.ds(n, 1)], min_val=0, max_val=BLOCKS - 1)
                            pe.wait_ge(multiplied, n + RING - 1)
                            for t in range(TPS):
                                e = (s * TPS + t) * P
                                last = nc.tensor.matmul(q_ps[s % 2][:, t, :], hot[:, q, e:e + P],
                                                        k.work[:, bass.ds(node_block * C, C)], start=True, stop=True)
                            last.then_inc(q_ready, 1)

            @block.vector
            def _(dve):
                def one_hot(half_done, q, times):
                    dve.wait_ge(local_in[q], 16 * times)
                    if half_done is not None:
                        dve.wait_ge(q_ready, half_done)
                    nc.vector.tensor_scalar(hot[:, q, :], local[:, q, :], k.iota_col[:, 0:1], None,
                                            ALU.is_equal).then_inc(hot_ready, 1)

                def multiply(n, s, times):
                    dve.wait_ge(k.rows_in[s % RING], 16 * TPS * (gathered_before + times))
                    dve.wait_ge(q_ready, n + HALF + 1)
                    dve.wait_ge(act_summed, n + 1)
                    dve.wait_ge(dve_summed, n + 1)
                    nc.vector.tensor_tensor(prod[:, s % PRODS], q_ps[s % 2][:], rows[:, s % RING], ALU.mult
                                            ).then_inc(multiplied, 1)

                def add_up(n, s):
                    dve.wait_ge(multiplied, n + RING + 1)
                    nc.vector.tensor_reduce(
                        k.edge[:, bass.ds(n * TPS, TPS), 0:DVE_HEADS1],
                        prod[:, s % PRODS, :, 0:DVE_HEADS1 * D].rearrange("p t (h d) -> p t h d", d=D), AX.X, ALU.add
                    ).then_inc(dve_summed, 1)

                dve.sem_inc(multiplied, RING)
                dve.sem_inc(dve_summed, PRODS)
                dve.sem_inc(hot_ready, 1)
                one_hot(None, 0, 1)
                with dve.Fori(0, STEPS // BODY) as it:
                    for q in range(2):
                        n = BODY * it + HALF * q
                        multiply(n, 0, 2 * it + q + 1)
                        one_hot(HALF * (2 * it + q) + HALF, 1 - q, it + q + 1)
                        for s in range(1, HALF):
                            multiply(n + s, s, 2 * it + q + 1)
                            add_up(n + s - 1, s - 1)
                        add_up(n + HALF - 1, HALF - 1)

            @block.scalar
            def _(act):
                act.sem_inc(act_summed, PRODS)
                with act.Fori(0, STEPS // BODY) as it:
                    for s in range(BODY):
                        n = BODY * it + s
                        act.wait_ge(multiplied, n + RING + 1)
                        for t in range(TPS):
                            for h in range(DVE_HEADS1, HEADS):
                                at = prod[:, s % PRODS, t, h * D:(h + 1) * D]
                                last = nc.scalar.activation(
                                    at, at, ACT.Copy,
                                    accum_out=k.edge[:, bass.ds(n * TPS + t, 1), h:h + 1].rearrange("p a b -> p (a b)"))
                        last.then_inc(act_summed, 1)


def soften_collect(nc, k, layer):
    with ExitStack() as stack:
        ph = Phase(nc, stack, f"coll{layer}")
        fwd = ph.sb("fwd", [P, SLOTS])
        bwd = ph.sb("bwd", [P, SLOTS])
        seeds = [ph.sb(f"seeds{i}", [1, HEADS, CHUNKS]) for i in range(2)]
        carry = [ph.sb(f"carry{i}", [1, HEADS, CHUNKS]) for i in range(2)]
        carry_ch = [ph.sb(f"carry_ch{i}", [1, CHUNKS, HEADS]) for i in range(2)]
        carry_col = ph.sb("carry_col", [P, 2])
        rows = ph.sb("rows", [P, RING, TPS, C])
        index = ph.sb("index", [P, 2, HALF * TPS], I32)
        hot = ph.sb("hot", [P, HOTS, HOT_STEPS * TPS, P])
        ev = ph.sb("ev", [P, SUMS, TPS, AGG])
        banks = ph.ps("banks", [P, 8, 512])
        flat_banks = banks[:].rearrange("p b n -> p (b n)")
        big, small, cols = flat_banks[:, 0:6 * 512], banks[:, 6, :], banks[:, 7, :]
        sums = [banks[:, 2 * i:2 * i + 2, 0:AGG // 2] for i in range(SUMS)]

        sorted_out, turned = ph.sem("sorted_out"), ph.sem("turned")
        ends_ready, ends_turned = ph.sem("ends_ready"), ph.sem("ends_turned")
        carry_ready, carry_turned = ph.sem("carry_ready"), ph.sem("carry_turned")
        less_max, raised, back, steps = ph.sem("less_max"), ph.sem("raised"), ph.sem("back"), ph.sem("steps")
        e_known, cleared = ph.sem("e_known"), ph.sem("cleared")
        gathered_before = (2 * layer + 1) * STEPS // RING
        index_ready = ph.sem("index_ready")
        asked = ph.sem("asked")
        hot_ready, ev_dve, ev_act = ph.sem("hot_ready"), ph.sem("ev_dve"), ph.sem("ev_act")
        summed, added = ph.sem("summed"), ph.sem("added")

        scores = k.edge[:].rearrange("p (c g) h -> p g c h", g=CT)
        local_flat = k.local_t[:].rearrange("p s t -> p (s t)")
        flat = lambda x: x[:].rearrange("p h c -> p (h c)")
        flip = lambda x: x[:, ::-1]
        QUART = 4
        QUARTS = -(-CT // QUART)

        with nc.Block() as block:
            @block.gpsimd
            def _(pool):
                nc.gpsimd.memset(k.work[:], 0.0).then_inc(cleared, 1)
                gather_rows(nc, k, pool, k.v_d, rows, index, index_ready, asked, [ev_dve, ev_act])

            @block.tensor
            def _(pe):
                pe.wait_ge(sorted_out, 1)
                for g in range(CT):
                    last = nc.tensor.transpose(big[:, g * P:(g + 1) * P], fwd[:, g * P:(g + 1) * P], k.ident[:])
                last.then_inc(turned, 1)
                pe.wait_ge(ends_ready, 1)
                nc.tensor.matmul(small[0:1, 0:P], fwd[:, SLOTS - 1:SLOTS], k.ident[:], start=True, stop=True)
                nc.tensor.matmul(small[0:1, P:2 * P], bwd[:, 0:1], k.ident[:], start=True, stop=True).then_inc(ends_turned, 1)
                pe.wait_ge(carry_ready, 1)
                for i in range(2):
                    last = nc.tensor.matmul(cols[:, i:i + 1], carry_ch[i][:].rearrange("p c h -> p (c h)"),
                                            k.ones[0:1, 0:1], start=True, stop=True)
                last.then_inc(carry_turned, 1)
                pe.wait_ge(raised, 1)
                for g in range(CT):
                    last = nc.tensor.transpose(big[:, g * P:(g + 1) * P], bwd[:, g * P:(g + 1) * P], k.ident[:])
                    if g % QUART == QUART - 1 or g == CT - 1:
                        last.then_inc(back, 1)
                with pe.Fori(0, STEPS // BODY) as it:
                    for s in range(BODY):
                        n = BODY * it + s
                        if s % HOT_STEPS == 0:
                            pe.wait_ge(hot_ready, BODY // HOT_STEPS * it + s // HOT_STEPS + 1)
                        pe.wait_ge(ev_dve, n + RING + 1)
                        pe.wait_ge(ev_act, n + RING + 1)
                        pe.wait_ge(added, n + 1)
                        for t in range(TPS):
                            m = hot[:, s // HOT_STEPS % HOTS, (s % HOT_STEPS) * TPS + t, :]
                            for part in range(2):
                                last = nc.tensor.matmul(sums[s % SUMS][:, part, :], m,
                                                        ev[:, s % SUMS, t, part * AGG // 2:(part + 1) * AGG // 2],
                                                        start=t == 0, stop=t == TPS - 1)
                        last.then_inc(summed, 1)

            @block.vector
            def _(dve):
                dve.sem_inc(ev_dve, RING)
                link = chain(dve, steps)
                v = nc.vector
                scan = lambda out, flags, data, first: v.tensor_tensor_scan(out, flags, data, first, ALU.add, ALU.max)
                before, after = k.fresh[:, 0:SLOTS], k.fresh[:, 1:SLOTS + 1]
                v.tensor_copy(fwd[:].rearrange("p (g c h) -> p g c h", g=CT, h=HEADS), scores).then_inc(sorted_out, 1)
                for x in seeds:
                    v.memset(x[:], -BIG)
                dve.wait_ge(turned, 1)
                link(scan(fwd[:], before, big[:, 0:SLOTS], -BIG))
                scan(flip(bwd), flip(after), flip(big[:, 0:SLOTS]), -BIG).then_inc(ends_ready, 1)
                dve.wait_ge(ends_turned, 1)
                a, b = slice(1, CHUNKS), slice(0, CHUNKS - 1)
                last_f = small[0:1, 0:P].rearrange("p (c h) -> p h c", h=HEADS)
                first_b = small[0:1, P:2 * P].rearrange("p (c h) -> p h c", h=HEADS)
                link(v.tensor_tensor(seeds[0][:, :, a], last_f[:, :, b], k.seed_f[:, :, a], ALU.add))
                link(v.tensor_tensor(seeds[1][:, :, b], first_b[:, :, a], k.seed_b[:, :, b], ALU.add))
                link(scan(flat(carry[0]), flat(k.link_f), flat(seeds[0]), -BIG))
                link(scan(flip(flat(carry[1])), flip(flat(k.link_b)), flip(flat(seeds[1])), -BIG))
                v.tensor_copy(carry_ch[0][:], carry[0][:].rearrange("p h c -> p c h"))
                v.tensor_copy(carry_ch[1][:], carry[1][:].rearrange("p h c -> p c h")).then_inc(carry_ready, 1)
                dve.wait_ge(carry_turned, 1)
                link(v.tensor_copy(carry_col[:], cols[:, 0:2]))
                link(scan(fwd[:], before, big[:, 0:SLOTS], carry_col[:, 0:1]))
                link(scan(flip(bwd), flip(after), flip(big[:, 0:SLOTS]), carry_col[:, 1:2]))
                link(v.tensor_tensor(fwd[:], fwd[:], bwd[:], ALU.max))
                v.tensor_tensor(fwd[:], big[:, 0:SLOTS], fwd[:], ALU.subtract).then_inc(less_max, 1)
                for n, g in enumerate(range(0, CT, QUART)):
                    if n % 2 == 0:
                        m = min(QUART, CT - g)
                        dve.wait_ge(back, n + 1)
                        v.tensor_copy(scores[:, g:g + m],
                                      big[:, g * P:(g + m) * P].rearrange("p (g c h) -> p g c h", g=m, h=HEADS)
                                      ).then_inc(e_known, 1)

                def one_hot(pair, slot, free):
                    if free is not None:
                        dve.wait_ge(summed, free)
                    n = HOT_STEPS * TPS
                    nc.vector.tensor_tensor(hot[:, slot], k.iota_row[:].unsqueeze(1).to_broadcast([P, n, P]),
                                            local_flat[:, bass.ds(pair * n, n)].unsqueeze(2).to_broadcast([P, n, P]),
                                            ALU.is_equal).then_inc(hot_ready, 1)

                def weigh(n, s, times):
                    dve.wait_ge(k.rows_in[s % RING], 16 * TPS * (gathered_before + times))
                    dve.wait_ge(summed, n + 1)
                    cut = DVE_HEADS2 * D
                    nc.vector.tensor_tensor(
                        ev[:, s % SUMS, :, 0:cut].rearrange("p t (h d) -> p t h d", d=D),
                        rows[:, s % RING, :, 0:cut].rearrange("p t (h d) -> p t h d", d=D),
                        k.edge[:, bass.ds(n * TPS, TPS), 0:DVE_HEADS2].unsqueeze(3).to_broadcast([P, TPS, DVE_HEADS2, D]),
                        ALU.mult).then_inc(ev_dve, 1)

                def add(n, s):
                    node_block = dve.value_load(k.block_row[0:1, bass.ds(n, 1)], min_val=0, max_val=BLOCKS - 1)
                    at = k.work[:, bass.ds(node_block * AGG, AGG)].rearrange("p (b n) -> p b n", b=2)
                    dve.wait_ge(summed, n + SUMS + 1)
                    dve.wait_ge(added, n + SUMS)
                    nc.vector.tensor_tensor(at, at, sums[s % SUMS], ALU.add).then_inc(added, 1)

                dve.sem_inc(summed, SUMS)
                dve.sem_inc(added, SUMS)
                for pair in range(HOTS - 1):
                    one_hot(pair, pair, None)
                dve.wait_ge(e_known, QUARTS)
                dve.wait_ge(cleared, 1)
                weigh(0, 0, 1)
                weigh(1, 1, 1)

                def body(it, last):
                    for s in range(BODY):
                        n = BODY * it + s
                        if not (last and s >= BODY - 2):
                            weigh(n + 2, (s + 2) % BODY, BODY // RING * it + (s + 2) // RING + 1)
                        add(n, s)
                        if s % HOT_STEPS == HOT_STEPS - 1:
                            pair = s // HOT_STEPS
                            one_hot(BODY // HOT_STEPS * it + pair + HOTS - 1, (pair + HOTS - 1) % HOTS, n + SUMS + 1 - HOT_STEPS)

                with dve.Fori(0, STEPS // BODY - 1) as it:
                    body(it, False)
                body(STEPS // BODY - 1, True)

            @block.scalar
            def _(act):
                act.sem_inc(ev_act, RING)
                act.wait_ge(less_max, 1)
                nc.scalar.activation(bwd[:], fwd[:], ACT.Exp, scale=float(D) ** -0.5).then_inc(raised, 1)
                for n, g in enumerate(range(0, CT, QUART)):
                    if n % 2 == 1:
                        m = min(QUART, CT - g)
                        act.wait_ge(back, n + 1)
                        nc.scalar.activation(scores[:, g:g + m],
                                             big[:, g * P:(g + m) * P].rearrange("p (g c h) -> p g c h", g=m, h=HEADS),
                                             ACT.Copy).then_inc(e_known, 1)
                act.wait_ge(e_known, QUARTS)
                with act.Fori(0, STEPS // BODY) as it:
                    for s in range(BODY):
                        n = BODY * it + s
                        act.wait_ge(summed, n + 1)
                        nc.scalar.activation(ev[:, s % SUMS, :, C:AGG], k.edge[:, bass.ds(n * TPS, TPS), :], ACT.Copy)
                        act.wait_ge(k.rows_in[s % RING], 16 * TPS * (BODY // RING * it + (gathered_before + s // RING + 1)))
                        for t in range(TPS):
                            for h in range(DVE_HEADS2, HEADS):
                                last = nc.scalar.activation(
                                    ev[:, s % SUMS, t, h * D:(h + 1) * D], rows[:, s % RING, t, h * D:(h + 1) * D], ACT.Copy,
                                    scale=k.edge[:, bass.ds(n * TPS + t, 1), h:h + 1].rearrange("p a b -> p (a b)"))
                        last.then_inc(ev_act, 1)


def finish(nc, k):
    GB = 4
    GROUPS = BLOCKS // GB
    GN = GB * P
    ZS = 4
    with ExitStack() as stack:
        ph = Phase(nc, stack, "mlp")
        w1 = [ph.sb(f"w1{part}", [P, KC, HID], F32R) for part in ("hi", "lo")]
        w2 = [ph.sb(f"w2{part}", [P, FC, C], F32R) for part in ("hi", "lo")]
        gain, shift, b2 = (ph.sb(n, [P, C]) for n in ("gain", "shift", "b2"))
        b1 = ph.sb("b1", [P, FC])
        skip = ph.sb("skip", [P, GB, C])
        enc = ph.sb("enc", [P, GB, C])
        y = ph.sb("y", [P, 2, GB, C])
        yt_hi = ph.sb("yt_hi", [P, KC, GN], F32R)
        yt_lo = ph.sb("yt_lo", [P, KC, GN], F32R)
        h_all = ph.sb("h_all", [P, 2, GN])
        z = ph.sb("z", [P, ZS, C])
        inv = ph.sb("inv", [P, GB, HEADS])
        y_stats, y_mean_var, y_scale = ph.sb("y_stats", [P, GB, 6]), ph.sb("y_mean_var", [P, GB, 2]), ph.sb("y_scale", [P, 2, GB])
        z_stats, z_mean_var, z_scale = ph.sb("z_stats", [P, 2, 6]), ph.sb("z_mean_var", [P, 2, 2]), ph.sb("z_scale", [P, 2, 2])
        yt_ps = [ph.ps(f"yt_ps{i}", [P, C]) for i in range(2)]
        h_ps = [ph.ps(f"h_ps{i}", [P, GN]) for i in range(2)]
        z_ps = [ph.ps(f"z_ps{i}", [P, C]) for i in range(2)]
        PIECES = 4
        with ExitStack() as early:
            raw_t = early.enter_context(nc.sbuf_tensor("mlp_raw", [P, PIECES, KC, C], F32))
        h_hi = ph.sb("h_hi", [P, FC, GN], F32R)
        h_lo = ph.sb("h_lo", [P, FC, GN], F32R)
        raw = [raw_t[:, i] for i in range(PIECES)]
        w1_v = k.W1.rearrange("(c p) n -> p c n", p=P)
        w2_v = k.W2.rearrange("(c p) n -> p c n", p=P)
        source = [w1_v[:, :, i * C:(i + 1) * C] for i in range(2)] + [w2_v[:, i * KC:(i + 1) * KC, :] for i in range(2)]
        split = [[part[:, :, i * C:(i + 1) * C] for part in w1] for i in range(2)]
        split += [[part[:, i * KC:(i + 1) * KC, :] for part in w2] for i in range(2)]

        const_in, b1_in = ph.sem("const_in"), ph.sem("b1_in")
        raw_in = [ph.sem(f"raw_in{i}") for i in range(PIECES)]
        w_hi, w1_lo, w2_lo = ph.sem("w_hi"), ph.sem("w1_lo"), ph.sem("w2_lo")
        skip_in, skip_free = ph.sem("skip_in"), ph.sem("skip_free")
        enc_in, enc_ready, enc_free = ph.sem("enc_in"), ph.sem("enc_ready"), ph.sem("enc_free")
        steps, var_known, std_known = ph.sem("steps"), ph.sem("var_known"), ph.sem("std_known")
        y_ready, turned, y_hi, y_lo = ph.sem("y_ready"), ph.sem("turned"), ph.sem("y_hi"), ph.sem("y_lo")
        y_b2 = ph.sem("y_b2")
        h_product, h_taken, h_split = ph.sem("h_product"), ph.sem("h_taken"), ph.sem("h_split")
        z_product, z_taken, out_ready = ph.sem("z_product"), ph.sem("z_taken"), ph.sem("out_ready")
        stored = [ph.sem(f"stored{i}") for i in range(ZS)]

        with nc.Block() as block:
            @block.sync
            def _(sp):
                def load_skip(g):
                    if g > 0:
                        sp.wait_ge(skip_free, g)
                    rows = k.skip_d[g * GN:(g + 1) * GN, :]
                    sp.dma_start(skip[:], rows.rearrange("(i p) c -> p i c", p=P)).then_inc(skip_in, 16)

                def load_enc(g):
                    if g > 0:
                        sp.wait_ge(enc_free, g)
                    rows = k.x[g * GN:(g + 1) * GN, :]
                    sp.dma_start(enc[:], rows.rearrange("(i p) c -> p i c", p=P)).then_inc(enc_in, 16)

                def store(b):
                    sp.wait_ge(out_ready, b + 1)
                    rows = min(P, NODES - b * P)
                    sp.dma_start(k.out[b * P:b * P + rows, :], z[0:rows, b % ZS, :]).then_inc(stored[b % ZS], 16)

                load_skip(0)
                for i in range(PIECES):
                    sp.dma_start(raw[i], source[i]).then_inc(raw_in[i], 16)
                with nc.allow_non_contiguous_dma(reason="a few hundred elements"):
                    sp.dma_start(b1[:], k.b1.rearrange("(c p) -> p c", p=P)).then_inc(b1_in, 16)
                load_enc(0)
                load_skip(1)
                for g in range(GROUPS):
                    if g > 0:
                        store(GB * g - 2)
                        store(GB * g - 1)
                        load_enc(g)
                    if g + 2 < GROUPS:
                        load_skip(g + 2)
                    store(GB * g)
                    store(GB * g + 1)
                store(BLOCKS - 2)
                store(BLOCKS - 1)
                for i in range(ZS):
                    sp.wait_ge(stored[i], 16 * (BLOCKS // ZS))

            @block.gpsimd
            def _(pool):
                for t, a in ((gain, k.ln_g), (shift, k.ln_b), (b2, k.b2)):
                    pool.dma_start(t[:], a.partition_broadcast(P)).then_inc(const_in, 16)

                def y_plus_b2(g):
                    for i in range(GB):
                        pool.wait_ge(turned, GB * g + i + 1)
                        nc.gpsimd.tensor_tensor(y[:, g % 2, i, :], y[:, g % 2, i, :], b2[:], ALU.add).then_inc(y_b2, 1)

                def h_low(g):
                    for f in range(FC):
                        pool.wait_ge(h_taken, 2 * (FC * g + f + 1))
                        nc.gpsimd.tensor_tensor(h_lo[:, f, :], h_all[:, f % 2, :], h_hi[:, f, :].bitcast(F32),
                                                ALU.subtract).then_inc(h_split, 1)

                def twice_enc(g):
                    pool.wait_ge(enc_in, 16 * (g + 1))
                    nc.gpsimd.tensor_tensor(enc[:], enc[:], enc[:], ALU.add).then_inc(enc_ready, 1)
                    pool.wait_ge(enc_ready, 2 * g + 1)
                    nc.gpsimd.tensor_tensor(enc[:], enc[:], shift[:].unsqueeze(1).to_broadcast([P, GB, C]),
                                            ALU.add).then_inc(enc_ready, 1)

                pool.wait_ge(const_in, 48)
                for i in (2, 3):
                    pool.wait_ge(w_hi, i + 1)
                    nc.gpsimd.tensor_tensor(split[i][1], raw[i], split[i][0].bitcast(F32), ALU.subtract).then_inc(w2_lo, 1)
                y_plus_b2(0)
                pool.wait_ge(w2_lo, 2)
                for g in range(GROUPS):
                    h_low(g)
                    twice_enc(g)
                    if g + 1 < GROUPS:
                        y_plus_b2(g + 1)

            @block.vector
            def _(dve):
                v = nc.vector
                marks, roots = [0], [0]

                def mark(ins):
                    marks[0] += 1
                    ins.then_inc(steps, 1)
                    return marks[0]

                def after(m):
                    dve.wait_ge(steps, m)

                def weight_low(i):
                    dve.wait_ge(w_hi, i + 1)
                    v.tensor_tensor(split[i][1], raw[i], split[i][0].bitcast(F32), ALU.subtract).then_inc(w1_lo, 1)

                def inverse_root(scale):
                    roots[0] += 1
                    dve.wait_ge(std_known, roots[0])
                    return mark(v.reciprocal(scale[:, 1], scale[:, 0]))

                def first_norms(g):
                    par = g % 2
                    group = k.work[:, GB * g * AGG:GB * (g + 1) * AGG].rearrange("p (i n) -> p i n", n=AGG)
                    by_head = lambda t: t.rearrange("p i (h d) -> p i h d", d=D)
                    if g > 0:
                        dve.wait_ge(y_ready, GB * g)
                    after(mark(v.tensor_scalar(inv[:], group[:, :, C:AGG], 1e-16, None, ALU.add)))
                    after(mark(v.reciprocal(inv[:], inv[:])))
                    if g >= 2:
                        dve.wait_ge(z_taken, GB * (g - 1))
                    after(mark(v.tensor_tensor(by_head(y[:, par]), by_head(group[:, :, 0:C]),
                                               inv[:].unsqueeze(3).to_broadcast([P, GB, HEADS, D]), ALU.mult)))
                    dve.wait_ge(skip_in, 16 * (g + 1))
                    after(mark(v.tensor_tensor(y[:, par], y[:, par], skip[:], ALU.add)))
                    dve.sem_inc(skip_free, 1)
                    done = [mark(v.bn_stats(y_stats[:, i], y[:, par, i, :])) for i in range(GB)]
                    for i in range(GB):
                        after(done[i])
                        last = v.bn_aggr(y_mean_var[:, i], y_stats[:, i])
                    last.then_inc(var_known, 1)
                    scaled = inverse_root(y_scale)
                    for i in range(GB):
                        done[i] = mark(v.scalar_tensor_tensor(y[:, par, i, :], y[:, par, i, :], y_mean_var[:, i, 0:1], gain[:],
                                                              ALU.subtract, ALU.mult))
                    after(scaled)
                    for i in range(GB):
                        after(done[i])
                        v.scalar_tensor_tensor(y[:, par, i, :], y[:, par, i, :], y_scale[:, 1, i:i + 1], shift[:],
                                               ALU.mult, ALU.add).then_inc(y_ready, 1)

                def y_low(g, i):
                    b = GB * g + i
                    dve.wait_ge(y_hi, b + 1)
                    v.tensor_tensor(yt_lo[:, :, i * P:(i + 1) * P], yt_ps[i % 2][:].rearrange("p (c n) -> p c n", c=KC),
                                    yt_hi[:, :, i * P:(i + 1) * P].bitcast(F32), ALU.subtract).then_inc(y_lo, 1)

                def moments(b):
                    j = b % 2
                    after(mark(v.bn_stats(z_stats[:, j], z[:, b % ZS, :])))
                    last = v.bn_aggr(z_mean_var[:, j], z_stats[:, j])
                    if j == 1:
                        last.then_inc(var_known, 1)

                def take(b):
                    dve.wait_ge(z_product, b + 1)
                    dve.wait_ge(y_b2, b + 1)
                    if b >= ZS:
                        dve.wait_ge(stored[b % ZS], 16 * (b // ZS))
                    v.tensor_tensor(z[:, b % ZS, :], z_ps[b % 2][:], y[:, b // GB % 2, b % GB, :], ALU.add).then_inc(z_taken, 1)
                    dve.wait_ge(z_taken, b + 1)
                    if b >= 2:
                        dve.wait_ge(out_ready, b // 2 * 2)
                    moments(b)

                def last_norms(pair):
                    g = pair[0] // GB
                    known = [0, 0]
                    after(inverse_root(z_scale))
                    for n, b in enumerate(pair):
                        at = z[:, b % ZS, :]
                        known[n] = mark(v.scalar_tensor_tensor(at, at, z_mean_var[:, b % 2, 0:1], gain[:], ALU.subtract, ALU.mult))
                    dve.wait_ge(enc_ready, 2 * (g + 1))
                    for n, b in enumerate(pair):
                        after(known[n])
                        at = z[:, b % ZS, :]
                        known[n] = mark(v.scalar_tensor_tensor(at, at, z_scale[:, 1, b % 2:b % 2 + 1], enc[:, b % GB, :], ALU.mult, ALU.add))
                    for n, b in enumerate(pair):
                        after(known[n])
                        moments(b)
                    if pair[1] % GB == GB - 1:
                        dve.sem_inc(enc_free, 1)
                    after(inverse_root(z_scale))
                    for n, b in enumerate(pair):
                        at = z[:, b % ZS, :]
                        v.tensor_scalar(at, at, z_mean_var[:, b % 2, 0:1], z_scale[:, 1, b % 2:b % 2 + 1],
                                        ALU.subtract, ALU.mult).then_inc(out_ready, 1)

                weight_low(0)
                dve.wait_ge(const_in, 48)
                first_norms(0)
                for i in range(GB):
                    y_low(0, i)
                weight_low(1)
                for g in range(GROUPS):
                    if g > 0:
                        pair = (GB * g - 2, GB * g - 1)
                        for b in pair:
                            take(b)
                        last_norms(pair)
                    if g + 1 < GROUPS:
                        first_norms(g + 1)
                    pair = (GB * g, GB * g + 1)
                    for b in pair:
                        take(b)
                    if g + 1 < GROUPS:
                        y_low(g + 1, 0)
                        y_low(g + 1, 1)
                    last_norms(pair)
                    if g + 1 < GROUPS:
                        y_low(g + 1, 2)
                        y_low(g + 1, 3)
                pair = (BLOCKS - 2, BLOCKS - 1)
                for b in pair:
                    take(b)
                last_norms(pair)

            @block.scalar
            def _(act):
                roots = [0]

                def root(scale, mean_var):
                    roots[0] += 1
                    act.wait_ge(var_known, roots[0])
                    nc.scalar.activation(scale[:, 0], mean_var[:, :, 1], ACT.Sqrt, bias=k.eps[:, 0:1]).then_inc(std_known, 1)

                def y_high(g, blocks):
                    for i in blocks:
                        act.wait_ge(turned, GB * g + i + 1)
                        nc.scalar.activation(yt_hi[:, :, i * P:(i + 1) * P], yt_ps[i % 2][:].rearrange("p (c n) -> p c n", c=KC),
                                             ACT.Copy).then_inc(y_hi, 1)

                def h_high(g, f):
                    n = FC * g + f
                    act.wait_ge(h_product, n + 1)
                    if n >= 2:
                        act.wait_ge(h_split, n - 1)
                    nc.scalar.activation(h_all[:, f % 2, :], h_ps[f % 2][:], ACT.Relu, bias=b1[:, f:f + 1]).then_inc(h_taken, 1)
                    nc.scalar.activation(h_hi[:, f, :], h_ps[f % 2][:], ACT.Relu, bias=b1[:, f:f + 1]).then_inc(h_taken, 1)

                for i in range(PIECES):
                    act.wait_ge(raw_in[i], 16)
                    nc.scalar.activation(split[i][0], raw[i], ACT.Copy).then_inc(w_hi, 1)
                act.wait_ge(b1_in, 16)
                root(y_scale, y_mean_var)
                y_high(0, range(GB))
                act.wait_ge(w1_lo, 2)
                for g in range(GROUPS):
                    for f in range(FC):
                        if g > 0 and f in (0, 2):
                            root(z_scale, z_mean_var)
                        if g + 1 < GROUPS and f == (6 if g > 0 else 5):
                            root(y_scale, y_mean_var)
                        h_high(g, f)
                    root(z_scale, z_mean_var)
                    if g + 1 < GROUPS:
                        y_high(g + 1, range(0, 2))
                    root(z_scale, z_mean_var)
                    if g + 1 < GROUPS:
                        y_high(g + 1, range(2, GB))
                root(z_scale, z_mean_var)
                root(z_scale, z_mean_var)

            @block.tensor
            def _(pe):
                def turn(g, i):
                    b = GB * g + i
                    pe.wait_ge(y_ready, b + 1)
                    if b >= 2:
                        pe.wait_ge(y_lo, b - 1)
                    for c in range(KC):
                        last = nc.tensor.transpose(yt_ps[i % 2][:, c * P:(c + 1) * P],
                                                   y[:, g % 2, i, c * P:(c + 1) * P], k.ident[:])
                    last.then_inc(turned, 1)

                def hidden(g):
                    pe.wait_ge(y_lo, GB * (g + 1))
                    for f in range(FC):
                        n = FC * g + f
                        if g == 0 and f % KC == 0:
                            pe.wait_ge(w1_lo, f // KC + 1)
                        if n >= 2:
                            pe.wait_ge(h_taken, 2 * (n - 1))
                        split_product(nc, h_ps[f % 2][:], lambda c: w1[0][:, c, f * P:(f + 1) * P],
                                      lambda c: w1[1][:, c, f * P:(f + 1) * P], lambda c: yt_hi[:, c, :],
                                      lambda c: yt_lo[:, c, :], range(KC)).then_inc(h_product, 1)

                def result(g, i):
                    b = GB * g + i
                    if b >= 2:
                        pe.wait_ge(z_taken, b - 1)
                    at = slice(i * P, (i + 1) * P)
                    for f in range(FC):
                        if i == 0:
                            pe.wait_ge(h_split, FC * g + f + 1)
                            if g == 0 and f % KC == 0:
                                pe.wait_ge(w2_lo, f // KC + 1)
                        for n, (a, w) in enumerate(((h_hi, w2[0]), (h_hi, w2[1]), (h_lo, w2[0]))):
                            last = nc.tensor.matmul(z_ps[i % 2][:], a[:, f, at], w[:, f, :],
                                                    start=f == 0 and n == 0, stop=f == FC - 1 and n == 2)
                    last.then_inc(z_product, 1)

                for i in range(GB):
                    turn(0, i)
                for g in range(GROUPS):
                    hidden(g)
                    for i in range(GB):
                        result(g, i)
                        if g + 1 < GROUPS and i in (1, 2):
                            turn(g + 1, 2 * i - 2)
                            turn(g + 1, 2 * i - 1)


def graph_attention(nc, x, src, dst, Wq, bq, Wk, bk, Wv, bv, Ws, bs, W1, b1, W2, b2, ln_g, ln_b, out):
    k = Shared()
    k.x, k.src, k.dst, k.out = x, src, dst, out
    k.Wq, k.bq, k.Wk, k.bk, k.Wv, k.bv, k.Ws, k.bs = Wq, bq, Wk, bk, Wv, bv, Ws, bs
    k.W1, k.b1, k.W2, k.b2, k.ln_g, k.ln_b = W1, b1, W2, b2, ln_g, ln_b
    k.k_d, k.v_d, k.skip_d = (nc.dram_tensor(n, [ROWS, C], F32).ap() for n in ("k_rows", "v_rows", "skip_rows"))
    k.local_d = nc.dram_tensor("local_dst", [TABLE * SE], BF16).ap()
    with ExitStack() as stack:
        ph = Phase(nc, stack, "all")
        k.ident, k.iota_row, k.ones = (ph.sb(n, [P, P]) for n in ("ident", "iota_row", "ones"))
        k.iota_col, k.eps = ph.sb("iota_col", [P, 1]), ph.sb("eps", [P, 1])
        k.work = ph.sb("work", [P, BLOCKS * AGG])
        build_constants(nc, k)
        with ExitStack() as graph:
            gr = Phase(nc, graph, "graph")
            k.src_t = gr.sb("src_t", [P, TABLE, TPS], I32)
            k.local_t = gr.sb("local_t", [P, TABLE, TPS])
            k.block_row = gr.sb("block_row", [1, TABLE], I32)
            k.fresh = gr.sb("fresh", [P, SLOTS + 1])
            k.link_f, k.link_b, k.seed_f, k.seed_b = (gr.sb(n, [1, HEADS, CHUNKS])
                                                      for n in ("link_f", "link_b", "seed_f", "seed_b"))
            k.rows_in = [gr.sem(f"rows_in{r}") for r in range(RING)]
            build_step_tables(nc, k)
            for layer in range(LAYERS):
                project(nc, k, layer)
                with ExitStack() as edges:
                    k.edge = Phase(nc, edges, f"layer{layer}").sb("edge", [P, TILES, HEADS])
                    score(nc, k, layer)
                    soften_collect(nc, k, layer)
        finish(nc, k)


_WEIGHTS = ["Wq", "bq", "Wk", "bk", "Wv", "bv", "Ws", "bs", "W1", "b1", "W2", "b2", "ln_g", "ln_b"]


def kernel(**inputs):
    import numpy as _np
    import concourse.bacc as _bacc
    from concourse.bass_utils import run_bass_kernel_spmd as _run

    x = _np.zeros((ROWS, C), _np.float32)
    x[:NODES] = inputs["x"]
    src = _np.zeros((EDGE_ROWS, SE), _np.int32)
    src.reshape(-1)[:EDGES] = inputs["src"]
    dst = _np.full(EDGE_ROWS * SE, PAD_DST, _np.int32)
    dst[:EDGES] = inputs["dst"]
    arrays = {"x": x, "src": src, "dst": dst}
    for name in _WEIGHTS:
        arrays[name] = _np.ascontiguousarray(inputs[f"L0_gnn_{name}"])

    nc = _bacc.Bacc("TRN2", target_bir_lowering=False, num_devices=1)
    args = {n: nc.dram_tensor(f"in_{n}", a.shape, mybir.dt.from_np(a.dtype), kind="ExternalInput").ap()
            for n, a in arrays.items()}
    out = nc.dram_tensor("out_0", (NODES, C), F32, kind="ExternalOutput").ap()
    graph_attention(nc, out=out, **args)
    r = _run(nc, [{f"in_{n}": a for n, a in arrays.items()}], core_ids=[0])
    return r.results[0]["out_0"]
```

```python
import concourse.bass as bass
from concourse import mybir
from contextlib import ExitStack

F32 = mybir.dt.float32
F32R = mybir.dt.float32r
BF16 = mybir.dt.bfloat16
I32 = mybir.dt.int32
ALU = mybir.AluOpType
ACT = mybir.ActivationFunctionType
AX = mybir.AxisListType

P = 128
NODES, EDGES, C, HEADS, LAYERS = 2500, 40000, 512, 8, 2
HID = 2 * C
D = C // HEADS
KC = C // P
FC = HID // P
BLOCKS = -(-NODES // P)
ROWS = BLOCKS * P
TPS = 2
SE = TPS * P
EDGE_ROWS = -(-EDGES // SE)
STEPS = EDGE_ROWS + BLOCKS - 1
TILES = STEPS * TPS
STEP_GROUPS = 2
TABLE = STEP_GROUPS * P
CHUNKS = P // HEADS
CT = TILES // CHUNKS
SLOTS = CT * P
HALF = 8
BODY = 2 * HALF
RING, V_RING = HALF, BODY
PRODS = 4
EVS, SUMS = 4, 2
HOT_STEPS, HOTS = 2, 4
Q_PARTS = 3
AGG = C + HEADS
DVE_HEADS1, DVE_HEADS2 = 4, 5
LAST_HEADS1 = 5
BIG = 1e30
PAD_DST = 1 << 20
EPS = 1e-5
assert STEPS % BODY == 0 and TILES % CHUNKS == 0 and STEPS + HALF <= TABLE and 2 * KC == HALF


class Shared:
    pass


class Phase:

    def __init__(self, nc, stack, tag):
        self.nc, self.stack, self.tag, self.sems = nc, stack, tag, []

    def sb(self, name, shape, dt=F32):
        return self.stack.enter_context(self.nc.sbuf_tensor(f"{self.tag}_{name}", shape, dt))

    def ps(self, name, shape):
        return self.stack.enter_context(self.nc.psum_tensor(f"{self.tag}_{name}", shape, F32))

    def sem(self, name):
        self.sems.append(self.nc.alloc_semaphore(f"{self.tag}_{name}"))
        return self.sems[-1]

    def give_back(self):
        self.nc.clear_and_free_semaphores(self.sems)
        self.nc.all_engine_barrier()


def chain(eng, sem):
    count = [0]

    def link(ins):
        count[0] += 1
        ins.then_inc(sem, 1)
        eng.wait_ge(sem, count[0])

    return link


def build_constants(nc, k):
    with ExitStack() as stack:
        ph = Phase(nc, stack, "const")
        row_i = ph.sb("row_i", [P, P], I32)
        col_i = ph.sb("col_i", [P, 1], I32)
        iotas_done, steps = ph.sem("iotas_done"), ph.sem("steps")
        with nc.Block() as block:
            @block.gpsimd
            def _(pool):
                nc.gpsimd.iota(row_i[:], pattern=[[1, P]], base=0, channel_multiplier=0).then_inc(iotas_done, 1)
                nc.gpsimd.iota(col_i[:], pattern=[[0, 1]], base=0, channel_multiplier=1).then_inc(iotas_done, 1)

            @block.vector
            def _(dve):
                link = chain(dve, steps)
                nc.vector.memset(k.ones[:], 1.0)
                nc.vector.memset(k.eps[:], EPS)
                dve.wait_ge(iotas_done, 2)
                nc.vector.tensor_copy(k.iota_row[:], row_i[:])
                link(nc.vector.tensor_copy(k.iota_col[:], col_i[:]))
                link(nc.vector.tensor_scalar(k.ident[:], k.iota_row[:], k.iota_col[:, 0:1], None, ALU.is_equal))


def build_step_tables(nc, k):
    with ExitStack() as stack:
        ph = Phase(nc, stack, "tab")
        cols = EDGE_ROWS * SE // P
        dst_i = ph.sb("dst_i", [P, cols], I32)
        dst_f = ph.sb("dst_f", [P, cols])
        below = ph.sb("below", [P, BLOCKS + 1, cols])
        count = ph.sb("count", [P, BLOCKS + 1])
        start = ph.sb("start", [P, BLOCKS + 1])
        start_i = ph.sb("start_i", [P, BLOCKS + 1], I32)
        first_row = ph.sb("first_row", [P, BLOCKS])
        stop_row = ph.sb("stop_row", [P, BLOCKS])
        n_steps = ph.sb("n_steps", [P, BLOCKS])
        zeros = ph.sb("zeros", [P, BLOCKS])
        steps_end = ph.sb("steps_end", [P, BLOCKS])
        lead = ph.sb("lead", [P, BLOCKS])
        lead_diff = ph.sb("lead_diff", [P, BLOCKS])
        passed = ph.sb("passed", [P, BLOCKS])
        step_no = ph.sb("step_no", [P, STEP_GROUPS])
        block_no = ph.sb("block_no", [P, STEP_GROUPS])
        block_lo = ph.sb("block_lo", [P, STEP_GROUPS])
        row_no = ph.sb("row_no", [P, STEP_GROUPS])
        row_i = ph.sb("row_i", [P, STEP_GROUPS], I32)
        src_i = ph.sb("src_i", [P, STEP_GROUPS, SE], I32)
        sdst_i = ph.sb("sdst_i", [P, STEP_GROUPS, SE], I32)
        src_f = ph.sb("src_f", [P, STEP_GROUPS, SE])
        sdst_f = ph.sb("sdst_f", [P, STEP_GROUPS, SE])
        local = ph.sb("local", [P, STEP_GROUPS, SE])
        inside = ph.sb("inside", [P, STEP_GROUPS, SE])
        inside_hi = ph.sb("inside_hi", [P, STEP_GROUPS, SE])
        key = ph.sb("key", [P, STEP_GROUPS, SE])
        local16 = ph.sb("local16", [P, STEP_GROUPS, SE], BF16)
        key_t = k.work[:, 0:TABLE * TPS].rearrange("p (s t) -> p s t", t=TPS)
        big = ph.ps("big", [P, 3 * STEP_GROUPS * TPS * P])
        small = ph.ps("small", [P, 512])

        dst_in, steps = ph.sem("dst_in"), ph.sem("steps")
        counted, summed = ph.sem("counted"), ph.sem("summed")
        rows_known, src_in, sdst_in = ph.sem("rows_known"), ph.sem("src_in"), ph.sem("sdst_in")
        steps_known, turned = ph.sem("steps_known"), ph.sem("turned")
        local_known, local_out = ph.sem("local_known"), ph.sem("local_out")

        def pair(which, g, t):
            n = (which * STEP_GROUPS + g) * TPS + t
            return big[:, n * P:(n + 1) * P]

        with nc.Block() as block:
            @block.sync
            def _(sp):
                sp.dma_start(dst_i[:], k.dst.rearrange("(p c) -> p c", p=P)).then_inc(dst_in, 16)
                sp.wait_ge(local_known, 1)
                for g in range(STEP_GROUPS):
                    sp.dma_start(k.local_d[g * P * SE:(g + 1) * P * SE].rearrange("(p e) -> p e", p=P),
                                 local16[:, g, :]).then_inc(local_out, 16)
                sp.wait_ge(local_out, 16 * STEP_GROUPS)

            @block.gpsimd
            def _(pool):
                pool.wait_ge(rows_known, 1)
                for g in range(STEP_GROUPS):
                    at = bass.IndirectOffsetOnAxis(ap=row_i[:, g:g + 1], axis=0)
                    nc.gpsimd.indirect_dma_start(src_i[:, g, :], None, k.src, at).then_inc(src_in, 16)
                    nc.gpsimd.indirect_dma_start(sdst_i[:, g, :], None,
                                                 k.dst.rearrange("(r e) -> r e", e=SE), at).then_inc(sdst_in, 16)

            @block.vector
            def _(dve):
                link = chain(dve, steps)
                v = nc.vector
                dve.wait_ge(dst_in, 16)
                link(v.tensor_copy(dst_f[:], dst_i[:]))
                for b in range(BLOCKS + 1):
                    last = v.tensor_scalar(below[:, b, :], dst_f[:], float(b * P), 0.0, ALU.is_lt, ALU.add,
                                           accum_out=count[:, b:b + 1])
                last.then_inc(counted, 1)
                dve.wait_ge(summed, 1)
                link(v.tensor_copy(start[:], small[:, 0:BLOCKS + 1]))
                link(v.tensor_copy(start_i[:], start[:]))
                link(v.tensor_scalar(start_i[:], start_i[:], SE.bit_length() - 1, None, ALU.logical_shift_right))
                link(v.tensor_copy(first_row[:], start_i[:, 0:BLOCKS]))
                link(v.tensor_scalar(stop_row[:], start[:, 1:], float(SE - 1), None, ALU.add))
                link(v.tensor_copy(start_i[:, 0:BLOCKS], stop_row[:]))
                link(v.tensor_scalar(start_i[:], start_i[:], SE.bit_length() - 1, None, ALU.logical_shift_right))
                link(v.tensor_copy(stop_row[:], start_i[:, 0:BLOCKS]))
                link(v.tensor_tensor(n_steps[:], stop_row[:], first_row[:], ALU.subtract))
                link(v.tensor_tensor(passed[:], start[:, 1:], start[:, 0:BLOCKS], ALU.is_gt))
                link(v.tensor_tensor(n_steps[:], n_steps[:], passed[:], ALU.mult))
                link(v.memset(zeros[:], 0.0))
                link(v.tensor_tensor_scan(steps_end[:], n_steps[:], zeros[:], 0.0, ALU.add, ALU.add))
                link(v.tensor_tensor(lead[:], first_row[:], n_steps[:], ALU.add))
                link(v.tensor_tensor(lead[:], lead[:], steps_end[:], ALU.subtract))
                link(v.memset(lead_diff[:], 0.0))
                link(v.tensor_tensor(lead_diff[:, 0:BLOCKS - 1], lead[:, 1:], lead[:, 0:BLOCKS - 1], ALU.subtract))
                for g in range(STEP_GROUPS):
                    link(v.tensor_scalar(step_no[:, g:g + 1], k.iota_col[:], float(g * P), None, ALU.add))
                    link(v.tensor_scalar(passed[:], steps_end[:], step_no[:, g:g + 1], None, ALU.is_le))
                    link(v.tensor_reduce(block_no[:, g:g + 1], passed[:], AX.X, ALU.add))
                    link(v.tensor_tensor(passed[:], passed[:], lead_diff[:], ALU.mult))
                    link(v.tensor_reduce(row_no[:, g:g + 1], passed[:], AX.X, ALU.add))
                    link(v.tensor_tensor(row_no[:, g:g + 1], row_no[:, g:g + 1], lead[:, 0:1], ALU.add))
                    link(v.tensor_tensor(row_no[:, g:g + 1], row_no[:, g:g + 1], step_no[:, g:g + 1], ALU.add))
                link(v.tensor_scalar(row_no[:], row_no[:], float(EDGE_ROWS - 1), 0.0, ALU.min, ALU.max))
                v.tensor_copy(row_i[:], row_no[:]).then_inc(rows_known, 1)
                link(v.tensor_scalar(block_lo[:], block_no[:], float(P), None, ALU.mult))
                v.tensor_scalar(block_no[:], block_no[:], float(BLOCKS - 1), None, ALU.min).then_inc(steps_known, 1)

                dve.wait_ge(src_in, 16 * STEP_GROUPS)
                link(v.tensor_copy(src_f[:], src_i[:]))
                dve.wait_ge(sdst_in, 16 * STEP_GROUPS)
                link(v.tensor_copy(sdst_f[:], sdst_i[:]))
                for g in range(STEP_GROUPS):
                    link(v.tensor_scalar(local[:, g, :], sdst_f[:, g, :], block_lo[:, g:g + 1], None, ALU.subtract))
                link(v.tensor_scalar(inside[:], local[:], 0.0, None, ALU.is_ge))
                link(v.tensor_scalar(inside_hi[:], local[:], float(P), None, ALU.is_lt))
                link(v.tensor_tensor(inside[:], inside[:], inside_hi[:], ALU.mult))
                for out, of in ((local, local), (key, sdst_f)):
                    link(v.tensor_scalar(out[:], of[:], 1.0, None, ALU.add))
                    link(v.tensor_tensor(out[:], out[:], inside[:], ALU.mult))
                    link(v.tensor_scalar(out[:], out[:], -1.0, None, ALU.add))
                v.tensor_copy(local16[:], local[:]).then_inc(local_known, 1)

                dve.wait_ge(turned, 1)
                v.tensor_copy(k.block_row[:], small[0:1, 128:128 + TABLE])
                for g in range(STEP_GROUPS):
                    for t in range(TPS):
                        at = slice(g * P, (g + 1) * P)
                        v.tensor_copy(k.local_t[:, at, t], pair(1, g, t))
                        v.tensor_copy(key_t[:, at, t], pair(2, g, t))
            @block.scalar
            def _(act):
                act.wait_ge(turned, 1)
                for g in range(STEP_GROUPS):
                    for t in range(TPS):
                        nc.scalar.copy(k.src_t[:, g * P:(g + 1) * P, t], pair(0, g, t))

            @block.tensor
            def _(pe):
                pe.wait_ge(counted, 1)
                nc.tensor.matmul(small[:, 0:BLOCKS + 1], k.ones[:], count[:], start=True, stop=True).then_inc(summed, 1)
                pe.wait_ge(steps_known, 1)
                pe.wait_ge(local_known, 1)
                for g in range(STEP_GROUPS):
                    nc.tensor.matmul(small[0:1, 128 + g * P:128 + (g + 1) * P], block_no[:, g:g + 1], k.ident[:],
                                     start=True, stop=True)
                for which, table in enumerate((src_f, local, key)):
                    for g in range(STEP_GROUPS):
                        for t in range(TPS):
                            last = nc.tensor.transpose(pair(which, g, t), table[:, g, t * P:(t + 1) * P], k.ident[:])
                last.then_inc(turned, 1)
        ph.give_back()


def split_product(nc, out, a_hi, a_lo, b_hi, b_lo, chunks):
    n = 3 * len(chunks)
    i = 0
    for c in chunks:
        for a, b in ((a_hi, b_hi), (a_hi, b_lo), (a_lo, b_hi)):
            last = nc.tensor.matmul(out, a(c), b(c), start=i == 0, stop=i == n - 1)
            i += 1
    return last


def project(nc, k, layer):
    with ExitStack() as stack:
        ph = Phase(nc, stack, f"proj{layer}")
        OUTS = 2
        whole = lambda t, n: t.rearrange("p (c n) -> p c n", n=n)
        at_edges = k.edge[:].rearrange("p t h -> p (t h)")[:, 0:KC * C]
        at_q = k.q3[:, (BLOCKS - 3) * Q_PARTS * C:].bitcast(F32)[:, 0:KC * C]
        raw = [whole(at_edges, C), whole(at_q, C)]
        w = [[ph.sb(f"w{i}{part}", [P, KC, C], F32R) for part in ("hi", "lo")] for i in range(OUTS)]
        bias = ph.sb("bias", [P, OUTS + 1, C])
        x = ph.sb("x", [P, 2, C])
        enc = ph.sb("enc", [P, 2, C]) if layer else x
        skip = ph.sb("skip", [P, 2, C]) if layer else None
        inv = ph.sb("inv", [P, 2, HEADS]) if layer else None
        xt = ph.sb("xt", [P, 2, 2, KC, P], F32R)
        k_out = ph.sb("k_out", [P, 2, C])
        q_out = ph.sb("q_out", [P, 2, C])
        base = ph.sb("base", [P, 2, C])
        xt_ps = [ph.ps(f"xt_ps{i}", [P, C]) for i in range(2)]
        out_ps = [[ph.ps(f"out_ps{u}{i}", [P, C]) for i in range(OUTS)] for u in range(2)]

        if layer == 0:
            key_t = k.work[:, 0:TILES].rearrange("p (c g) -> p g c", g=CT)
            key8 = k.work[:, TABLE * TPS:TABLE * TPS + SLOTS].rearrange("p (g c h) -> p g c h", g=CT, h=HEADS)
            key_s = k.work[:, TABLE * TPS + SLOTS:TABLE * TPS + 2 * SLOTS]
            row_first, row_last, goes_on, whole_chunk = (ph.sb(n, [1, HEADS, CHUNKS]) for n in
                                                         ("row_first", "row_last", "goes_on", "whole_chunk"))
            key_ps = ph.ps("key_ps", [P, 2, 512])
            QUART = 512 // P
            QUARTS = -(-CT // QUART)
            keys_ready, keys_turned, keys_copied = ph.sem("keys_ready"), ph.sem("keys_turned"), ph.sem("keys_copied")
            ends_turned, marks = ph.sem("ends_turned"), ph.sem("marks")

        raw_in = [ph.sem(f"raw_in{i}") for i in range(OUTS)]
        w_hi, w_lo = ph.sem("w_hi"), ph.sem("w_lo")
        bias_in = ph.sem("bias_in")
        enc_in = [ph.sem("enc_in0"), ph.sem("enc_in1")]
        skip_in = [ph.sem("skip_in0"), ph.sem("skip_in1")] if layer else None
        enc_free, skip_free = ph.sem("enc_free"), ph.sem("skip_free")
        x_ready, turned = ph.sem("x_ready"), ph.sem("turned")
        hi_ready, lo_ready, product = ph.sem("hi_ready"), ph.sem("lo_ready"), ph.sem("product")
        out_done, steps = ph.sem("out_done"), ph.sem("steps")
        q_part, q_rest = ph.sem("q_part"), ph.sem("q_rest")
        xt_stored = [ph.sem("xt_stored0"), ph.sem("xt_stored1")]
        k_stored = [ph.sem("k_stored0"), ph.sem("k_stored1")]
        base_out = [ph.sem("base_out0"), ph.sem("base_out1")]
        flat_xt = lambda u, part: xt[:, u, part].rearrange("p c n -> p (c n)")
        q3_at = lambda b, part: k.q3[:, bass.ds(b * (Q_PARTS * C) + part * C, C)]

        with nc.Block() as block:
            @block.gpsimd
            def _(pool):
                for i, b in enumerate((k.bk, k.bq, k.bs)):
                    pool.dma_start(bias[:, i, :], b[layer].partition_broadcast(P)).then_inc(bias_in, 16)
                pool.wait_ge(bias_in, 16 * (OUTS + 1))

                def skip_base(b, u, it, first):
                    if not first:
                        pool.wait_ge(base_out[u], 16 * it)
                    pool.wait_ge(enc_in[u], 16 * (it + 1))
                    nc.gpsimd.tensor_tensor(base[:, u, :], enc[:, u, :], bias[:, OUTS, :], ALU.add).then_inc(enc_free, 1)
                    pool.wait_ge(enc_free, b + 3)
                    pool.sem_inc(stored_base, 1)
                    pool.dma_start(k.skip_d[layer][bass.ds(b * P, P), :], base[:, u, :]).then_inc(base_out[u], 16)

                def q_leftover(b, u):
                    pool.wait_ge(q_part, 2 * b + 1)
                    nc.gpsimd.tensor_tensor(q_out[:, u, :], q_out[:, u, :], q3_at(b, 0), ALU.subtract).then_inc(q_rest, 1)
                    pool.wait_ge(q_part, 2 * b + 2)
                    nc.gpsimd.tensor_tensor(q3_at(b, 2), q_out[:, u, :], q3_at(b, 1), ALU.subtract).then_inc(q_rest, 1)

                stored_base = ph.sem("stored_base")
                for u in range(2):
                    skip_base(u, u, 0, True)
                with pool.Fori(1, BLOCKS // 2) as it:
                    for u in range(2):
                        skip_base(2 * it + u, u, it, False)
                        q_leftover(2 * it + u - 2, u)
                for u in range(2):
                    q_leftover(BLOCKS - 2 + u, u)
                for u in range(2):
                    pool.wait_ge(base_out[u], 16 * (BLOCKS // 2))

            @block.tensor
            def _(pe):
                def turn(b, u, it):
                    if layer:
                        pe.wait_ge(x_ready, b + 1)
                    else:
                        pe.wait_ge(enc_in[u], 16 * (it + 1))
                    pe.wait_ge(lo_ready, b + 1)
                    for c in range(KC):
                        last = nc.tensor.transpose(xt_ps[u][:, c * P:(c + 1) * P], x[:, u, c * P:(c + 1) * P], k.ident[:])
                    last.then_inc(turned, 1)

                def products(b, u, it, first, ahead):
                    if ahead and not first:
                        turn(b + 1, 1 - u, it + u)
                    pe.wait_ge(lo_ready, b + 3)
                    for i in range(OUTS):
                        if first and i == 1:
                            turn(b + 1, 1 - u, it + u)
                        if first:
                            pe.wait_ge(w_lo, i + 1)
                        pe.wait_ge(out_done, OUTS * b + i + 1)
                        split_product(nc, out_ps[u][i][:], lambda c: xt[:, u, 0, c, :], lambda c: xt[:, u, 1, c, :],
                                      lambda c: w[i][0][:, c, :], lambda c: w[i][1][:, c, :],
                                      range(KC)).then_inc(product, 1)

                if layer == 0:
                    pe.wait_ge(keys_ready, 1)
                    for n in range(QUARTS):
                        if n >= 2:
                            pe.wait_ge(keys_copied, n - 1)
                        for g in range(n * QUART, min((n + 1) * QUART, CT)):
                            last = nc.tensor.transpose(key_ps[:, n % 2, (g % QUART) * P:(g % QUART + 1) * P],
                                                       key8[:, g].rearrange("p c h -> p (c h)"), k.ident[:])
                        last.then_inc(keys_turned, 1)
                turn(0, 0, 0)
                if layer == 0:
                    pe.wait_ge(keys_copied, QUARTS)
                    nc.tensor.matmul(key_ps[0:1, 0, 0:P], key_s[:, 0:1], k.ident[:], start=True, stop=True)
                    nc.tensor.matmul(key_ps[0:1, 0, P:2 * P], key_s[:, SLOTS - 1:SLOTS], k.ident[:],
                                     start=True, stop=True).then_inc(ends_turned, 1)
                products(0, 0, 0, True, True)
                products(1, 1, 0, False, True)
                with pe.Fori(1, BLOCKS // 2 - 1) as it:
                    for u in range(2):
                        products(2 * it + u, u, it, False, True)
                products(BLOCKS - 2, 0, BLOCKS // 2 - 1, False, True)
                products(BLOCKS - 1, 1, BLOCKS // 2 - 1, False, False)

            @block.scalar
            def _(act):
                def load(b, u):
                    first = act.snap(b * P)
                    if layer:
                        act.wait_ge(skip_free, b + 1)
                        act.dma_start(skip[:, u, :], k.skip_d[layer - 1][bass.ds(first, P), :]).then_inc(skip_in[u], 16)
                    act.wait_ge(enc_free, b + 1)
                    act.dma_start(enc[:, u, :], k.x[bass.ds(first, P), :]).then_inc(enc_in[u], 16)

                def high_part(b, u, it):
                    act.wait_ge(turned, b + 1)
                    act.wait_ge(product, OUTS * b + OUTS)
                    act.wait_ge(xt_stored[u], 16 * (it + 1))
                    nc.scalar.activation(flat_xt(u, 0), xt_ps[u][:], ACT.Copy).then_inc(hi_ready, 1)

                def q_parts(b, u):
                    act.wait_ge(out_done, OUTS * (b + 3))
                    nc.scalar.activation(q3_at(b, 0), q_out[:, u, :], ACT.Copy).then_inc(q_part, 1)
                    act.wait_ge(q_rest, 2 * b + 5)
                    nc.scalar.activation(q3_at(b, 1), q_out[:, u, :], ACT.Copy).then_inc(q_part, 1)

                load(0, 0)
                load(1, 1)
                if layer == 0:
                    for n in range(QUARTS):
                        at = slice(n * QUART * P, min((n + 1) * QUART, CT) * P)
                        act.wait_ge(keys_turned, n + 1)
                        nc.scalar.copy(key_s[:, at], key_ps[:, n % 2, 0:at.stop - at.start]).then_inc(keys_copied, 1)
                for i in range(OUTS):
                    act.wait_ge(raw_in[i], 16)
                    nc.scalar.activation(w[i][0][:], raw[i], ACT.Copy).then_inc(w_hi, 1)
                    if i == 0:
                        high_part(0, 0, 0)
                load(2, 0)
                high_part(1, 1, 0)
                with act.Fori(1, BLOCKS // 2 - 1) as it:
                    for u in range(2):
                        load(2 * it + u + 1, 1 - u)
                        high_part(2 * it + u, u, it)
                        q_parts(2 * it + u - 2, u)
                load(BLOCKS - 1, 1)
                for u in range(2):
                    high_part(BLOCKS - 2 + u, u, BLOCKS // 2 - 1)
                    q_parts(BLOCKS - 4 + u, u)
                for u in range(2):
                    q_parts(BLOCKS - 2 + u, u)

            @block.vector
            def _(dve):
                dve.sem_inc(enc_free, 2)
                dve.sem_inc(skip_free, 2)
                dve.sem_inc(lo_ready, 2)
                dve.sem_inc(out_done, 2 * OUTS)
                dve.sem_inc(product, 2 * OUTS)
                dve.sem_inc(q_rest, 4)
                for u in range(2):
                    dve.sem_inc(xt_stored[u], 16)
                    dve.sem_inc(k_stored[u], 16)

                def weight_low(i):
                    dve.wait_ge(w_hi, i + 1)
                    nc.vector.tensor_tensor(w[i][1][:], raw[i], w[i][0][:].bitcast(F32),
                                            ALU.subtract).then_inc(w_lo, 1)

                def assemble(b, u, it):
                    sums = k.work[:, bass.ds(b * AGG, C)]
                    total = k.work[:, bass.ds(b * AGG + C, HEADS)]
                    nc.vector.tensor_scalar(inv[:, u, :], total, 1e-16, None, ALU.add).then_inc(steps, 1)
                    dve.wait_ge(steps, 3 * b + 1)
                    nc.vector.reciprocal(inv[:, u, :], inv[:, u, :]).then_inc(steps, 1)
                    dve.wait_ge(steps, 3 * b + 2)
                    nc.vector.tensor_tensor(x[:, u, :].rearrange("p (h d) -> p h d", h=HEADS),
                                            sums.rearrange("p (h d) -> p h d", h=HEADS),
                                            inv[:, u, :].unsqueeze(2).to_broadcast([P, HEADS, D]), ALU.mult).then_inc(steps, 1)
                    dve.wait_ge(steps, 3 * b + 3)
                    dve.wait_ge(skip_in[u], 16 * (it + 1))
                    nc.vector.tensor_tensor(x[:, u, :], x[:, u, :], skip[:, u, :], ALU.add).then_inc(x_ready, 1)
                    dve.wait_ge(x_ready, b + 1)
                    dve.sem_inc(skip_free, 1)

                def low_part(b, u):
                    dve.wait_ge(hi_ready, b + 1)
                    nc.vector.tensor_tensor(flat_xt(u, 1), xt_ps[u][:], flat_xt(u, 0).bitcast(F32),
                                            ALU.subtract).then_inc(lo_ready, 1)

                def outputs(b, u, it, ahead, beyond):
                    if beyond and layer:
                        assemble(b + 2, u, it + 1)
                    if ahead:
                        low_part(b + 1, 1 - u)
                    dve.wait_ge(k_stored[u], 16 * (it + 1))
                    dve.wait_ge(product, OUTS * (b + 2) + 1)
                    nc.vector.tensor_tensor(k_out[:, u, :], out_ps[u][0][:], bias[:, 0, :], ALU.add).then_inc(out_done, 1)
                    dve.wait_ge(product, OUTS * (b + 2) + 2)
                    dve.wait_ge(q_rest, 2 * b + 4)
                    nc.vector.tensor_tensor(q_out[:, u, :], out_ps[u][1][:], bias[:, 1, :], ALU.add).then_inc(out_done, 1)

                link = chain(dve, marks) if layer == 0 else None
                v = nc.vector

                def mark_starts():
                    dve.wait_ge(keys_copied, QUARTS)
                    v.memset(k.fresh[:, 0:1], 0.0)
                    v.memset(k.fresh[:, SLOTS:SLOTS + 1], 0.0)
                    link(v.tensor_tensor(k.fresh[:, 1:SLOTS], key_s[:, 1:SLOTS], key_s[:, 0:SLOTS - 1], ALU.not_equal))

                def scale_starts():
                    link(v.tensor_scalar(k.fresh[:, 1:SLOTS], k.fresh[:, 1:SLOTS], -BIG, None, ALU.mult))

                def compare_chunks():
                    dve.wait_ge(ends_turned, 1)
                    v.tensor_copy(row_first[:], key_ps[0:1, 0, 0:P].rearrange("p (c h) -> p h c", h=HEADS))
                    for t in (goes_on, k.link_f, k.link_b, k.seed_b):
                        v.memset(t[:], 0.0)
                    link(v.tensor_copy(row_last[:], key_ps[0:1, 0, P:2 * P].rearrange("p (c h) -> p h c", h=HEADS)))
                    v.tensor_tensor(whole_chunk[:], row_first[:], row_last[:], ALU.is_equal)
                    link(v.tensor_tensor(goes_on[:, :, 1:], row_first[:, :, 1:], row_last[:, :, 0:CHUNKS - 1], ALU.is_equal))

                def link_chunks():
                    a, b = slice(1, CHUNKS), slice(0, CHUNKS - 1)
                    v.tensor_tensor(k.link_f[:, :, a], goes_on[:, :, a], whole_chunk[:, :, b], ALU.mult)
                    v.tensor_tensor(k.link_b[:, :, b], goes_on[:, :, a], whole_chunk[:, :, a], ALU.mult)
                    v.tensor_copy(k.seed_b[:, :, b], goes_on[:, :, a])
                    link(v.tensor_copy(k.seed_f[:], goes_on[:]))
                    for t in (k.link_f, k.link_b, k.seed_f, k.seed_b):
                        last = v.tensor_scalar(t[:], t[:], -1.0, BIG, ALU.add, ALU.mult)
                    link(last)

                between = [mark_starts, scale_starts, compare_chunks, link_chunks] if layer == 0 else []
                peeled = len(between) // 2
                if layer == 0:
                    v.tensor_copy(key8, key_t.unsqueeze(3).to_broadcast([P, CT, CHUNKS, HEADS])).then_inc(keys_ready, 1)
                if layer:
                    assemble(0, 0, 0)
                weight_low(0)
                low_part(0, 0)
                weight_low(1)
                if layer:
                    assemble(1, 1, 0)
                dve.wait_ge(bias_in, 16 * (OUTS + 1))
                for b, step in enumerate(between):
                    outputs(b, b % 2, b // 2, True, True)
                    step()
                with dve.Fori(peeled, BLOCKS // 2 - 1) as it:
                    for u in range(2):
                        outputs(2 * it + u, u, it, True, True)
                outputs(BLOCKS - 2, 0, BLOCKS // 2 - 1, True, False)
                outputs(BLOCKS - 1, 1, BLOCKS // 2 - 1, False, False)

            @block.sync
            def _(sp):
                for i, m in enumerate((k.Wk, k.Wq)):
                    sp.dma_start(raw[i], m[layer].rearrange("(c p) n -> p c n", p=P)).then_inc(raw_in[i], 16)
                with sp.Fori(0, BLOCKS // 2) as it:
                    for u in range(2):
                        b = 2 * it + u
                        first = sp.snap(b * P)
                        sp.wait_ge(lo_ready, b + 3)
                        sp.dma_start(k.xt_d[bass.ds(first, P), :], xt[:, u].rearrange("p a c n -> p (a c n)").bitcast(F32)
                                     ).then_inc(xt_stored[u], 16)
                        sp.wait_ge(out_done, OUTS * (b + 3))
                        sp.dma_start(k.k_d[bass.ds(first, P), :], k_out[:, u, :]).then_inc(k_stored[u], 16)
                for u in range(2):
                    sp.wait_ge(xt_stored[u], 16 * (BLOCKS // 2 + 1))
                    sp.wait_ge(k_stored[u], 16 * (BLOCKS // 2 + 1))
        ph.give_back()


def side_product(nc, out, xt, w, c, done):
    for n, (a, b) in enumerate(((0, 0), (0, 1), (1, 0))):
        last = nc.tensor.matmul(out, xt[:, a, c, :], w[b][:, c, :], start=c == 0 and n == 0, stop=done is not None and c == KC - 1 and n == 2)
    if done is not None and c == KC - 1:
        last.then_inc(done, 1)


def gather_rows(nc, k, pool, table, rows, index, held, first_index, wait_index, asked, arrived, rows_used):
    sources = k.src_t[:].rearrange("p s t -> p (s t)")
    n = HALF * TPS
    ring = len(arrived)
    turns = 2 * ring // HALF
    halves = STEPS // HALF
    nc.gpsimd.tensor_copy(index[:, 0:held, :], sources[:, 0:held * n].rearrange("p (h n) -> p h n", n=n)).then_inc(first_index, 1)
    pool.wait_ge(first_index, 1)

    def gather_half(half, turn, times):
        wait_index(half, turn, times)
        for s in range(HALF):
            for used in rows_used:
                pool.wait_ge(used, HALF * half + s + 1)
            pool.sem_inc(asked, 1)
            slot = (HALF * turn + s) % ring
            for t in range(TPS):
                at = bass.IndirectOffsetOnAxis(ap=index[:, turn, s * TPS + t:s * TPS + t + 1], axis=0)
                nc.gpsimd.indirect_dma_start(rows[:, slot, t, :], None, table, at).then_inc(arrived[slot], 16)

    with pool.Fori(0, halves // turns) as it:
        for turn in range(turns):
            gather_half(turns * it + turn, turn, it)
    for turn in range(halves % turns):
        gather_half(halves // turns * turns + turn, turn, halves // turns)


def score(nc, k, layer):
    with ExitStack() as stack:
        ph = Phase(nc, stack, f"score{layer}")
        rows = ph.sb("rows", [P, RING, TPS, C])
        index = ph.sb("index", [P, 2, HALF * TPS], I32)
        spare = [0]

        def in_work(n):
            spare[0] += n
            return k.work[:, spare[0] - n:spare[0]]

        prod = in_work(PRODS * TPS * C).rearrange("p (r t n) -> p r t n", t=TPS, n=C)
        by_chunk = lambda a: a.rearrange("p (c n) -> p c n", n=C)
        raw = [by_chunk(k.work[:, i * KC * C:(i + 1) * KC * C]) for i in range(2)]
        w_v = [ph.sb(f"w_v_{part}", [P, KC, C], F32R)[:] for part in ("hi", "lo")]
        w_skip = [ph.sb(f"w_skip_{part}", [P, KC, C], F32R)[:] for part in ("hi", "lo")]
        local, hot = (in_work(HALF * SE).bitcast(BF16).rearrange("p (q n) -> p q n", q=2) for i in range(2))
        bias, v_out = in_work(C), in_work(C)
        skip = in_work(2 * C).rearrange("p (u n) -> p u n", n=C)
        xt = ph.sb("xt", [P, 2, 2, KC, P], F32R)
        q_ps = [ph.ps(f"q_ps{i}", [P, TPS, C]) for i in range(2)]
        v_ps, skip_ps = ph.ps("v_ps", [P, C]), ph.ps("skip_ps", [P, C])

        gathered_before = layer * STEPS // RING
        first_index, index_ready = ph.sem("first_index"), ph.sem("index_ready")
        asked = ph.sem("asked")
        local_in = [ph.sem("local_in0"), ph.sem("local_in1")]
        hot_ready, q_ready = ph.sem("hot_ready"), ph.sem("q_ready")
        multiplied, act_summed, dve_summed = ph.sem("multiplied"), ph.sem("act_summed"), ph.sem("dve_summed")
        raw_in, bias_in = [ph.sem("raw_in0"), ph.sem("raw_in1")], ph.sem("bias_in")
        w_hi, w_lo = ph.sem("w_hi"), ph.sem("w_lo")
        xt_in = [ph.sem("xt_in0"), ph.sem("xt_in1")]
        base_in = [ph.sem("base_in0"), ph.sem("base_in1")]
        skip_product, skip_done = ph.sem("skip_product"), ph.sem("skip_done")
        skip_stored = [ph.sem("skip_stored0"), ph.sem("skip_stored1")]
        v_product, v_done, v_stored = ph.sem("v_product"), ph.sem("v_done"), ph.sem("v_stored")
        half_edges = HALF * SE
        LOOPS = STEPS // BODY
        assert 2 * (LOOPS - 1) == BLOCKS

        with nc.Block() as block:
            @block.gpsimd
            def _(pool):
                gather_rows(nc, k, pool, k.k_d, rows, index, 1, first_index,
                            lambda half, turn, times: pool.wait_ge(index_ready, half + 1), asked, k.k_in, [multiplied])

            @block.sync
            def _(sp):
                def load(first, q):
                    sp.dma_start(local[:, q, :], k.local_d[bass.ds(first, half_edges)].partition_broadcast(P)
                                 ).then_inc(local_in[q], 16)

                def load_block(node, u):
                    sp.dma_start(xt[:, u].rearrange("p a c n -> p (a c n)").bitcast(F32), k.xt_d[bass.ds(node, P), :]
                                 ).then_inc(xt_in[u], 16)
                    sp.dma_start(skip[:, u, :], k.skip_d[layer][bass.ds(node, P), :]).then_inc(base_in[u], 16)

                def body(it, ahead):
                    for q in range(2):
                        half = 2 * it + q
                        node = sp.snap(half * P)
                        sp.wait_ge(hot_ready, half + 2)
                        load(sp.snap((half + 2) * half_edges), q)
                        sp.wait_ge(v_done, half + 2)
                        sp.dma_start(k.v_d[bass.ds(node, P), :], v_out).then_inc(v_stored, 16)
                        sp.wait_ge(skip_done, half + 2)
                        sp.dma_start(k.skip_d[layer][bass.ds(node, P), :], skip[:, q, :]).then_inc(skip_stored[q], 16)
                        if ahead:
                            sp.wait_ge(skip_stored[q], 16 * (it + 1))
                            load_block(sp.snap((half + 2) * P), q)

                load(0, 0)
                for i, m in enumerate((k.Wv, k.Ws)):
                    sp.dma_start(raw[i], m[layer].rearrange("(c p) n -> p c n", p=P)).then_inc(raw_in[i], 16)
                sp.dma_start(bias, k.bv[layer].partition_broadcast(P)).then_inc(bias_in, 16)
                load_block(0, 0)
                load(half_edges, 1)
                load_block(P, 1)
                with sp.Fori(0, LOOPS - 2) as it:
                    body(it, True)
                body(LOOPS - 2, False)
                sp.wait_ge(v_stored, 16 * (BLOCKS + 1))
                for u in range(2):
                    sp.wait_ge(skip_stored[u], 16 * (BLOCKS // 2))

            @block.tensor
            def _(pe):
                pe.sem_inc(q_ready, HALF)

                def body(it, with_blocks, first):
                    for q in range(2):
                        half = 2 * it + q
                        pe.wait_ge(hot_ready, half + 2)
                        for s in range(HALF):
                            n = BODY * it + HALF * q + s
                            node_block = pe.value_load(k.block_row[0:1, bass.ds(n, 1)], min_val=0, max_val=BLOCKS - 1)
                            pe.wait_ge(multiplied, n + RING - 1)
                            q3 = k.q3[:, bass.ds(node_block * (Q_PARTS * C), Q_PARTS * C)]
                            for t in range(TPS):
                                e = (s * TPS + t) * P
                                for part in range(Q_PARTS):
                                    last = nc.tensor.matmul(q_ps[s % 2][:, t, :], hot[:, q, e:e + P],
                                                            q3[:, part * C:(part + 1) * C],
                                                            start=part == 0, stop=part == Q_PARTS - 1)
                            last.then_inc(q_ready, 1)
                            if with_blocks and s < KC:
                                if first and half == 0 and s == 0:
                                    pe.wait_ge(w_lo, 1)
                                if s == 0:
                                    pe.wait_ge(xt_in[q], 16 * (it + 1))
                                    pe.wait_ge(v_done, half + 1)
                                side_product(nc, v_ps[:], xt[:, q], w_v, s, v_product)
                            elif with_blocks:
                                if first and half == 0 and s == KC:
                                    pe.wait_ge(w_lo, 2)
                                if s == KC:
                                    pe.wait_ge(skip_done, half + 1)
                                side_product(nc, skip_ps[:], xt[:, q], w_skip, s - KC, skip_product)

                body(0, True, True)
                with pe.Fori(1, LOOPS - 1) as it:
                    body(it, True, False)
                body(LOOPS - 1, False, False)

            @block.vector
            def _(dve):
                def one_hot(half_done, q, times):
                    dve.wait_ge(local_in[q], 16 * times)
                    if half_done is not None:
                        dve.wait_ge(q_ready, half_done)
                    nc.vector.tensor_scalar(hot[:, q, :], local[:, q, :], k.iota_col[:, 0:1], None,
                                            ALU.is_equal).then_inc(hot_ready, 1)

                def multiply(n, s, times):
                    dve.wait_ge(k.k_in[s % RING], 16 * TPS * (gathered_before + times))
                    dve.wait_ge(q_ready, n + HALF + 1)
                    dve.wait_ge(act_summed, n + 1)
                    dve.wait_ge(dve_summed, n + 1)
                    nc.vector.tensor_tensor(prod[:, s % PRODS], q_ps[s % 2][:], rows[:, s % RING], ALU.mult
                                            ).then_inc(multiplied, 1)

                def add_up(n, s, heads):
                    dve.wait_ge(multiplied, n + RING + 1)
                    nc.vector.tensor_reduce(
                        k.edge[:, bass.ds(n * TPS, TPS), 0:heads],
                        prod[:, s % PRODS, :, 0:heads * D].rearrange("p t (h d) -> p t h d", d=D), AX.X, ALU.add
                    ).then_inc(dve_summed, 1)

                def take_v(half):
                    dve.wait_ge(v_product, half + 1)
                    dve.wait_ge(v_stored, 16 * (half + 1))
                    nc.vector.tensor_tensor(v_out, v_ps[:], bias, ALU.add).then_inc(v_done, 1)

                def take_skip(half, u, it):
                    dve.wait_ge(skip_product, half + 1)
                    dve.wait_ge(base_in[u], 16 * (it + 1))
                    nc.vector.tensor_tensor(skip[:, u, :], skip_ps[:], skip[:, u, :], ALU.add).then_inc(skip_done, 1)

                sources = k.src_t[:].rearrange("p s t -> p (s t)")
                dve.sem_inc(index_ready, 1)
                dve.sem_inc(multiplied, RING)
                dve.sem_inc(dve_summed, PRODS)
                dve.sem_inc(hot_ready, 1)
                dve.sem_inc(v_stored, 16)
                dve.sem_inc(v_done, 1)
                dve.sem_inc(skip_done, 1)
                one_hot(None, 0, 1)
                for i, parts in enumerate((w_v, w_skip)):
                    dve.wait_ge(w_hi, i + 1)
                    nc.vector.tensor_tensor(parts[1], raw[i], parts[0].bitcast(F32), ALU.subtract).then_inc(w_lo, 1)
                dve.wait_ge(w_lo, 2)
                dve.wait_ge(bias_in, 16)

                def body(it, with_blocks, heads):
                    for q in range(2):
                        half = 2 * it + q
                        n = BODY * it + HALF * q
                        for s in range(HALF):
                            multiply(n + s, s, half + 1)
                            if s == 0 and (with_blocks or q == 0):
                                nc.vector.tensor_copy(index[:, 1 - q, :], sources[:, bass.ds((half + 1) * HALF * TPS, HALF * TPS)]
                                                      ).then_inc(index_ready, 1)
                            if s > 0:
                                add_up(n + s - 1, s - 1, heads)
                            if s == HALF // 2 and (with_blocks or q == 0):
                                one_hot(HALF * half + HALF, 1 - q, it + q + 1)
                            if with_blocks and s == HALF - 2:
                                take_v(half)
                        if with_blocks:
                            take_skip(half, q, it)
                        add_up(n + HALF - 1, HALF - 1, heads)

                with dve.Fori(0, LOOPS - 1) as it:
                    body(it, True, DVE_HEADS1)
                body(LOOPS - 1, False, LAST_HEADS1)

            @block.scalar
            def _(act):
                act.sem_inc(act_summed, PRODS)
                for i, parts in enumerate((w_v, w_skip)):
                    act.wait_ge(raw_in[i], 16)
                    nc.scalar.activation(parts[0], raw[i], ACT.Copy).then_inc(w_hi, 1)

                def body(it, heads):
                    for s in range(BODY):
                        n = BODY * it + s
                        act.wait_ge(multiplied, n + RING + 1)
                        for t in range(TPS):
                            for h in range(heads, HEADS):
                                at = prod[:, s % PRODS, t, h * D:(h + 1) * D]
                                last = nc.scalar.activation(
                                    at, at, ACT.Copy,
                                    accum_out=k.edge[:, bass.ds(n * TPS + t, 1), h:h + 1].rearrange("p a b -> p (a b)"))
                        last.then_inc(act_summed, 1)

                with act.Fori(0, LOOPS - 1) as it:
                    body(it, DVE_HEADS1)
                body(LOOPS - 1, LAST_HEADS1)


def soften_collect(nc, k, layer):
    with ExitStack() as stack:
        ph = Phase(nc, stack, f"coll{layer}")
        fwd = ph.sb("fwd", [P, SLOTS])
        bwd = ph.sb("bwd", [P, SLOTS])
        seeds = [ph.sb(f"seeds{i}", [1, HEADS, CHUNKS]) for i in range(2)]
        carry = [ph.sb(f"carry{i}", [1, HEADS, CHUNKS]) for i in range(2)]
        carry_ch = [ph.sb(f"carry_ch{i}", [1, CHUNKS, HEADS]) for i in range(2)]
        carry_col = ph.sb("carry_col", [P, 2])
        rows = ph.sb("rows", [P, V_RING, TPS, C])
        TURNS = 2 * V_RING // HALF
        index = ph.sb("index", [P, TURNS, HALF * TPS], I32)
        hot = ph.sb("hot", [P, HOTS, HOT_STEPS * TPS, P])
        ev = ph.sb("ev", [P, EVS, TPS, AGG])
        banks = ph.ps("banks", [P, 8, 512])
        flat_banks = banks[:].rearrange("p b n -> p (b n)")
        big, small, cols = flat_banks[:, 0:6 * 512], banks[:, 6, 0:2 * P], banks[:, 6, 2 * P:2 * P + 2]
        sums = [banks[:, 2 * i:2 * i + 2, 0:AGG // 2] for i in range(SUMS)]

        sorted_out, turned = ph.sem("sorted_out"), ph.sem("turned")
        ends_ready, ends_turned = ph.sem("ends_ready"), ph.sem("ends_turned")
        carry_ready, carry_turned = ph.sem("carry_ready"), ph.sem("carry_turned")
        max_known = ph.sem("max_known")
        less_max, raised, back, steps = ph.sem("less_max"), ph.sem("raised"), ph.sem("back"), ph.sem("steps")
        e_known, cleared = ph.sem("e_known"), ph.sem("cleared")
        gathered_before = layer * STEPS // V_RING
        first_index = ph.sem("first_index")
        index_in = [ph.sem(f"index_in{i}") for i in range(TURNS)]
        asked = ph.sem("asked")
        hot_ready, ev_dve, ev_act = ph.sem("hot_ready"), ph.sem("ev_dve"), ph.sem("ev_act")
        summed, added = ph.sem("summed"), ph.sem("added")
        LOOPS = STEPS // BODY

        scores = k.edge[:].rearrange("p (c g) h -> p g c h", g=CT)
        local_flat = k.local_t[:].rearrange("p s t -> p (s t)")
        flat = lambda x: x[:].rearrange("p h c -> p (h c)")
        flip = lambda x: x[:, ::-1]
        QUART = 4
        QUARTS = -(-CT // QUART)

        with nc.Block() as block:
            @block.gpsimd
            def _(pool):
                gather_rows(nc, k, pool, k.v_d, rows, index, TURNS - 1, first_index,
                            lambda half, turn, times: pool.wait_ge(index_in[turn], 16 * (times + 1)), asked, k.v_in, [ev_dve, ev_act])

            @block.sync
            def _(sp):
                sources = k.src_t[:].rearrange("p s t -> p (s t)")
                n = HALF * TPS

                def load(half, turn):
                    sp.dma_start(index[:, turn, :], sources[:, bass.ds(half * n, n)]).then_inc(index_in[turn], 16)

                def load_when_free(half, turn):
                    sp.wait_ge(ev_dve, V_RING + HALF * (half - TURNS + 1))
                    load(half, turn)

                for turn in range(TURNS - 1):
                    sp.sem_inc(index_in[turn], 16)
                load(TURNS - 1, TURNS - 1)
                halves = STEPS // HALF
                with sp.Fori(1, halves // TURNS) as it:
                    for turn in range(TURNS):
                        load_when_free(TURNS * it + turn, turn)
                for half in range(halves // TURNS * TURNS, halves):
                    load_when_free(half, half % TURNS)

            @block.tensor
            def _(pe):
                pe.wait_ge(sorted_out, 1)
                for g in range(CT):
                    last = nc.tensor.transpose(big[:, g * P:(g + 1) * P], fwd[:, g * P:(g + 1) * P], k.ident[:])
                last.then_inc(turned, 1)
                pe.wait_ge(ends_ready, 1)
                nc.tensor.matmul(small[0:1, 0:P], fwd[:, SLOTS - 1:SLOTS], k.ident[:], start=True, stop=True)
                nc.tensor.matmul(small[0:1, P:2 * P], bwd[:, 0:1], k.ident[:], start=True, stop=True).then_inc(ends_turned, 1)
                pe.wait_ge(carry_ready, 1)
                for i in range(2):
                    last = nc.tensor.matmul(cols[:, i:i + 1], carry_ch[i][:].rearrange("p c h -> p (c h)"),
                                            k.ones[0:1, 0:1], start=True, stop=True)
                last.then_inc(carry_turned, 1)
                for n, g in enumerate(range(0, CT, QUART)):
                    pe.wait_ge(raised, n + 1)
                    for i in range(g, min(g + QUART, CT)):
                        last = nc.tensor.transpose(big[:, i * P:(i + 1) * P], bwd[:, i * P:(i + 1) * P], k.ident[:])
                    last.then_inc(back, 1)

                with pe.Fori(0, LOOPS) as it:
                    for s in range(BODY):
                        n = BODY * it + s
                        if s % HOT_STEPS == 0:
                            pe.wait_ge(hot_ready, BODY // HOT_STEPS * it + s // HOT_STEPS + 1)
                        pe.wait_ge(ev_dve, n + V_RING + 1)
                        pe.wait_ge(ev_act, n + V_RING + 1)
                        pe.wait_ge(added, n + 1)
                        for t in range(TPS):
                            m = hot[:, s // HOT_STEPS % HOTS, (s % HOT_STEPS) * TPS + t, :]
                            for part in range(2):
                                last = nc.tensor.matmul(sums[s % SUMS][:, part, :], m,
                                                        ev[:, s % EVS, t, part * AGG // 2:(part + 1) * AGG // 2],
                                                        start=t == 0, stop=t == TPS - 1)
                        last.then_inc(summed, 1)

            @block.vector
            def _(dve):
                dve.sem_inc(ev_dve, V_RING)
                link = chain(dve, steps)
                v = nc.vector
                scan = lambda out, flags, data, first: v.tensor_tensor_scan(out, flags, data, first, ALU.add, ALU.max)
                before, after = k.fresh[:, 0:SLOTS], k.fresh[:, 1:SLOTS + 1]
                v.tensor_copy(fwd[:].rearrange("p (g c h) -> p g c h", g=CT, h=HEADS), scores).then_inc(sorted_out, 1)
                for x in seeds:
                    v.memset(x[:], -BIG)
                dve.wait_ge(turned, 1)
                link(scan(fwd[:], before, big[:, 0:SLOTS], -BIG))
                scan(flip(bwd), flip(after), flip(big[:, 0:SLOTS]), -BIG).then_inc(ends_ready, 1)
                dve.wait_ge(ends_turned, 1)
                a, b = slice(1, CHUNKS), slice(0, CHUNKS - 1)
                last_f = small[0:1, 0:P].rearrange("p (c h) -> p h c", h=HEADS)
                first_b = small[0:1, P:2 * P].rearrange("p (c h) -> p h c", h=HEADS)
                link(v.tensor_tensor(seeds[0][:, :, a], last_f[:, :, b], k.seed_f[:, :, a], ALU.add))
                link(v.tensor_tensor(seeds[1][:, :, b], first_b[:, :, a], k.seed_b[:, :, b], ALU.add))
                link(scan(flat(carry[0]), flat(k.link_f), flat(seeds[0]), -BIG))
                link(scan(flip(flat(carry[1])), flip(flat(k.link_b)), flip(flat(seeds[1])), -BIG))
                v.tensor_copy(carry_ch[0][:], carry[0][:].rearrange("p h c -> p c h"))
                v.tensor_copy(carry_ch[1][:], carry[1][:].rearrange("p h c -> p c h")).then_inc(carry_ready, 1)
                dve.wait_ge(carry_turned, 1)
                link(v.tensor_copy(carry_col[:], cols[:, 0:2]))
                link(scan(fwd[:], before, big[:, 0:SLOTS], carry_col[:, 0:1]))
                link(scan(flip(bwd), flip(after), flip(big[:, 0:SLOTS]), carry_col[:, 1:2]))
                quarters = [slice(g * P, min(g + QUART, CT) * P) for g in range(0, CT, QUART)]
                for n in range(QUARTS + 1):
                    if n < QUARTS:
                        at = quarters[n]
                        v.tensor_tensor(fwd[:, at], fwd[:, at], bwd[:, at], ALU.max).then_inc(max_known, 1)
                    if n > 0:
                        at = quarters[n - 1]
                        dve.wait_ge(max_known, n)
                        v.tensor_tensor(fwd[:, at], big[:, at], fwd[:, at], ALU.subtract).then_inc(less_max, 1)

                def one_hot(pair, slot, free):
                    if free is not None:
                        dve.wait_ge(summed, free)
                    n = HOT_STEPS * TPS
                    nc.vector.tensor_tensor(hot[:, slot], k.iota_row[:].unsqueeze(1).to_broadcast([P, n, P]),
                                            local_flat[:, bass.ds(pair * n, n)].unsqueeze(2).to_broadcast([P, n, P]),
                                            ALU.is_equal).then_inc(hot_ready, 1)

                def weigh(n, s, times):
                    dve.wait_ge(k.v_in[s % V_RING], 16 * TPS * (gathered_before + times))
                    dve.wait_ge(summed, n + 1)
                    cut = DVE_HEADS2 * D
                    nc.vector.tensor_tensor(
                        ev[:, s % EVS, :, 0:cut].rearrange("p t (h d) -> p t h d", d=D),
                        rows[:, s % V_RING, :, 0:cut].rearrange("p t (h d) -> p t h d", d=D),
                        k.edge[:, bass.ds(n * TPS, TPS), 0:DVE_HEADS2].unsqueeze(3).to_broadcast([P, TPS, DVE_HEADS2, D]),
                        ALU.mult).then_inc(ev_dve, 1)

                def add(n, s):
                    node_block = dve.value_load(k.block_row[0:1, bass.ds(n, 1)], min_val=0, max_val=BLOCKS - 1)
                    at = k.work[:, bass.ds(node_block * AGG, AGG)].rearrange("p (b n) -> p b n", b=2)
                    dve.wait_ge(summed, n + EVS + 1)
                    dve.wait_ge(added, n + SUMS)
                    nc.vector.tensor_tensor(at, at, sums[s % SUMS], ALU.add).then_inc(added, 1)

                dve.sem_inc(summed, EVS)
                dve.sem_inc(added, SUMS)
                for pair in range(HOTS - 1):
                    one_hot(pair, pair, None)
                dve.wait_ge(e_known, QUARTS)
                dve.wait_ge(cleared, 1)
                weigh(0, 0, 1)
                weigh(1, 1, 1)

                def body(it, last):
                    for s in range(BODY):
                        n = BODY * it + s
                        if not (last and s >= BODY - 2):
                            weigh(n + 2, (s + 2) % BODY, it + (s + 2) // V_RING + 1)
                        add(n, s)
                        if s % HOT_STEPS == HOT_STEPS - 1:
                            pair = s // HOT_STEPS
                            one_hot(BODY // HOT_STEPS * it + pair + HOTS - 1, (pair + HOTS - 1) % HOTS, n + EVS + 1 - HOT_STEPS)

                with dve.Fori(0, LOOPS - 1) as it:
                    body(it, False)
                body(LOOPS - 1, True)

            @block.scalar
            def _(act):
                act.sem_inc(ev_act, V_RING)
                nc.scalar.activation(k.work[:], k.ones[:, 0:1].to_broadcast([P, BLOCKS * AGG]), ACT.Copy, scale=0.0
                                     ).then_inc(cleared, 1)
                for n in range(QUARTS + 1):
                    if n < QUARTS:
                        at = slice(n * QUART * P, min((n + 1) * QUART, CT) * P)
                        act.wait_ge(less_max, n + 1)
                        nc.scalar.activation(bwd[:, at], fwd[:, at], ACT.Exp, scale=float(D) ** -0.5).then_inc(raised, 1)
                    if n > 0:
                        g = (n - 1) * QUART
                        m = min(QUART, CT - g)
                        act.wait_ge(back, n)
                        nc.scalar.activation(scores[:, g:g + m],
                                             big[:, g * P:(g + m) * P].rearrange("p (g c h) -> p g c h", g=m, h=HEADS),
                                             ACT.Copy).then_inc(e_known, 1)
                act.wait_ge(e_known, QUARTS)
                with act.Fori(0, STEPS // BODY) as it:
                    for s in range(BODY):
                        n = BODY * it + s
                        act.wait_ge(summed, n + 1)
                        nc.scalar.activation(ev[:, s % EVS, :, C:AGG], k.edge[:, bass.ds(n * TPS, TPS), :], ACT.Copy)
                        act.wait_ge(k.v_in[s % V_RING], 16 * TPS * (it + (gathered_before + 1)))
                        for t in range(TPS):
                            for h in range(DVE_HEADS2, HEADS):
                                last = nc.scalar.activation(
                                    ev[:, s % EVS, t, h * D:(h + 1) * D], rows[:, s % V_RING, t, h * D:(h + 1) * D], ACT.Copy,
                                    scale=k.edge[:, bass.ds(n * TPS + t, 1), h:h + 1].rearrange("p a b -> p (a b)"))
                        last.then_inc(ev_act, 1)
        if layer == 0:
            ph.give_back()


def finish(nc, k):
    GB = 4
    GROUPS = BLOCKS // GB
    GN = GB * P
    ZS = 4
    with ExitStack() as stack:
        ph = Phase(nc, stack, "mlp")
        w1 = [ph.sb(f"w1{part}", [P, KC, HID], F32R) for part in ("hi", "lo")]
        w2 = [ph.sb(f"w2{part}", [P, FC, C], F32R) for part in ("hi", "lo")]
        gain, shift, b2 = (ph.sb(n, [P, C]) for n in ("gain", "shift", "b2"))
        b1 = ph.sb("b1", [P, FC])
        skip = ph.sb("skip", [P, GB, C])
        enc = ph.sb("enc", [P, GB, C])
        y = ph.sb("y", [P, 2, GB, C])
        yt_hi = ph.sb("yt_hi", [P, KC, GN], F32R)
        yt_lo = ph.sb("yt_lo", [P, KC, GN], F32R)
        h_all = ph.sb("h_all", [P, 2, GN])
        z = ph.sb("z", [P, ZS, C])
        inv = ph.sb("inv", [P, GB, HEADS])
        y_stats, y_mean_var, y_scale = ph.sb("y_stats", [P, GB, 6]), ph.sb("y_mean_var", [P, GB, 2]), ph.sb("y_scale", [P, 2, GB])
        z_stats, z_mean_var, z_scale = ph.sb("z_stats", [P, 2, 6]), ph.sb("z_mean_var", [P, 2, 2]), ph.sb("z_scale", [P, 2, 2])
        yt_ps = [ph.ps(f"yt_ps{i}", [P, C]) for i in range(2)]
        h_ps = [ph.ps(f"h_ps{i}", [P, GN]) for i in range(2)]
        z_ps = [ph.ps(f"z_ps{i}", [P, C]) for i in range(2)]
        PIECES = 4
        with ExitStack() as early:
            raw_t = early.enter_context(nc.sbuf_tensor("mlp_raw", [P, PIECES, KC, C], F32))
        h_hi = ph.sb("h_hi", [P, FC, GN], F32R)
        h_lo = ph.sb("h_lo", [P, FC, GN], F32R)
        raw = [raw_t[:, i] for i in range(PIECES)]
        w1_v = k.W1.rearrange("(c p) n -> p c n", p=P)
        w2_v = k.W2.rearrange("(c p) n -> p c n", p=P)
        source = [w1_v[:, :, i * C:(i + 1) * C] for i in range(2)] + [w2_v[:, i * KC:(i + 1) * KC, :] for i in range(2)]
        split = [[part[:, :, i * C:(i + 1) * C] for part in w1] for i in range(2)]
        split += [[part[:, i * KC:(i + 1) * KC, :] for part in w2] for i in range(2)]

        const_in, bias_in = ph.sem("const_in"), ph.sem("bias_in")
        raw_in = [ph.sem(f"raw_in{i}") for i in range(PIECES)]
        w_hi, w1_lo, w2_lo = ph.sem("w_hi"), ph.sem("w1_lo"), ph.sem("w2_lo")
        skip_in, skip_free = ph.sem("skip_in"), ph.sem("skip_free")
        enc_in, enc_ready, enc_free = ph.sem("enc_in"), ph.sem("enc_ready"), ph.sem("enc_free")
        steps, var_known, std_known = ph.sem("steps"), ph.sem("var_known"), ph.sem("std_known")
        y_ready, turned, y_hi, y_lo = ph.sem("y_ready"), ph.sem("turned"), ph.sem("y_hi"), ph.sem("y_lo")
        y_b2 = ph.sem("y_b2")
        h_product, h_taken, h_split = ph.sem("h_product"), ph.sem("h_taken"), ph.sem("h_split")
        z_product, z_taken, out_ready = ph.sem("z_product"), ph.sem("z_taken"), ph.sem("out_ready")
        stored = [ph.sem(f"stored{i}") for i in range(ZS)]

        with nc.Block() as block:
            @block.sync
            def _(sp):
                def load_skip(g):
                    if g > 0:
                        sp.wait_ge(skip_free, g)
                    rows = k.skip_d[LAYERS - 1][g * GN:(g + 1) * GN, :]
                    sp.dma_start(skip[:], rows.rearrange("(i p) c -> p i c", p=P)).then_inc(skip_in, 16)

                def load_enc(g):
                    if g > 0:
                        sp.wait_ge(enc_free, g)
                    rows = k.x[g * GN:(g + 1) * GN, :]
                    sp.dma_start(enc[:], rows.rearrange("(i p) c -> p i c", p=P)).then_inc(enc_in, 16)

                def store(b):
                    sp.wait_ge(out_ready, b + 1)
                    rows = min(P, NODES - b * P)
                    sp.dma_start(k.out[b * P:b * P + rows, :], z[0:rows, b % ZS, :]).then_inc(stored[b % ZS], 16)

                load_skip(0)
                sp.dma_start(raw[0], source[0]).then_inc(raw_in[0], 16)
                for t, a in ((gain, k.ln_g), (shift, k.ln_b)):
                    sp.dma_start(t[:], a.partition_broadcast(P)).then_inc(const_in, 16)
                for i in range(1, PIECES):
                    sp.dma_start(raw[i], source[i]).then_inc(raw_in[i], 16)
                with nc.allow_non_contiguous_dma(reason="a few hundred elements"):
                    sp.dma_start(b1[:], k.b1.rearrange("(c p) -> p c", p=P)).then_inc(bias_in, 16)
                sp.dma_start(b2[:], k.b2.partition_broadcast(P)).then_inc(bias_in, 16)
                load_enc(0)
                load_skip(1)
                for g in range(GROUPS):
                    if g > 0:
                        store(GB * g - 2)
                        store(GB * g - 1)
                        load_enc(g)
                    if g + 2 < GROUPS:
                        load_skip(g + 2)
                    store(GB * g)
                    store(GB * g + 1)
                store(BLOCKS - 2)
                store(BLOCKS - 1)
                for i in range(ZS):
                    sp.wait_ge(stored[i], 16 * (BLOCKS // ZS))

            @block.gpsimd
            def _(pool):
                def y_plus_b2(g):
                    for i in range(GB):
                        pool.wait_ge(turned, GB * g + i + 1)
                        nc.gpsimd.tensor_tensor(y[:, g % 2, i, :], y[:, g % 2, i, :], b2[:], ALU.add).then_inc(y_b2, 1)

                def h_low(g):
                    for f in range(FC):
                        pool.wait_ge(h_taken, 2 * (FC * g + f + 1))
                        nc.gpsimd.tensor_tensor(h_lo[:, f, :], h_all[:, f % 2, :], h_hi[:, f, :].bitcast(F32),
                                                ALU.subtract).then_inc(h_split, 1)

                def twice_enc(g):
                    pool.wait_ge(enc_in, 16 * (g + 1))
                    nc.gpsimd.tensor_tensor(enc[:], enc[:], enc[:], ALU.add).then_inc(enc_ready, 1)
                    pool.wait_ge(enc_ready, 2 * g + 1)
                    nc.gpsimd.tensor_tensor(enc[:], enc[:], shift[:].unsqueeze(1).to_broadcast([P, GB, C]),
                                            ALU.add).then_inc(enc_ready, 1)

                for i in (0, 1):
                    pool.wait_ge(w_hi, i + 1)
                    nc.gpsimd.tensor_tensor(split[i][1], raw[i], split[i][0].bitcast(F32), ALU.subtract).then_inc(w1_lo, 1)
                pool.wait_ge(const_in, 32)
                pool.wait_ge(bias_in, 32)
                pool.wait_ge(w2_lo, 2)
                for g in range(GROUPS):
                    h_low(g)
                    if g == 0:
                        y_plus_b2(0)
                    twice_enc(g)
                    if g + 1 < GROUPS:
                        y_plus_b2(g + 1)

            @block.vector
            def _(dve):
                v = nc.vector
                marks, roots = [0], [0]

                def mark(ins):
                    marks[0] += 1
                    ins.then_inc(steps, 1)
                    return marks[0]

                def after(m):
                    dve.wait_ge(steps, m)

                def inverse_root(scale):
                    roots[0] += 1
                    dve.wait_ge(std_known, roots[0])
                    return mark(v.reciprocal(scale[:, 1], scale[:, 0]))

                def first_norms(g):
                    par = g % 2
                    group = k.work[:, GB * g * AGG:GB * (g + 1) * AGG].rearrange("p (i n) -> p i n", n=AGG)
                    by_head = lambda t: t.rearrange("p i (h d) -> p i h d", d=D)
                    if g > 0:
                        dve.wait_ge(y_ready, GB * g)
                    after(mark(v.tensor_scalar(inv[:], group[:, :, C:AGG], 1e-16, None, ALU.add)))
                    after(mark(v.reciprocal(inv[:], inv[:])))
                    if g >= 2:
                        dve.wait_ge(z_taken, GB * (g - 1))
                    after(mark(v.tensor_tensor(by_head(y[:, par]), by_head(group[:, :, 0:C]),
                                               inv[:].unsqueeze(3).to_broadcast([P, GB, HEADS, D]), ALU.mult)))
                    dve.wait_ge(skip_in, 16 * (g + 1))
                    after(mark(v.tensor_tensor(y[:, par], y[:, par], skip[:], ALU.add)))
                    dve.sem_inc(skip_free, 1)
                    done = [mark(v.bn_stats(y_stats[:, i], y[:, par, i, :])) for i in range(GB)]
                    for i in range(GB):
                        after(done[i])
                        last = v.bn_aggr(y_mean_var[:, i], y_stats[:, i])
                    last.then_inc(var_known, 1)
                    scaled = inverse_root(y_scale)
                    if g == 0:
                        dve.wait_ge(const_in, 32)

                    def gains(i):
                        done[i] = mark(v.scalar_tensor_tensor(y[:, par, i, :], y[:, par, i, :], y_mean_var[:, i, 0:1], gain[:],
                                                              ALU.subtract, ALU.mult))

                    def shifts(i):
                        after(done[i])
                        v.scalar_tensor_tensor(y[:, par, i, :], y[:, par, i, :], y_scale[:, 1, i:i + 1], shift[:],
                                               ALU.mult, ALU.add).then_inc(y_ready, 1)

                    if g == 0:
                        gains(0)
                        gains(1)
                        after(scaled)
                        shifts(0)
                        shifts(1)
                        gains(2)
                        gains(3)
                        y_low(0, 0)
                        shifts(2)
                        shifts(3)
                        for i in range(1, GB):
                            y_low(0, i)
                    else:
                        for i in range(GB):
                            gains(i)
                        after(scaled)
                        for i in range(GB):
                            shifts(i)

                def y_low(g, i):
                    b = GB * g + i
                    dve.wait_ge(y_hi, b + 1)
                    v.tensor_tensor(yt_lo[:, :, i * P:(i + 1) * P], yt_ps[i % 2][:].rearrange("p (c n) -> p c n", c=KC),
                                    yt_hi[:, :, i * P:(i + 1) * P].bitcast(F32), ALU.subtract).then_inc(y_lo, 1)

                def moments(b):
                    j = b % 2
                    after(mark(v.bn_stats(z_stats[:, j], z[:, b % ZS, :])))
                    last = v.bn_aggr(z_mean_var[:, j], z_stats[:, j])
                    if j == 1:
                        last.then_inc(var_known, 1)

                def take(b):
                    dve.wait_ge(z_product, b + 1)
                    dve.wait_ge(y_b2, b + 1)
                    if b >= ZS:
                        dve.wait_ge(stored[b % ZS], 16 * (b // ZS))
                    v.tensor_tensor(z[:, b % ZS, :], z_ps[b % 2][:], y[:, b // GB % 2, b % GB, :], ALU.add).then_inc(z_taken, 1)
                    dve.wait_ge(z_taken, b + 1)
                    if b >= 2:
                        dve.wait_ge(out_ready, b // 2 * 2)
                    moments(b)

                def last_norms(pair):
                    g = pair[0] // GB
                    known = [0, 0]
                    after(inverse_root(z_scale))
                    for n, b in enumerate(pair):
                        at = z[:, b % ZS, :]
                        known[n] = mark(v.scalar_tensor_tensor(at, at, z_mean_var[:, b % 2, 0:1], gain[:], ALU.subtract, ALU.mult))
                    dve.wait_ge(enc_ready, 2 * (g + 1))
                    for n, b in enumerate(pair):
                        after(known[n])
                        at = z[:, b % ZS, :]
                        known[n] = mark(v.scalar_tensor_tensor(at, at, z_scale[:, 1, b % 2:b % 2 + 1], enc[:, b % GB, :], ALU.mult, ALU.add))
                    for n, b in enumerate(pair):
                        after(known[n])
                        moments(b)
                    if pair[1] % GB == GB - 1:
                        dve.sem_inc(enc_free, 1)
                    after(inverse_root(z_scale))
                    for n, b in enumerate(pair):
                        at = z[:, b % ZS, :]
                        v.tensor_scalar(at, at, z_mean_var[:, b % 2, 0:1], z_scale[:, 1, b % 2:b % 2 + 1],
                                        ALU.subtract, ALU.mult).then_inc(out_ready, 1)

                first_norms(0)
                for i in (2, 3):
                    dve.wait_ge(w_hi, i + 1)
                    v.tensor_tensor(split[i][1], raw[i], split[i][0].bitcast(F32), ALU.subtract).then_inc(w2_lo, 1)
                for g in range(GROUPS):
                    if g > 0:
                        pair = (GB * g - 2, GB * g - 1)
                        for b in pair:
                            take(b)
                        last_norms(pair)
                    if g + 1 < GROUPS:
                        first_norms(g + 1)
                    pair = (GB * g, GB * g + 1)
                    for b in pair:
                        take(b)
                    if g + 1 < GROUPS:
                        y_low(g + 1, 0)
                        y_low(g + 1, 1)
                    last_norms(pair)
                    if g + 1 < GROUPS:
                        y_low(g + 1, 2)
                        y_low(g + 1, 3)
                pair = (BLOCKS - 2, BLOCKS - 1)
                for b in pair:
                    take(b)
                last_norms(pair)

            @block.scalar
            def _(act):
                roots = [0]

                def root(scale, mean_var):
                    roots[0] += 1
                    act.wait_ge(var_known, roots[0])
                    nc.scalar.activation(scale[:, 0], mean_var[:, :, 1], ACT.Sqrt, bias=k.eps[:, 0:1]).then_inc(std_known, 1)

                def y_high(g, blocks):
                    for i in blocks:
                        act.wait_ge(turned, GB * g + i + 1)
                        nc.scalar.activation(yt_hi[:, :, i * P:(i + 1) * P], yt_ps[i % 2][:].rearrange("p (c n) -> p c n", c=KC),
                                             ACT.Copy).then_inc(y_hi, 1)

                def h_high(g, f):
                    n = FC * g + f
                    act.wait_ge(h_product, n + 1)
                    if n >= 2:
                        act.wait_ge(h_split, n - 1)
                    nc.scalar.activation(h_all[:, f % 2, :], h_ps[f % 2][:], ACT.Relu, bias=b1[:, f:f + 1]).then_inc(h_taken, 1)
                    nc.scalar.activation(h_hi[:, f, :], h_ps[f % 2][:], ACT.Relu, bias=b1[:, f:f + 1]).then_inc(h_taken, 1)

                def weight_high(i):
                    act.wait_ge(raw_in[i], 16)
                    nc.scalar.activation(split[i][0], raw[i], ACT.Copy).then_inc(w_hi, 1)

                root(y_scale, y_mean_var)
                weight_high(0)
                y_high(0, range(2))
                weight_high(1)
                y_high(0, range(2, GB))
                weight_high(2)
                weight_high(3)
                act.wait_ge(bias_in, 32)
                act.wait_ge(w1_lo, 2)
                for g in range(GROUPS):
                    for f in range(FC):
                        if g > 0 and f in (0, 2):
                            root(z_scale, z_mean_var)
                        if g + 1 < GROUPS and f == (6 if g > 0 else 5):
                            root(y_scale, y_mean_var)
                        h_high(g, f)
                    root(z_scale, z_mean_var)
                    if g + 1 < GROUPS:
                        y_high(g + 1, range(0, 2))
                    root(z_scale, z_mean_var)
                    if g + 1 < GROUPS:
                        y_high(g + 1, range(2, GB))
                root(z_scale, z_mean_var)
                root(z_scale, z_mean_var)

            @block.tensor
            def _(pe):
                def turn(g, i):
                    b = GB * g + i
                    pe.wait_ge(y_ready, b + 1)
                    if b >= 2:
                        pe.wait_ge(y_lo, b - 1)
                    for c in range(KC):
                        last = nc.tensor.transpose(yt_ps[i % 2][:, c * P:(c + 1) * P],
                                                   y[:, g % 2, i, c * P:(c + 1) * P], k.ident[:])
                    last.then_inc(turned, 1)

                def hidden_pair(f, half):
                    at = slice(half * 2 * P, (half + 1) * 2 * P)
                    return split_product(nc, h_ps[f][:, at], lambda c: w1[0][:, c, f * P:(f + 1) * P],
                                         lambda c: w1[1][:, c, f * P:(f + 1) * P], lambda c: yt_hi[:, c, at],
                                         lambda c: yt_lo[:, c, at], range(KC))

                def hidden(g):
                    if g == 0:
                        pe.wait_ge(w1_lo, 1)
                        pe.wait_ge(y_lo, 2)
                        for f in range(2):
                            hidden_pair(f, 0)
                    pe.wait_ge(y_lo, GB * (g + 1))
                    if g == 0:
                        for f in range(2):
                            hidden_pair(f, 1).then_inc(h_product, 1)
                    for f in range(2 if g == 0 else 0, FC):
                        n = FC * g + f
                        if g == 0 and f % KC == 0:
                            pe.wait_ge(w1_lo, f // KC + 1)
                        if n >= 2:
                            pe.wait_ge(h_taken, 2 * (n - 1))
                        split_product(nc, h_ps[f % 2][:], lambda c: w1[0][:, c, f * P:(f + 1) * P],
                                      lambda c: w1[1][:, c, f * P:(f + 1) * P], lambda c: yt_hi[:, c, :],
                                      lambda c: yt_lo[:, c, :], range(KC)).then_inc(h_product, 1)

                def result(g, i):
                    b = GB * g + i
                    if b >= 2:
                        pe.wait_ge(z_taken, b - 1)
                    at = slice(i * P, (i + 1) * P)
                    for f in range(FC):
                        if i == 0:
                            pe.wait_ge(h_split, FC * g + f + 1)
                            if g == 0 and f % KC == 0:
                                pe.wait_ge(w2_lo, f // KC + 1)
                        for n, (a, w) in enumerate(((h_hi, w2[0]), (h_hi, w2[1]), (h_lo, w2[0]))):
                            last = nc.tensor.matmul(z_ps[i % 2][:], a[:, f, at], w[:, f, :],
                                                    start=f == 0 and n == 0, stop=f == FC - 1 and n == 2)
                    last.then_inc(z_product, 1)

                for i in range(GB):
                    turn(0, i)
                for g in range(GROUPS):
                    hidden(g)
                    for i in range(GB):
                        result(g, i)
                        if g + 1 < GROUPS and i in (1, 2):
                            turn(g + 1, 2 * i - 2)
                            turn(g + 1, 2 * i - 1)


def graph_attention(nc, x, src, dst, Wq, bq, Wk, bk, Wv, bv, Ws, bs, W1, b1, W2, b2, ln_g, ln_b, out):
    k = Shared()
    k.x, k.src, k.dst, k.out = x, src, dst, out
    k.Wq, k.bq, k.Wk, k.bk, k.Wv, k.bv, k.Ws, k.bs = Wq, bq, Wk, bk, Wv, bv, Ws, bs
    k.W1, k.b1, k.W2, k.b2, k.ln_g, k.ln_b = W1, b1, W2, b2, ln_g, ln_b
    k.k_d, k.v_d = (nc.dram_tensor(n, [ROWS, C], F32).ap() for n in ("k_rows", "v_rows"))
    k.skip_d = [nc.dram_tensor(f"skip_rows{layer}", [ROWS, C], F32).ap() for layer in range(LAYERS)]
    k.xt_d = nc.dram_tensor("x_turned", [ROWS, 2 * C], F32).ap()
    k.local_d = nc.dram_tensor("local_dst", [TABLE * SE], BF16).ap()
    with ExitStack() as stack:
        ph = Phase(nc, stack, "all")
        k.ident, k.iota_row, k.ones = (ph.sb(n, [P, P]) for n in ("ident", "iota_row", "ones"))
        k.iota_col, k.eps = ph.sb("iota_col", [P, 1]), ph.sb("eps", [P, 1])
        k.work = ph.sb("work", [P, BLOCKS * AGG])
        build_constants(nc, k)
        with ExitStack() as graph:
            gr = Phase(nc, graph, "graph")
            k.src_t = gr.sb("src_t", [P, TABLE, TPS], I32)
            k.local_t = gr.sb("local_t", [P, TABLE, TPS])
            k.block_row = gr.sb("block_row", [1, TABLE], I32)
            k.fresh = gr.sb("fresh", [P, SLOTS + 1])
            k.link_f, k.link_b, k.seed_f, k.seed_b = (gr.sb(n, [1, HEADS, CHUNKS])
                                                      for n in ("link_f", "link_b", "seed_f", "seed_b"))
            k.k_in = [gr.sem(f"k_in{i}") for i in range(RING)]
            k.v_in = [gr.sem(f"v_in{i}") for i in range(V_RING)]
            build_step_tables(nc, k)
            k.edge = gr.sb("edge", [P, TILES, HEADS])
            for layer in range(LAYERS):
                with ExitStack() as queries:
                    k.q3 = Phase(nc, queries, f"layer{layer}").sb("q3", [P, BLOCKS * Q_PARTS * C], BF16)
                    project(nc, k, layer)
                    score(nc, k, layer)
                soften_collect(nc, k, layer)
        finish(nc, k)


_WEIGHTS = ["Wq", "bq", "Wk", "bk", "Wv", "bv", "Ws", "bs", "W1", "b1", "W2", "b2", "ln_g", "ln_b"]


def kernel(**inputs):
    import numpy as _np
    import concourse.bacc as _bacc
    from concourse.bass_utils import run_bass_kernel_spmd as _run

    x = _np.zeros((ROWS, C), _np.float32)
    x[:NODES] = inputs["x"]
    src = _np.zeros((EDGE_ROWS, SE), _np.int32)
    src.reshape(-1)[:EDGES] = inputs["src"]
    dst = _np.full(EDGE_ROWS * SE, PAD_DST, _np.int32)
    dst[:EDGES] = inputs["dst"]
    arrays = {"x": x, "src": src, "dst": dst}
    for name in _WEIGHTS:
        arrays[name] = _np.ascontiguousarray(inputs[f"L0_gnn_{name}"])

    nc = _bacc.Bacc("TRN2", target_bir_lowering=False, num_devices=1)
    args = {n: nc.dram_tensor(f"in_{n}", a.shape, mybir.dt.from_np(a.dtype), kind="ExternalInput").ap()
            for n, a in arrays.items()}
    out = nc.dram_tensor("out_0", (NODES, C), F32, kind="ExternalOutput").ap()
    graph_attention(nc, out=out, **args)
    r = _run(nc, [{f"in_{n}": a for n, a in arrays.items()}], core_ids=[0])
    return r.results[0]["out_0"]
```
